# Optimizing a Trainium2 kernel written in Bass

```python
import numpy as np
import jax
import jax.numpy as jnp

def _softmax(x, axis=-1):
    return jax.nn.softmax(x, axis=axis)
def _gelu(x):
    return jax.nn.gelu(x, approximate=True)
def _silu(x):
    return jax.nn.silu(x)
def _sigmoid(x):
    return jax.nn.sigmoid(x)
def _layernorm(x, axis=-1, eps=1e-5):
    m = jnp.mean(x, axis=axis, keepdims=True)
    v = jnp.var(x, axis=axis, keepdims=True)
    return (x - m) / jnp.sqrt(v + eps)
def _scatter_add(tgt, idx, src, axis=0):
    return tgt.at[idx].add(src)
def _segment_sum(src, seg, n):
    return jax.ops.segment_sum(src, seg, n)

kernel_name = 'mk_adj_preln_d4_adj_128_a83021'

def setup_inputs(seed: int = 0):
    np.random.seed(seed)
    _w = jnp.asarray
    def _rec_inputs():
        import jax
        import jax.numpy as jnp
        _gk = jax.random.key(seed)
        x = -0.0005207 + 1.001 * jax.random.normal(jax.random.fold_in(_gk, 1), (8, 2048, 128), jnp.float32)
        _a = jax.random.bernoulli(jax.random.fold_in(_gk, 2), 0.015625, (2048, 2048))
        _a = jnp.logical_or(_a, jnp.swapaxes(_a, -1, -2))
        _a = jnp.logical_or(_a, jnp.eye(2048, dtype=bool))
        adj = _a.astype(jnp.int32)
        return x, adj
    x, adj = _rec_inputs()
    def _L0_gnn_setup():
        import jax, jax.numpy as jnp
        import numpy as np
        ALPHA = 0.2
        LN_EPS = 1e-05
        NEG_INF = -9000000000000000.0
        key = jax.random.key(seed)
        ks = jax.random.split(key, 6)
        B, N, Fin, Fout = (8, 2048, 128, 128)
        x = jax.random.normal(ks[0], (B, N, Fin), dtype=jnp.float32)
        adj = jax.random.randint(ks[1], (N, N), 0, 2, dtype=jnp.int32)
        W = jax.random.normal(ks[2], (Fin, Fout), dtype=jnp.float32) * 0.05
        a = jax.random.normal(ks[3], (2 * Fout, 1), dtype=jnp.float32) * 0.05
        node_weights = jax.random.normal(ks[4], (N,), dtype=jnp.float32)
        node_bias = jnp.zeros((N,), dtype=jnp.float32)
        ln_gamma = jnp.ones((Fout,), dtype=jnp.float32)
        ln_beta = jnp.zeros((Fout,), dtype=jnp.float32)
        return {'x': x, 'adj': adj, 'W': W, 'a': a, 'node_weights': node_weights, 'node_bias': node_bias, 'ln_gamma': ln_gamma, 'ln_beta': ln_beta}
    _L0_gnn_all = _L0_gnn_setup()
    _L0_gnn_in = {k: v for k, v in _L0_gnn_all.items() if k in ('W', 'a', 'node_weights', 'node_bias', 'ln_gamma', 'ln_beta', )}
    del _L0_gnn_all

    def _L1_gnn_setup():
        import jax, jax.numpy as jnp
        import numpy as np
        IN_DIM = 128
        OUT_DIM = 128
        NUM_HEADS = 4
        HEAD_DIM = OUT_DIM // NUM_HEADS
        B, N = (4, 4096)
        key = jax.random.key(seed)
        ks = jax.random.split(key, 7)
        s_in = 1.0 / np.sqrt(IN_DIM)
        s_out = 1.0 / np.sqrt(OUT_DIM)
        return {'x': jax.random.normal(ks[0], (B, N, IN_DIM), dtype=jnp.float32), 'adjacency': jax.random.randint(ks[1], (N, N), 0, 2, dtype=jnp.int32), 'W_q': jax.random.uniform(ks[2], (IN_DIM, NUM_HEADS * HEAD_DIM), jnp.float32, -s_in, s_in), 'W_k': jax.random.uniform(ks[3], (IN_DIM, NUM_HEADS * HEAD_DIM), jnp.float32, -s_in, s_in), 'W_v': jax.random.uniform(ks[4], (IN_DIM, NUM_HEADS * HEAD_DIM), jnp.float32, -s_in, s_in), 'W_o': jax.random.uniform(ks[5], (OUT_DIM, OUT_DIM), jnp.float32, -s_out, s_out), 'b_o': jax.random.uniform(ks[6], (OUT_DIM,), jnp.float32, -s_out, s_out)}
    _L1_gnn_all = _L1_gnn_setup()
    _L1_gnn_in = {k: v for k, v in _L1_gnn_all.items() if k in ('W_q', 'W_k', 'W_v', 'W_o', 'b_o', )}
    del _L1_gnn_all

    def _L2_gnn_setup():
        import jax, jax.numpy as jnp
        import numpy as np
        B, N, F_IN, F_OUT = (4, 8192, 128, 128)
        key = jax.random.key(seed)
        k = jax.random.split(key, 6)
        x = jax.random.normal(k[0], (B, N, F_IN), dtype=jnp.float32)
        adj_matrix = jax.random.randint(k[1], (N, N), 0, 2, dtype=jnp.int32)
        s = 1.0 / np.sqrt(F_IN)
        W_self = jax.random.uniform(k[2], (F_IN, F_OUT), jnp.float32, -s, s)
        b_self = jax.random.uniform(k[3], (F_OUT,), jnp.float32, -s, s)
        W_neigh = jax.random.uniform(k[4], (F_IN, F_OUT), jnp.float32, -s, s)
        b_neigh = jax.random.uniform(k[5], (F_OUT,), jnp.float32, -s, s)
        return {'x': x, 'adj_matrix': adj_matrix, 'W_self': W_self, 'b_self': b_self, 'W_neigh': W_neigh, 'b_neigh': b_neigh}
    _L2_gnn_all = _L2_gnn_setup()
    _L2_gnn_in = {k: v for k, v in _L2_gnn_all.items() if k in ('W_self', 'b_self', 'W_neigh', 'b_neigh', )}
    del _L2_gnn_all

    def _L3_gnn_setup():
        import jax, jax.numpy as jnp
        import numpy as np
        B, N, F_IN, F_OUT = (8, 2048, 128, 128)
        key = jax.random.key(seed)
        k1, k2, k3, k4 = jax.random.split(key, 4)
        x = jax.random.normal(k1, (B, N, F_IN), dtype=jnp.float32)
        adj = jax.random.randint(k2, (N, N), 0, 2, dtype=jnp.int32)
        W = jax.random.normal(k3, (F_OUT, F_IN), dtype=jnp.float32) * 0.05
        a = jax.random.normal(k4, (2 * F_OUT, 1), dtype=jnp.float32) * 0.05
        return {'x': x, 'adj': adj, 'W': W, 'a': a}
    _L3_gnn_all = _L3_gnn_setup()
    _L3_gnn_in = {k: v for k, v in _L3_gnn_all.items() if k in ('W', 'a', )}
    del _L3_gnn_all

    return {
        "x": x,
        "adj": adj,
        "L0_gnn_W": _L0_gnn_in["W"],
        "L0_gnn_a": _L0_gnn_in["a"],
        "L0_gnn_node_weights": _L0_gnn_in["node_weights"],
        "L0_gnn_node_bias": _L0_gnn_in["node_bias"],
        "L0_gnn_ln_gamma": _L0_gnn_in["ln_gamma"],
        "L0_gnn_ln_beta": _L0_gnn_in["ln_beta"],
        "L1_gnn_W_q": _L1_gnn_in["W_q"],
        "L1_gnn_W_k": _L1_gnn_in["W_k"],
        "L1_gnn_W_v": _L1_gnn_in["W_v"],
        "L1_gnn_W_o": _L1_gnn_in["W_o"],
        "L1_gnn_b_o": _L1_gnn_in["b_o"],
        "L2_gnn_W_self": _L2_gnn_in["W_self"],
        "L2_gnn_b_self": _L2_gnn_in["b_self"],
        "L2_gnn_W_neigh": _L2_gnn_in["W_neigh"],
        "L2_gnn_b_neigh": _L2_gnn_in["b_neigh"],
        "L3_gnn_W": _L3_gnn_in["W"],
        "L3_gnn_a": _L3_gnn_in["a"],
    }

def reference(x, adj, L0_gnn_W, L0_gnn_a, L0_gnn_node_weights, L0_gnn_node_bias, L0_gnn_ln_gamma, L0_gnn_ln_beta, L1_gnn_W_q, L1_gnn_W_k, L1_gnn_W_v, L1_gnn_W_o, L1_gnn_b_o, L2_gnn_W_self, L2_gnn_b_self, L2_gnn_W_neigh, L2_gnn_b_neigh, L3_gnn_W, L3_gnn_a):
    import jax
    import jax.numpy as jnp
    def _L0_gnn_ref(x, adj, W, a, node_weights, node_bias, ln_gamma, ln_beta):
        import jax, jax.numpy as jnp
        import numpy as np
        ALPHA = 0.2
        LN_EPS = 1e-05
        NEG_INF = -9000000000000000.0
        x = x * node_weights[None, :, None] + node_bias[None, :, None] + x
        Fout = W.shape[1]
        h = jnp.einsum('bnf,fo->bno', x, W)
        mu = jnp.mean(h, axis=-1, keepdims=True)
        var = jnp.mean((h - mu) ** 2, axis=-1, keepdims=True)
        h = (h - mu) * jax.lax.rsqrt(var + LN_EPS) * ln_gamma + ln_beta
        residual = h
        a1, a2 = (a[:Fout, 0], a[Fout:, 0])
        s1 = h @ a1
        s2 = h @ a2
        e = jax.nn.leaky_relu(s1[:, :, None] + s2[:, None, :], negative_slope=ALPHA)
        attention = jnp.where(adj[None, :, :] > 0, e, NEG_INF)
        attention = jax.nn.softmax(attention, axis=-1)
        h_prime = jnp.einsum('bij,bjo->bio', attention, h) + residual
        return jax.nn.elu(h_prime)

    def _L1_gnn_ref(x, adjacency, W_q, W_k, W_v, W_o, b_o):
        import jax, jax.numpy as jnp
        import numpy as np
        IN_DIM = 128
        OUT_DIM = 128
        NUM_HEADS = 4
        HEAD_DIM = OUT_DIM // NUM_HEADS
        B, N = (4, 4096)
        Bn, Nn, _ = x.shape
        q = (x @ W_q).reshape(Bn, Nn, NUM_HEADS, HEAD_DIM).transpose(0, 2, 1, 3)
        k = (x @ W_k).reshape(Bn, Nn, NUM_HEADS, HEAD_DIM).transpose(0, 2, 1, 3)
        v = (x @ W_v).reshape(Bn, Nn, NUM_HEADS, HEAD_DIM).transpose(0, 2, 1, 3)
        scores = jnp.einsum('bhnd,bhmd->bhnm', q, k) / np.sqrt(HEAD_DIM).astype(np.float32)
        adj = adjacency[None, None, :, :]
        scores = jnp.where(adj == 0, -jnp.inf, scores)
        attn = jax.nn.softmax(scores, axis=-1)
        out = jnp.einsum('bhnm,bhmd->bhnd', attn, v)
        out = out.transpose(0, 2, 1, 3).reshape(Bn, Nn, NUM_HEADS * HEAD_DIM)
        return out @ W_o + b_o

    def _L2_gnn_ref(x, adj_matrix, W_self, b_self, W_neigh, b_neigh):
        import jax, jax.numpy as jnp
        import numpy as np
        B, N, F_IN, F_OUT = (4, 8192, 128, 128)
        mask = (adj_matrix > 0).astype(x.dtype)
        deg = jnp.sum(mask, axis=-1)
        agg = jnp.einsum('ij,bjf->bif', mask, x)
        agg = agg / jnp.maximum(deg, 1.0)[None, :, None]
        self_out = x @ W_self + b_self
        neigh_out = agg @ W_neigh + b_neigh
        neigh_out = jnp.where((deg > 0)[None, :, None], neigh_out, 0.0)
        return jax.nn.relu(self_out + neigh_out)

    def _L3_gnn_ref(x, adj, W, a):
        import jax, jax.numpy as jnp
        import numpy as np
        B, N, F_IN, F_OUT = (8, 2048, 128, 128)
        h = jnp.einsum('bni,oi->bno', x, W)
        fo = W.shape[0]
        a_src = a[:fo, 0]
        a_dst = a[fo:, 0]
        s = jnp.einsum('bnf,f->bn', h, a_src)
        d = jnp.einsum('bnf,f->bn', h, a_dst)
        e = s[:, :, None] + d[:, None, :]
        e = jnp.where(e > 0, e, 0.2 * e)
        e = jnp.where(adj[None, :, :] == 0, jnp.float32(-1000000000.0), e)
        attention = jax.nn.softmax(e, axis=-1)
        return jnp.einsum('bij,bjf->bif', attention, h)

    h = jnp.maximum(_layernorm(x, axis=-1), 0.0)
    x = x + _L0_gnn_ref(h, adj, L0_gnn_W, L0_gnn_a, L0_gnn_node_weights, L0_gnn_node_bias, L0_gnn_ln_gamma, L0_gnn_ln_beta)
    h = jnp.maximum(_layernorm(x, axis=-1), 0.0)
    x = x + _L1_gnn_ref(h, adj, L1_gnn_W_q, L1_gnn_W_k, L1_gnn_W_v, L1_gnn_W_o, L1_gnn_b_o)
    h = jnp.maximum(_layernorm(x, axis=-1), 0.0)
    x = x + _L2_gnn_ref(h, adj, L2_gnn_W_self, L2_gnn_b_self, L2_gnn_W_neigh, L2_gnn_b_neigh)
    h = jnp.maximum(_layernorm(x, axis=-1), 0.0)
    x = x + _L3_gnn_ref(h, adj, L3_gnn_W, L3_gnn_a)
    return x


_drawn_inputs = setup_inputs


def setup_inputs(seed=0):
    import zlib

    import numpy as np

    out = dict(_drawn_inputs(seed))
    spreads = {'L0_gnn_node_bias': (0.0, 0.1),
     'L0_gnn_ln_gamma': (1.0, 0.2),
     'L0_gnn_ln_beta': (0.0, 0.1)}
    factors = {'L1_gnn_W_q': 8.0, 'L1_gnn_W_k': 8.0, 'L3_gnn_a': 8.0}
    for name, (base, spread) in spreads.items():
        noise = np.random.default_rng([zlib.crc32(name.encode()), seed]).standard_normal(out[name].shape)
        drawn = base * np.exp(spread * noise) if base else spread * noise
        out[name] = jnp.asarray(drawn.astype(out[name].dtype))
    for name, factor in factors.items():
        out[name] = (out[name] * factor).astype(out[name].dtype)
    return out
```

```python
from contextlib import ExitStack

import concourse.bass as bass
from concourse import mybir

ALU = mybir.AluOpType
ACT = mybir.ActivationFunctionType
AX = mybir.AxisListType
F32 = mybir.dt.float32
F16 = mybir.dt.float16
BF16 = mybir.dt.bfloat16
I32 = mybir.dt.int32

P = 128
B = 8
N = 2048
F = 128
T = N // P
HEADS = 4
HD = F // HEADS
BANK = 512
CH = N // BANK
LN_EPS = 1e-5
SLOPE = 0.2
LEVELS = 64
MASKED = 1.0e30
SHIFT_UNIT = 1024.0


class Scope:

    used_sems = []

    def __init__(self, nc, stack, name):
        self.nc, self.stack, self.name = nc, stack, name

    def sb(self, name, shape, dtype=F32):
        return self.stack.enter_context(self.nc.sbuf_tensor(f"{self.name}_{name}", shape, dtype))

    def ps(self, name, shape, dtype=F32):
        return self.stack.enter_context(self.nc.psum_tensor(f"{self.name}_{name}", shape, dtype))

    def sem(self, name):
        sem = self.nc.alloc_semaphore(name=f"{self.name}_{name}")
        self.used_sems.append(sem)
        return sem

    def block(self):
        return self.stack.enter_context(self.nc.Block())


def clear_semaphores(nc):
    nc.clear_and_free_semaphores(list(Scope.used_sems))
    Scope.used_sems.clear()
    nc.all_engine_barrier()


def node_tiles(dram, b):
    return dram[bass.ds(b, 1)].rearrange("one (p t) f -> p (one t f)", p=P)


def flat(buf):
    return buf.rearrange("p t f -> p (t f)")


def norm_stats(nc, dve, st, tmp, rstd, shift, done, base, rooted, roots):
    mean2, diff, ssq, var = (tmp[:, k, :] for k in range(4))
    nc.vector.tensor_tensor(mean2, st[:, :, 1], st[:, :, 4], ALU.add).then_inc(done, 1)
    nc.vector.tensor_tensor(diff, st[:, :, 1], st[:, :, 4], ALU.subtract).then_inc(done, 1)
    nc.vector.tensor_tensor(ssq, st[:, :, 2], st[:, :, 5], ALU.add).then_inc(done, 1)
    dve.wait_ge(done, base + 2)
    nc.vector.scalar_tensor_tensor(out=diff, in0=diff, scalar=0.25, in1=diff,
                                   op0=ALU.mult, op1=ALU.mult).then_inc(done, 1)
    dve.wait_ge(done, base + 3)
    nc.vector.tensor_scalar(ssq, ssq, 1.0 / F, LN_EPS, ALU.mult, ALU.add).then_inc(done, 1)
    dve.wait_ge(done, base + 5)
    nc.vector.tensor_tensor(var, ssq, diff, ALU.add).then_inc(done, 1)
    dve.wait_ge(rooted, roots)
    nc.vector.scalar_tensor_tensor(out=shift, in0=mean2, scalar=-0.5, in1=rstd,
                                   op0=ALU.mult, op1=ALU.mult).then_inc(done, 1)


def norm_root(nc, pool, tmp, minus_half, rstd, done, value, rooted):
    pool.wait_ge(done, value)
    nc.gpsimd.tensor_tensor(rstd, tmp[:, 3, :], minus_half, ALU.pow).then_inc(rooted, 1)


NORM_STEPS = 7


def masks_and_nodes0(nc, io, keep):
    with ExitStack() as stack:
        s = Scope(nc, stack, "p0")
        adj_in = s.sb("adj_in", [P, 2, N], I32)
        m01 = s.sb("m01", [P, 2, N], BF16)
        mbias = s.sb("mbias", [P, 2, N], BF16)
        x = s.sb("x", [P, T, F])
        hn = s.sb("hn", [P, T, F])
        hT = s.sb("hT", [P, N])
        h0 = s.sb("h0", [P, T, F])
        h = s.sb("h", [P, T, F + 1])
        w = s.sb("w", [P, F])
        gamma = s.sb("gamma", [P, F])
        beta = s.sb("beta", [P, F])
        a12 = s.sb("a12", [P, 2, F])
        nw = s.sb("nw", [P, T])
        nw1 = s.sb("nw1", [P, T])
        nb = s.sb("nb", [P, T])
        stx = s.sb("stx", [P, T, 6])
        sth = s.sb("sth", [P, T, 6])
        tmp = s.sb("tmp", [P, 4, T])
        rstd_x, shift_x = s.sb("rstd_x", [P, T]), s.sb("shift_x", [P, T])
        rstd_h, shift_h = s.sb("rstd_h", [P, T]), s.sb("shift_h", [P, T])
        dots = s.sb("dots", [P, 2, T])
        products = s.sb("products", [P, T, F])
        minus_half = s.sb("minus_half", [P, T])
        mt_ps = s.ps("mt_ps", [P, 2, T, P], BF16)
        tp_ps = s.ps("tp_ps", [P, 2, BANK])
        pj_ps = s.ps("pj_ps", [P, 2, BANK])

        weights_in, ident_zero, ident_ready = s.sem("weights_in"), s.sem("ident_zero"), s.sem("ident_ready")
        adj_loaded, x_loaded = [s.sem(f"adj_loaded{k}") for k in range(2)], s.sem("x_loaded")
        m01_ready, mbias_ready = s.sem("m01_ready"), s.sem("mbias_ready")
        mbias_stored = [s.sem(f"mbias_stored{k}") for k in range(2)]
        mt_turned, mt_kept = s.sem("mt_turned"), s.sem("mt_kept")
        consts_ready, chain, rooted = s.sem("consts_ready"), s.sem("chain"), s.sem("rooted")
        x_normed, x_scaled, h_turned, hT_kept = s.sem("x_normed"), s.sem("x_scaled"), s.sem("h_turned"), s.sem("hT_kept")
        projected, h0_kept, h0_normed = s.sem("projected"), s.sem("h0_kept"), s.sem("h0_normed")
        gamma_done, h_ready, dots_done, h_stored = s.sem("gamma_done"), s.sem("h_ready"), s.sem("dots_done"), s.sem("h_stored")
        block = s.block()
        CHAIN = 2 * NORM_STEPS + 2

        @block.sync
        def _(sp):
            sp.dma_start(w[:], io["L0_gnn_W"][:]).then_inc(weights_in, 16)
            sp.dma_start(gamma[:], io["L0_gnn_ln_gamma"][0:1, :].partition_broadcast(P)).then_inc(weights_in, 16)
            sp.dma_start(beta[:], io["L0_gnn_ln_beta"][0:1, :].partition_broadcast(P)).then_inc(weights_in, 16)
            for k in range(2):
                sp.dma_start(a12[:, k, :], io["L0_gnn_a"][k:k + 1, :].partition_broadcast(P)).then_inc(weights_in, 16)
            sp.dma_start(nw[:], io["L0_gnn_node_weights"][:]).then_inc(weights_in, 16)
            sp.dma_start(nb[:], io["L0_gnn_node_bias"][:]).then_inc(weights_in, 16)
            with sp.Fori(0, B) as b:
                sp.wait_ge(x_normed, b + 1)
                sp.dma_start(flat(x[:]), node_tiles(io["x"], b)).then_inc(x_loaded, 16)
                for k in range(2):
                    sp.wait_ge(m01_ready, 2 * b + k + 1)
                    sp.dma_start(adj_in[:, k, :], io["adj"].rearrange("(p t) j -> p t j", t=T)[:, bass.ds(2 * b + k, 1), :].rearrange("p one j -> p (one j)")).then_inc(adj_loaded[k], 16)

        @block.gpsimd
        def _(pool):
            nc.gpsimd.memset(keep["ident"][:], 0.0).then_inc(ident_zero, 1)
            nc.gpsimd.memset(keep["ident16"][:], 0.0).then_inc(ident_zero, 1)
            nc.gpsimd.memset(h[:, :, F:F + 1], 1.0).then_inc(consts_ready, 1)
            nc.gpsimd.memset(minus_half[:], -0.5).then_inc(ident_zero, 1)
            pool.wait_ge(ident_zero, 3)
            for m in (keep["ident"], keep["ident16"]):
                nc.gpsimd.affine_select(out=m[:], in_=m[:], compare_op=ALU.not_equal, fill=1.0, base=0,
                                        pattern=[[-1, P]], channel_multiplier=1).then_inc(ident_ready, 1)
            with pool.Fori(0, B) as b:
                norm_root(nc, pool, tmp, minus_half[:], rstd_x[:], chain, b * CHAIN + NORM_STEPS, rooted)
                for k in range(2):
                    pool.wait_ge(mbias_ready, 2 * b + k + 1)
                    pool.dma_start(io["mask_bias"][bass.ds((2 * b + k) * P, P), :], mbias[:, k, :]).then_inc(mbias_stored[k], 16)
                norm_root(nc, pool, tmp, minus_half[:], rstd_h[:], chain, b * CHAIN + 2 * NORM_STEPS + 1, rooted)
                pool.wait_ge(gamma_done, b + 1)
                pool.wait_ge(h_stored, 16 * b)
                pool.wait_ge(dots_done, 2 * b)
                nc.gpsimd.tensor_tensor(h[:, :, 0:F], h0[:], beta[:].unsqueeze(1).to_broadcast([P, T, F]),
                                        ALU.add).then_inc(h_ready, 1)
                pool.wait_ge(h_ready, b + 1)
                pool.dma_start(io["h_nodes"][bass.ds(b, 1)].rearrange("one p t f -> p (one t) f"), h[:]).then_inc(h_stored, 16)
            for k in range(2):
                pool.wait_ge(mbias_stored[k], 16 * B)
            pool.wait_ge(h_stored, 16 * B)

        @block.vector
        def _(dve):
            dve.sem_inc(m01_ready, 2)
            dve.wait_ge(weights_in, 16 * 7)
            nc.vector.tensor_scalar(nw1[:], nw[:], 1.0, None, ALU.add).then_inc(consts_ready, 1)
            dve.wait_ge(consts_ready, 2)
            with dve.Fori(0, B) as b:
                for k in range(2):
                    dve.wait_ge(adj_loaded[k], 16 * (b + 1))
                    dve.wait_ge(mt_turned, 2 * b + k + 1)
                    nc.vector.tensor_scalar(m01[:, k, :].rearrange("p (t q) -> p t q", q=P),
                                            adj_in[:, k, :].rearrange("p (q t) -> p t q", t=T), 0, None, ALU.is_gt).then_inc(m01_ready, 1)
                    dve.wait_ge(m01_ready, 2 * b + k + 3)
                    dve.wait_ge(mbias_stored[k], 16 * b)
                    nc.vector.tensor_scalar(mbias[:, k, :], m01[:, k, :], MASKED, -MASKED,
                                            ALU.mult, ALU.add).then_inc(mbias_ready, 1)
                dve.wait_ge(x_loaded, 16 * (b + 1))
                for t in range(T):
                    last = nc.vector.bn_stats(stx[:, t, :], x[:, t, :])
                last.then_inc(chain, 1)
                dve.wait_ge(chain, b * CHAIN + 1)
                norm_stats(nc, dve, stx, tmp, rstd_x[:], shift_x[:], chain, b * CHAIN + 1, rooted, 2 * b + 1)
                dve.wait_ge(x_normed, b + 2)
                for t in range(T):
                    last = nc.vector.tensor_scalar(hn[:, t, :], hn[:, t, :], nw1[:, t:t + 1], nb[:, t:t + 1],
                                                   ALU.mult, ALU.add)
                last.then_inc(x_scaled, 1)
                dve.wait_ge(h0_kept, CH * (b + 1) + 2)
                for t in range(T):
                    last = nc.vector.bn_stats(sth[:, t, :], h0[:, t, :])
                last.then_inc(chain, 1)
                dve.wait_ge(chain, b * CHAIN + NORM_STEPS + 2)
                norm_stats(nc, dve, sth, tmp, rstd_h[:], shift_h[:], chain, b * CHAIN + NORM_STEPS + 2,
                           rooted, 2 * b + 2)
                dve.wait_ge(h0_normed, b + 1)
                nc.vector.tensor_tensor(h0[:], h0[:], gamma[:].unsqueeze(1).to_broadcast([P, T, F]),
                                        ALU.mult).then_inc(gamma_done, 1)
                dve.wait_ge(h_ready, b + 1)
                for k in range(2):
                    for t in range(T):
                        last = nc.vector.tensor_tensor_reduce(
                            out=products[:, t, :], in0=h[:, t, 0:F], in1=a12[:, k, :], scale=1.0, scalar=0.0,
                            op0=ALU.mult, op1=ALU.add, accum_out=dots[:, k, t:t + 1])
                    last.then_inc(dots_done, 1)
                    dve.wait_ge(dots_done, 2 * b + k + 1)
                nc.vector.tensor_copy(keep["s1"][:, bass.ds(b, 1), :], dots[:, 0:1, :])
                nc.vector.tensor_copy(keep["s2"][:, bass.ds(b, 1), :], dots[:, 1:2, :])

        @block.scalar
        def _(act):
            act.sem_inc(x_normed, 1)
            act.sem_inc(mt_kept, 2)
            act.sem_inc(hT_kept, 2)
            act.sem_inc(h0_kept, 2)
            with act.Fori(0, B) as b:
                for k in range(2):
                    act.wait_ge(mt_turned, 2 * b + k + 3)
                    nc.scalar.activation(keep["mask_t"][:, :, bass.ds((2 * b + k) * P, P)], mt_ps[:, k],
                                         ACT.Copy).then_inc(mt_kept, 1)
                act.wait_ge(chain, b * CHAIN + NORM_STEPS + 1)
                act.wait_ge(h_turned, CH * b + 1)
                for t in range(T):
                    last = nc.scalar.activation(hn[:, t, :], x[:, t, :], ACT.Relu, bias=shift_x[:, t:t + 1],
                                                scale=rstd_x[:, t:t + 1])
                last.then_inc(x_normed, 1)
                act.wait_ge(h_ready, b)
                for q in range(CH):
                    act.wait_ge(h_turned, CH * b + q + 2)
                    nc.scalar.copy(hT[:, q * BANK:(q + 1) * BANK], tp_ps[:, q % 2, :]).then_inc(hT_kept, 1)
                    act.wait_ge(projected, CH * b + q + 1)
                    nc.scalar.copy(h0[:, 4 * q:4 * q + 4, :],
                                   pj_ps[:, q % 2, :].rearrange("p (t f) -> p t f", f=F)).then_inc(h0_kept, 1)
                act.wait_ge(chain, (b + 1) * CHAIN)
                for t in range(T):
                    last = nc.scalar.activation(h0[:, t, :], h0[:, t, :], ACT.Identity, bias=shift_h[:, t:t + 1],
                                                scale=rstd_h[:, t:t + 1])
                last.then_inc(h0_normed, 1)

        @block.tensor
        def _(pe):
            pe.sem_inc(mt_turned, 2)
            pe.sem_inc(h_turned, 1)
            pe.wait_ge(ident_ready, 2)
            pe.wait_ge(weights_in, 16 * 7)
            with pe.Fori(0, B) as b:
                for k in range(2):
                    pe.wait_ge(m01_ready, 2 * b + k + 3)
                    pe.wait_ge(mt_kept, 2 * b + k + 1)
                    for t in range(T):
                        mm = nc.tensor.transpose(mt_ps[:, k, t, :], m01[:, k, t * P:(t + 1) * P], keep["ident16"][:])
                    mm.then_inc(mt_turned, 1)
                pe.wait_ge(x_scaled, b + 1)
                for q in range(CH):
                    pe.wait_ge(hT_kept, CH * b + q + 1)
                    for t in range(4 * q, 4 * q + 4):
                        mm = nc.tensor.transpose(tp_ps[:, q % 2, (t % 4) * P:(t % 4 + 1) * P], hn[:, t, :], keep["ident"][:])
                    mm.then_inc(h_turned, 1)
                    pe.wait_ge(hT_kept, CH * b + q + 3)
                    pe.wait_ge(h0_kept, CH * b + q + 1)
                    for t in range(4 * q, 4 * q + 4):
                        mm = nc.tensor.matmul(pj_ps[:, q % 2, (t % 4) * P:(t % 4 + 1) * P], hT[:, t * P:(t + 1) * P],
                                              w[:], start=True, stop=True)
                    mm.then_inc(projected, 1)

def row_shifts(nc, io, keep, name, first):
    with ExitStack() as stack:
        s = Scope(nc, stack, name)
        ext = s.sb("ext", [P, 2 * B])
        ext_col = s.sb("ext_col", [2 * B, 1])
        ext_diag = s.sb("ext_diag", [2 * B, 2 * B])
        ones = s.sb("ones", [2 * B, P])
        ext_all = s.sb("ext_all", [P, 2 * B])
        step = s.sb("step", [P, B])
        lev_i = s.sb("lev_i", [P, LEVELS], I32)
        lev = s.sb("lev", [P, LEVELS])
        rank = s.sb("rank", [P, B, LEVELS], BF16)
        tau = s.sb("tau", [P, B, LEVELS])
        above = s.sb("above", [P, T, B * LEVELS], BF16)
        hit = s.sb("hit", [P, 2, B * LEVELS], BF16)
        top = s.sb("top", [P, B, T])
        lk = s.sb("lk", [P, B, T])
        deg = s.sb("deg", [P, T])
        rows = s.sb("rows", [P, 2, P])
        ext_ps = s.ps("ext_ps", [2 * B, P])
        all_ps = s.ps("all_ps", [P, 2 * B])
        cnt_ps = s.ps("cnt_ps", [P, 4, BANK])
        rows_ps = s.ps("rows_ps", [P, 2, P])
        levels_in, step_done = s.sem("levels_in"), s.sem("step_done")
        ext_done, ext_turned, diag_done, spread = s.sem("ext_done"), s.sem("ext_turned"), s.sem("diag_done"), s.sem("spread")
        above_done, counted, hit_done, top_done = s.sem("above_done"), s.sem("counted"), s.sem("hit_done"), s.sem("top_done")
        shifts_done, rows_turned, rows_kept, rows_stored = (s.sem("shifts_done"), s.sem("rows_turned"), s.sem("rows_kept"),
                                                            s.sem("rows_stored"))
        block = s.block()
        s1, s2 = keep["s1"], keep["s2"]

        @block.gpsimd
        def _(pool):
            nc.gpsimd.memset(ones[:], 1.0).then_inc(levels_in, 1)
            nc.gpsimd.iota(lev_i[:], pattern=[[1, LEVELS]], base=0, channel_multiplier=0).then_inc(levels_in, 1)

        @block.vector
        def _(dve):
            nc.vector.tensor_reduce(ext[:, 0:B], s2[:], AX.X, ALU.max).then_inc(ext_done, 1)
            nc.vector.tensor_reduce(ext[:, B:2 * B], s2[:], AX.X, ALU.min, negate=True).then_inc(ext_done, 1)
            nc.vector.tensor_scalar(keep["s2_08"][:], s2[:], 1.0 - SLOPE, None, ALU.mult)
            nc.vector.tensor_scalar(keep["s2_02"][:], s2[:], SLOPE, None, ALU.mult)
            dve.wait_ge(levels_in, 2)
            nc.vector.tensor_copy(lev[:], lev_i[:]).then_inc(step_done, 1)
            dve.wait_ge(step_done, 1)
            nc.vector.tensor_scalar(rank[:], lev[:].unsqueeze(1).to_broadcast([P, B, LEVELS]), 1.0, None, ALU.add).then_inc(step_done, 1)
            dve.wait_ge(ext_turned, 1)
            nc.vector.tensor_reduce(ext_col[:], ext_ps[:], AX.X, ALU.max).then_inc(diag_done, 1)
            dve.wait_ge(diag_done, 1)
            nc.vector.tensor_scalar(ext_diag[:], keep["ident"][0:2 * B, 0:2 * B], ext_col[:, 0:1], None, ALU.mult).then_inc(diag_done, 1)
            dve.wait_ge(spread, 1)
            nc.vector.tensor_copy(ext_all[:], all_ps[:]).then_inc(step_done, 1)
            dve.wait_ge(step_done, 3)
            nc.vector.tensor_tensor(step[:], ext_all[:, 0:B], ext_all[:, B:2 * B], ALU.add).then_inc(step_done, 1)
            dve.wait_ge(step_done, 4)
            nc.vector.tensor_scalar(step[:], step[:], 1.0 / (LEVELS - 1), None, ALU.mult).then_inc(step_done, 1)
            dve.wait_ge(step_done, 5)
            for b in range(B):
                last = nc.vector.tensor_scalar(tau[:, b, :], lev[:], step[:, b:b + 1], ext_all[:, B + b:B + b + 1],
                                               ALU.mult, ALU.subtract)
            last.then_inc(step_done, 1)
            dve.wait_ge(step_done, 6)
            for t in range(T):
                nc.vector.tensor_tensor(above[:, t, :].rearrange("p (b l) -> p b l", l=LEVELS),
                                        s2[:, :, t:t + 1].to_broadcast([P, B, LEVELS]), tau[:], ALU.is_ge).then_inc(above_done, 1)
            for t in range(T):
                dve.wait_ge(counted, t + 1)
                if first:
                    nc.vector.tensor_copy(deg[:, t:t + 1], cnt_ps[:, t % 4, 0:1])
                if t >= 2:
                    dve.wait_ge(top_done, t - 1)
                nc.vector.scalar_tensor_tensor(out=hit[:, t % 2, :], in0=cnt_ps[:, t % 4, :], scalar=0.0,
                                               in1=rank[:].rearrange("p b l -> p (b l)"), op0=ALU.is_gt, op1=ALU.mult).then_inc(hit_done, 1)
                dve.wait_ge(hit_done, t + 1)
                nc.vector.tensor_reduce(top[:, :, t], hit[:, t % 2, :].rearrange("p (b l) -> p b l", l=LEVELS),
                                        AX.X, ALU.max).then_inc(top_done, 1)
            by_batch = [P, B, T]
            dve.wait_ge(top_done, T)
            nc.vector.tensor_scalar(top[:], top[:], -1.0, None, ALU.add).then_inc(shifts_done, 1)
            dve.wait_ge(shifts_done, 1)
            nc.vector.tensor_tensor(top[:], top[:], step[:].unsqueeze(2).to_broadcast(by_batch), ALU.mult).then_inc(shifts_done, 1)
            dve.wait_ge(shifts_done, 2)
            nc.vector.tensor_tensor(top[:], top[:], ext_all[:, B:2 * B].unsqueeze(2).to_broadcast(by_batch),
                                    ALU.subtract).then_inc(shifts_done, 1)
            dve.wait_ge(shifts_done, 3)
            nc.vector.tensor_tensor(top[:], top[:], s1[:], ALU.add).then_inc(shifts_done, 1)
            dve.wait_ge(shifts_done, 4)
            nc.vector.scalar_tensor_tensor(out=lk[:], in0=top[:], scalar=SLOPE, in1=top[:], op0=ALU.mult, op1=ALU.max).then_inc(shifts_done, 1)
            dve.wait_ge(shifts_done, 5)
            nc.vector.tensor_tensor(keep["u"][:], s1[:], lk[:], ALU.subtract).then_inc(shifts_done, 1)
            nc.vector.scalar_tensor_tensor(out=keep["v"][:], in0=s1[:], scalar=SLOPE, in1=lk[:], op0=ALU.mult,
                                           op1=ALU.subtract).then_inc(shifts_done, 1)
            if first:
                nc.vector.tensor_scalar(keep["has_deg"][:], deg[:], 0.0, None, ALU.is_gt).then_inc(shifts_done, 1)
                nc.vector.tensor_scalar(deg[:], deg[:], 1.0, None, ALU.max).then_inc(shifts_done, 1)
                dve.wait_ge(shifts_done, 9)
                nc.vector.reciprocal(keep["rdeg"][:], deg[:]).then_inc(shifts_done, 1)
            dve.wait_ge(rows_turned, 1)
            nc.vector.tensor_copy(rows[:], rows_ps[:]).then_inc(rows_kept, 1)

        @block.tensor
        def _(pe):
            pe.wait_ge(ext_done, 2)
            nc.tensor.transpose(ext_ps[:], ext[:], keep["ident"][:]).then_inc(ext_turned, 1)
            pe.wait_ge(levels_in, 2)
            pe.wait_ge(diag_done, 2)
            nc.tensor.matmul(all_ps[:], ones[:], ext_diag[:], start=True, stop=True).then_inc(spread, 1)
            for it in range(T):
                if it >= 4:
                    pe.wait_ge(hit_done, it - 3)
                for jt in range(T):
                    if it == 0:
                        pe.wait_ge(above_done, jt + 1)
                    mm = nc.tensor.matmul(cnt_ps[:, it % 4, :], keep["mask_t"][:, jt, it * P:(it + 1) * P], above[:, jt, :],
                                          start=(jt == 0), stop=(jt == T - 1))
                mm.then_inc(counted, 1)
            pe.wait_ge(shifts_done, 7)
            for k, m in enumerate(("u", "v")):
                mm = nc.tensor.transpose(rows_ps[:, k, :], keep[m][:].rearrange("p b t -> p (b t)"), keep["ident"][:])
            mm.then_inc(rows_turned, 1)

        @block.sync
        def _(sp):
            sp.wait_ge(rows_kept, 1)
            for k, m in enumerate(("u_rows", "v_rows")):
                sp.dma_start(io[m].rearrange("b (t p) -> (b t) p", p=P), rows[:, k, :]).then_inc(rows_stored, 16)
            sp.wait_ge(rows_stored, 32)


def gat_attention(nc, io, keep, name, x_in, x_out, residual_elu):
    HALF = N // 2
    IT = HALF // P
    STEPS = 4 * T
    ZB, PB = 2, 4
    mine = [g for g in range(STEPS) if g % 4 == 1]
    FIN = 2
    with ExitStack() as stack:
        s = Scope(nc, stack, name)
        h = s.sb("h", [P, 2, T, F + 1])
        x = s.sb("x", [P, 2, T, F])
        urow = s.sb("urow", [P, 2, N])
        vrow = s.sb("vrow", [P, 2, N])
        s2_02 = s.sb("s2_02", [P, 2, T])
        z = s.sb("z", [P, ZB, HALF])
        w = s.sb("w", [P, PB, HALF])
        rz = s.sb("rz", [P, IT])
        y = s.sb("y", [P, IT, F])
        e = s.sb("e", [P, IT, F])
        o = s.sb("o", [P, IT, F])
        acc = s.ps("acc", [P, 2, 3, BANK])
        h_loaded, x_loaded = [s.sem(f"h_loaded{k}") for k in range(2)], [s.sem(f"x_loaded{k}") for k in range(2)]
        rows_loaded = [s.sem(f"rows_loaded{k}") for k in range(2)]
        z_ready, exp_done, masked_pool, masked_dve = s.sem("z_ready"), s.sem("exp_done"), s.sem("masked_pool"), s.sem("masked_dve")
        weighed, drained = s.sem("weighed"), s.sem("drained")
        rz_done, y_ready, e_ready, o_ready, o_stored, r_done = (s.sem("rz_done"), s.sem("y_ready"), s.sem("e_ready"),
                                                                s.sem("o_ready"), [s.sem(f"o_stored{k}") for k in range(2)], s.sem("r_done"))
        block = s.block()

        def tile(half, it):
            return acc[:, half, it // 3, (it % 3) * (F + 1):(it % 3 + 1) * (F + 1)]

        def half_rows(dram, b, half):
            return node_tiles(dram, b)[:, half * IT * F:(half + 1) * IT * F]

        @block.sync
        def _(sp):
            def load(b, k):
                sp.dma_start(h[:, k], io["h_nodes"][bass.ds(b, 1)].rearrange("one p t f -> p (one t) f")).then_inc(h_loaded[k], 16)
                for rows, m in ((urow, "u_rows"), (vrow, "v_rows")):
                    sp.dma_start(rows[:, k, :], io[m][bass.ds(b, 1), :].partition_broadcast(P)).then_inc(rows_loaded[k], 16)
                sp.dma_start(flat(x[:, k]), node_tiles(x_in, b)).then_inc(x_loaded[k], 16)

            def store(b, half, n):
                if residual_elu:
                    sp.wait_ge(o_ready, n + 1)
                else:
                    sp.wait_ge(drained, n + 2)
                sp.dma_start(half_rows(x_out, b, half), flat(o[:])).then_inc(o_stored[half], 16)

            load(0, 0)
            load(1, 1)
            with sp.Fori(0, B // 2) as i:
                with sp.If(i > 0):
                    store(nc.s_assert_within(2 * i - 1, 0, B - 1, skip_runtime_bounds_check_because="only where i > 0"), 1, 4 * i)
                    load(2 * i + 1, 1)
                store(2 * i, 0, 4 * i + 1)
                store(2 * i, 1, 4 * i + 2)
                with sp.If(i < B // 2 - 1):
                    load(nc.s_assert_within(2 * i + 2, 0, B - 1, skip_runtime_bounds_check_because="only before the last i"), 0)
                store(2 * i + 1, 0, 4 * i + 3)
            store(B - 1, 1, 2 * B)
            for half in range(2):
                sp.wait_ge(o_stored[half], 16 * B)

        @block.vector
        def _(dve):
            def stored_before(half, stores):
                dve.wait_ge(o_stored[1 - half], 16 * stores)

            def finish(k, half, n, stores):
                dve.wait_ge(weighed, T * (n + 1) + PB)
                sums = acc[:, half, :, 0:3 * (F + 1)].rearrange("p k (i f) -> p k i f", f=F + 1)[:, :, :, F]
                nc.vector.reciprocal(rz[:, 0:6].rearrange("p (k i) -> p k i", i=3), sums[:, 0:2, :])
                nc.vector.reciprocal(rz[:, 6:8], sums[:, 2, 0:2]).then_inc(rz_done, 1)
                dve.wait_ge(rz_done, n + 1)
                if not residual_elu:
                    stored_before(half, stores)
                for it in range(IT):
                    add = h[:, k, half * IT + it, 0:F] if residual_elu else x[:, k, half * IT + it, :]
                    last = nc.vector.scalar_tensor_tensor(out=(y if residual_elu else o)[:, it, :], in0=tile(half, it)[:, 0:F],
                                                          scalar=rz[:, it:it + 1], in1=add, op0=ALU.mult, op1=ALU.add)
                last.then_inc(drained, 1)

            def finish_elu(k, half, n, stores):
                dve.wait_ge(drained, n + 1 + 2)
                stored_before(half, stores)
                nc.vector.scalar_tensor_tensor(out=o[:], in0=y[:], scalar=0.0, in1=x[:, k, half * IT:(half + 1) * IT, :],
                                               op0=ALU.max, op1=ALU.add).then_inc(r_done, 1)
                dve.wait_ge(e_ready, n + 1)
                nc.vector.tensor_scalar(e[:], e[:], 1.0, -1.0, ALU.min, ALU.add).then_inc(r_done, 1)
                dve.wait_ge(r_done, 2 * n + 2)
                nc.vector.tensor_tensor(o[:], o[:], e[:], ALU.add).then_inc(o_ready, 1)

            def finish_all(k, half, n, stores, stage):
                if stage == 0:
                    finish(k, half, n, stores)
                elif residual_elu:
                    finish_elu(k, half, n, stores)

            dve.sem_inc(drained, 2)
            dve.sem_inc(o_ready, 1)
            with dve.Fori(0, B // 2) as i:
                for g in range(STEPS):
                    k, half, jt = g // (2 * T), g // T % 2, g % T
                    b = 2 * i + k
                    if g % (2 * T) == 0:
                        dve.wait_ge(rows_loaded[k], 32 * (i + 1))
                        dve.wait_ge(h_loaded[k], 16 * (i + 1))
                        dve.wait_ge(x_loaded[k], 16 * (i + 1))
                    dve.wait_ge(exp_done, STEPS * i + g + 1)
                    if g % (2 * T) == 0:
                        nc.vector.tensor_copy(s2_02[:, k:k + 1, :], keep["s2_02"][:, bass.ds(b, 1), :])
                    rows = slice(half * HALF, (half + 1) * HALF)
                    nc.vector.scalar_tensor_tensor(out=z[:, g % ZB, :], in0=urow[:, k, rows], scalar=keep["s2_08"][:, bass.ds(b, 1), jt],
                                                   in1=vrow[:, k, rows], op0=ALU.add, op1=ALU.max).then_inc(z_ready, 1)
                    if g - 1 in mine:
                        dve.wait_ge(exp_done, STEPS * i + g + ZB)
                        q = (g - 1) % PB
                        m_half, m_jt = (g - 1) // T % 2, (g - 1) % T
                        nc.vector.tensor_tensor(w[:, q, :], w[:, q, :], keep["mask_t"][:, m_jt, m_half * HALF:(m_half + 1) * HALF],
                                                ALU.mult).then_inc(masked_dve, 1)
                    for stage, at in ((0, FIN), (1, FIN + 2)):
                        if g % T == at:
                            n = g // T - 1
                            if n >= 0:
                                finish_all(n // 2, n % 2, 4 * i + n, 2 * i + (n + 1) // 2, stage)
                            else:
                                with dve.If(i > 0):
                                    finish_all(1, 1, 4 * i - 1, 2 * i, stage)
            for stage in range(2):
                finish_all(1, 1, 2 * B - 1, B, stage)

        @block.scalar
        def _(act):
            def exp_y(n):
                act.wait_ge(drained, n + 1 + 2)
                if residual_elu:
                    act.wait_ge(o_ready, n + 1)
                    nc.scalar.activation(e[:], y[:], ACT.Exp).then_inc(e_ready, 1)

            act.sem_inc(exp_done, ZB)
            with act.Fori(0, B // 2) as i:
                for g in range(STEPS):
                    k, jt = g // (2 * T), g % T
                    act.wait_ge(z_ready, STEPS * i + g + 1)
                    act.wait_ge(weighed, STEPS * i + g + 1)
                    nc.scalar.activation(w[:, g % PB, :], z[:, g % ZB, :], ACT.Exp,
                                         bias=s2_02[:, k, jt:jt + 1]).then_inc(exp_done, 1)
                    if g % T == FIN + 1 and residual_elu:
                        n = g // T - 1
                        if n >= 0:
                            exp_y(4 * i + n)
                        else:
                            with act.If(i > 0):
                                exp_y(4 * i - 1)
            if residual_elu:
                exp_y(2 * B - 1)

        @block.gpsimd
        def _(pool):
            with pool.Fori(0, B // 2) as i:
                for g in range(STEPS):
                    if g in mine:
                        continue
                    half, jt = g // T % 2, g % T
                    pool.wait_ge(exp_done, STEPS * i + g + 1 + ZB)
                    nc.gpsimd.tensor_tensor(w[:, g % PB, :], w[:, g % PB, :], keep["mask_t"][:, jt, half * HALF:(half + 1) * HALF],
                                            ALU.mult).then_inc(masked_pool, 1)

        @block.tensor
        def _(pe):
            pe.sem_inc(weighed, PB)
            with pe.Fori(0, B // 2) as i:
                for g in range(STEPS):
                    k, half, jt = g // (2 * T), g // T % 2, g % T
                    if g % (2 * T) == 0:
                        pe.wait_ge(h_loaded[k], 16 * (i + 1))
                    if jt == 0:
                        pe.wait_ge(drained, 4 * i + g // T + 1)
                    if g in mine:
                        pe.wait_ge(masked_dve, len(mine) * i + mine.index(g) + 1)
                    else:
                        pe.wait_ge(masked_pool, (STEPS - len(mine)) * i + g - sum(m < g for m in mine) + 1)
                    for it in range(IT):
                        mm = nc.tensor.matmul(tile(half, it), w[:, g % PB, it * P:(it + 1) * P], h[:, k, jt, :],
                                              start=(jt == 0 and it % 3 == 0), stop=(jt == T - 1), skip_group_check=True)
                    mm.then_inc(weighed, 1)


def nodes1(nc, io, keep):
    with ExitStack() as stack:
        s = Scope(nc, stack, "p1")
        x = s.sb("x", [P, T, F])
        hn = s.sb("hn", [P, T, F])
        hT = s.sb("hT", [P, N])
        wqk = [s.sb("wq", [P, F]), s.sb("wk", [P, F])]
        wv = s.sb("wv", [P, F])
        hi = [s.sb("q_hi", [P, N], F16), s.sb("k_hi", [P, N], F16)]
        lo = [s.sb("q_lo", [P, N], F16), s.sb("k_lo", [P, N], F16)]
        v = s.sb("v", [P, 2, T, 2, HD + 1])
        st = s.sb("st", [P, T, 6])
        tmp = s.sb("tmp", [P, 4, T])
        rstd, shift, minus_half = s.sb("rstd", [P, T]), s.sb("shift", [P, T]), s.sb("minus_half", [P, T])
        tp_ps = s.ps("tp_ps", [P, 2, BANK])
        qk_ps = s.ps("qk_ps", [P, 4, BANK])
        v_ps = s.ps("v_ps", [P, 2, BANK])
        weights_in, consts_ready, x_loaded = s.sem("weights_in"), s.sem("consts_ready"), s.sem("x_loaded")
        chain, rooted, normed, turned, hT_kept = s.sem("chain"), s.sem("rooted"), s.sem("normed"), s.sem("turned"), s.sem("hT_kept")
        qk_done, hi_done, lo_done, v_done, v_kept = (s.sem("qk_done"), s.sem("hi_done"), s.sem("lo_done"), s.sem("v_done"),
                                                     s.sem("v_kept"))
        stored = s.sem("stored")
        block = s.block()
        CHAIN = NORM_STEPS + 1
        QK = 2 * CH

        @block.sync
        def _(sp):
            for buf, m in ((wqk[0], "L1_gnn_W_q"), (wqk[1], "L1_gnn_W_k"), (wv, "L1_gnn_W_v")):
                sp.dma_start(buf[:], io[m][:]).then_inc(weights_in, 16)
            with sp.Fori(0, B) as b:
                sp.wait_ge(normed, b)
                sp.dma_start(flat(x[:]), node_tiles(io["x1"], b)).then_inc(x_loaded, 16)

        @block.gpsimd
        def _(pool):
            nc.gpsimd.memset(minus_half[:], -0.5).then_inc(consts_ready, 1)
            nc.gpsimd.memset(v[:], 1.0).then_inc(consts_ready, 1)
            pool.wait_ge(consts_ready, 2)
            with pool.Fori(0, B) as b:
                norm_root(nc, pool, tmp, minus_half[:], rstd[:], chain, b * CHAIN + NORM_STEPS, rooted)
                pool.wait_ge(lo_done, QK * (b + 1))
                pool.wait_ge(hi_done, QK * (b + 1))
                for part, names in ((hi, ("q_hi", "k_hi")), (lo, ("q_lo", "k_lo"))):
                    for buf, m in zip(part, names):
                        pool.dma_start(io[m][bass.ds(b, 1)].rearrange("one p n -> p (one n)"), buf[:]).then_inc(stored, 16)
                pool.wait_ge(v_kept, CH * (b + 1) + 2)
                pool.dma_start(io["v"][bass.ds(b, 1)].rearrange("one g p n -> p (one g) n"),
                               v[:].rearrange("p g t a d -> p g (t a d)")).then_inc(stored, 16)
            pool.wait_ge(stored, 16 * 5 * B)

        @block.vector
        def _(dve):
            dve.sem_inc(v_kept, 2)
            dve.wait_ge(consts_ready, 2)
            with dve.Fori(0, B) as b:
                dve.wait_ge(x_loaded, 16 * (b + 1))
                for t in range(T):
                    last = nc.vector.bn_stats(st[:, t, :], x[:, t, :])
                last.then_inc(chain, 1)
                dve.wait_ge(chain, b * CHAIN + 1)
                norm_stats(nc, dve, st, tmp, rstd[:], shift[:], chain, b * CHAIN + 1, rooted, b + 1)
                dve.wait_ge(stored, 80 * b)
                for q in range(CH):
                    for a in range(2):
                        c = 2 * q + a
                        dve.wait_ge(hi_done, QK * b + c + 1)
                        nc.vector.tensor_tensor(lo[a][:, q * BANK:(q + 1) * BANK], qk_ps[:, c % 4, :],
                                                hi[a][:, q * BANK:(q + 1) * BANK], ALU.subtract).then_inc(lo_done, 1)
                    dve.wait_ge(v_done, CH * b + q + 1)
                    for g in range(2):
                        ins = nc.vector.tensor_copy(v[:, g, 4 * q:4 * q + 4, :, 0:HD],
                                                    v_ps[:, q % 2, :].rearrange("p (t g a d) -> p g t a d", g=2, a=2, d=HD)[:, g])
                    ins.then_inc(v_kept, 1)

        @block.scalar
        def _(act):
            act.sem_inc(hT_kept, 2)
            with act.Fori(0, B) as b:
                act.wait_ge(chain, (b + 1) * CHAIN)
                act.wait_ge(turned, CH * b)
                for t in range(T):
                    last = nc.scalar.activation(hn[:, t, :], x[:, t, :], ACT.Relu, bias=shift[:, t:t + 1], scale=rstd[:, t:t + 1])
                last.then_inc(normed, 1)
                act.wait_ge(stored, 80 * b)
                for q in range(CH):
                    act.wait_ge(turned, CH * b + q + 1)
                    nc.scalar.copy(hT[:, q * BANK:(q + 1) * BANK], tp_ps[:, q % 2, :]).then_inc(hT_kept, 1)
                    for a in range(2):
                        c = 2 * q + a
                        act.wait_ge(qk_done, QK * b + c + 1)
                        nc.scalar.copy(hi[a][:, q * BANK:(q + 1) * BANK], qk_ps[:, c % 4, :]).then_inc(hi_done, 1)

        @block.tensor
        def _(pe):
            pe.wait_ge(weights_in, 16 * 3)
            with pe.Fori(0, B) as b:
                pe.wait_ge(normed, b + 1)
                for q in range(CH):
                    pe.wait_ge(hT_kept, CH * b + q + 1)
                    for t in range(4 * q, 4 * q + 4):
                        mm = nc.tensor.transpose(tp_ps[:, q % 2, (t % 4) * P:(t % 4 + 1) * P], hn[:, t, :], keep["ident"][:])
                    mm.then_inc(turned, 1)
                    pe.wait_ge(hT_kept, CH * b + q + 3)
                    for a in range(2):
                        c = 2 * q + a
                        if c < 4:
                            pe.wait_ge(lo_done, QK * b)
                        else:
                            pe.wait_ge(lo_done, QK * b + c - 3)
                        nc.tensor.matmul(qk_ps[:, c % 4, :], wqk[a][:], hT[:, q * BANK:(q + 1) * BANK], start=True,
                                         stop=True).then_inc(qk_done, 1)
                    pe.wait_ge(v_kept, CH * b + q + 1)
                    for t in range(4 * q, 4 * q + 4):
                        mm = nc.tensor.matmul(v_ps[:, q % 2, (t % 4) * P:(t % 4 + 1) * P], hT[:, t * P:(t + 1) * P], wv[:],
                                              start=True, stop=True)
                    mm.then_inc(v_done, 1)


def head_attention(nc, io, keep):
    SCALE = float(HD) ** -0.5
    K = 3 * HD
    STEPS = CH * T
    BODY = 2 * STEPS
    UNITS = 2 * T * CH
    FIRST, LAST = 4, 58
    PB, LAG = 4, 3
    done_by = [0] * (STEPS + 1)
    for g in range(STEPS):
        done_by[g + 1] = min(UNITS, max(0, (g + 1 - FIRST) * UNITS // (LAST - FIRST)))
    mine = [g for g in range(BODY) if not FIRST <= g % STEPS < LAST or g % 5 in (1, 3)]
    with ExitStack() as stack:
        s = Scope(nc, stack, "a1")
        mbias = s.sb("mbias", [P, T, N], BF16)
        qs = [[s.sb(f"qs{u}{a}", [K + 1, N], F16) for a in range(2)] for u in range(2)]
        ks = [[s.sb(f"ks{u}{a}", [K + 1, N], F16) for a in range(2)] for u in range(2)]
        v = [s.sb(f"v{u}", [P, T, 2, HD + 1]) for u in range(2)]
        w = s.sb("w", [P, PB, 2, BANK])
        mx = s.sb("mx", [P, 2 * T, CH])
        mrow = s.sb("mrow", [P, 2 * T])
        mshift = s.sb("mshift", [2 * T, P], F16)
        oe = s.sb("oe", [2 * (HD * 2), 2, BANK])
        sc_ps = s.ps("sc_ps", [P, 2, 2, BANK])
        mx_ps = s.ps("mx_ps", [P, 2, BANK])
        o_ps = s.ps("o_ps", [P, 2, BANK])
        mbias_loaded, units_ready = s.sem("mbias_loaded"), s.sem("units_ready")
        qk_loaded, v_loaded = [s.sem(f"qk_loaded{u}") for u in range(2)], [s.sem(f"v_loaded{u}") for u in range(2)]
        scored, exp_done, masked_pool, masked_dve, weighed = (s.sem("scored"), s.sem("exp_done"), s.sem("masked_pool"),
                                                              s.sem("masked_dve"), s.sem("weighed"))
        mx_scored, mx_taken, rows_done, rows_turned = s.sem("mx_scored"), s.sem("mx_taken"), s.sem("rows_done"), s.sem("rows_turned")
        shift_ready, shift_stored, shift_placed = s.sem("shift_ready"), s.sem("shift_stored"), s.sem("shift_placed")
        o_kept, o_stored = s.sem("o_kept"), [s.sem(f"o_stored{k}") for k in range(2)]
        block = s.block()

        def load(sp, b, u):
            for a in range(2):
                head = slice((2 * u + a) * HD, (2 * u + a + 1) * HD)
                for row, m in ((0, "k_hi"), (1, "k_lo"), (2, "k_hi")):
                    sp.dma_start(ks[u][a][row * HD:(row + 1) * HD, :],
                                 io[m][bass.ds(b, 1), head, :].rearrange("one p n -> p (one n)")).then_inc(qk_loaded[u], 16)
                for row, m in ((0, "q_hi"), (1, "q_hi"), (2, "q_lo")):
                    sp.dma_start(qs[u][a][row * HD:(row + 1) * HD, :],
                                 io[m][bass.ds(b, 1), head, :].rearrange("one p n -> p (one n)")).then_inc(qk_loaded[u], 16)

        def load_v(sp, b, u):
            sp.dma_start(v[u][:].rearrange("p t a d -> p (t a d)"),
                         io["v"][bass.ds(b, 1), u].rearrange("one p n -> p (one n)")).then_inc(v_loaded[u], 16)

        LOADS = 16 * 12

        def place_shift(sp, pair, u):
            sp.wait_ge(shift_ready, pair + 1)
            sp.dma_start(io["shifts"][:], mshift[:]).then_inc(shift_stored, 16)
            sp.wait_ge(shift_stored, 16 * (pair + 1))
            for a in range(2):
                sp.dma_start(qs[u][a][K:K + 1, :],
                             io["shifts"][a * T:(a + 1) * T, :].rearrange("(o t) p -> o (t p)", o=1)).then_inc(shift_placed, 16)

        @block.sync
        def _(sp):
            load(sp, 0, 0)
            load_v(sp, 0, 0)
            for t in range(T):
                sp.dma_start(mbias[:, t, :], io["mask_bias"][t * P:(t + 1) * P, :]).then_inc(mbias_loaded, 16)
            load(sp, 0, 1)
            load_v(sp, 0, 1)
            place_shift(sp, 0, 0)

            def store(b, c):
                sp.wait_ge(o_kept, 2 * CH * b + c + 1 + 2)
                u, rows = c // CH, slice(c % CH * BANK, (c % CH + 1) * BANK)
                for a in range(2):
                    head = 2 * u + a
                    sp.dma_start(io["heads_t"][bass.ds(b, 1), head * HD:(head + 1) * HD, rows].rearrange("one p n -> p (one n)"),
                                 oe[2 * HD * a:2 * HD * a + HD, c % 2, :]).then_inc(o_stored[c % 2], 16)
                    sp.dma_start(io["sums"][bass.ds(b, 1), head:head + 1, rows].rearrange("one p n -> p (one n)"),
                                 oe[2 * HD * a + HD:2 * HD * a + HD + 1, c % 2, :]).then_inc(o_stored[c % 2], 16)

            with sp.Fori(0, B) as b:
                following = (b + 1) % B
                for c in range(CH - 1):
                    store(b, c)
                place_shift(sp, 2 * b + 1, 1)
                sp.wait_ge(scored, BODY * b + STEPS)
                load(sp, following, 0)
                store(b, CH - 1)
                sp.wait_ge(weighed, BODY * b + STEPS + PB)
                load_v(sp, following, 0)
                for c in range(CH, 2 * CH - 1):
                    store(b, c)
                place_shift(sp, 2 * b + 2, 0)
                sp.wait_ge(scored, BODY * (b + 1))
                load(sp, following, 1)
                store(b, 2 * CH - 1)
                sp.wait_ge(weighed, BODY * (b + 1) + PB)
                load_v(sp, following, 1)
            for u in range(2):
                sp.wait_ge(qk_loaded[u], LOADS * (B + 1))
                sp.wait_ge(v_loaded[u], 16 * (B + 1))
                sp.wait_ge(o_stored[u], 64 * CH * B)
            sp.wait_ge(shift_placed, 32 * (2 * B + 1))

        @block.tensor
        def _(pe):
            def maxima(u, n0, n1, pair):
                for n in range(n0, n1):
                    a, t, c = n // (T * CH), n // CH % T, n % CH
                    if n == 0:
                        pe.wait_ge(shift_ready, pair)
                    pe.wait_ge(mx_taken, UNITS * pair + n + 1)
                    nc.tensor.matmul(mx_ps[:, n % 2, :], qs[u][a][0:K, t * P:(t + 1) * P], ks[u][a][0:K, c * BANK:(c + 1) * BANK],
                                     start=True, stop=True).then_inc(mx_scored, 1)

            def turn_maxima(pair):
                pe.wait_ge(rows_done, pair + 1)
                nc.tensor.transpose(mx_ps[0:2 * T, 0, 0:P], mrow[:], keep["ident"][:]).then_inc(rows_turned, 1)

            def weigh(g, i):
                u, c, jt = g // STEPS, g // T, g % T
                if jt == 0:
                    pe.wait_ge(o_kept, 2 * CH * i + c + 1)
                if g % STEPS == 0:
                    pe.wait_ge(v_loaded[u], 16 * (i + 1))
                if g in mine:
                    pe.wait_ge(masked_dve, len(mine) * i + mine.index(g) + 1)
                else:
                    pe.wait_ge(masked_pool, (BODY - len(mine)) * i + g - sum(m < g for m in mine) + 1)
                for a in range(2):
                    mm = nc.tensor.matmul(o_ps[2 * HD * a:2 * HD * a + HD + 1, c % 2, :], v[u][:, jt, a, :], w[:, g % PB, a, :],
                                          start=(jt == 0), stop=(jt == T - 1))
                mm.then_inc(weighed, 1)

            pe.sem_inc(weighed, PB)
            pe.wait_ge(qk_loaded[0], LOADS)
            maxima(0, 0, UNITS, 0)
            turn_maxima(0)
            pe.wait_ge(units_ready, 4)
            with pe.Fori(0, B) as i:
                for g in range(BODY):
                    u, r = g // STEPS, g % STEPS
                    c, jt = r // T, r % T
                    if r == 0:
                        pe.wait_ge(shift_placed, 32 * (2 * i + u + 1))
                    pe.wait_ge(exp_done, BODY * i + g + 1)
                    for a in range(2):
                        mm = nc.tensor.matmul(sc_ps[:, g % 2, a, :], ks[u][a][:, jt * P:(jt + 1) * P],
                                              qs[u][a][:, c * BANK:(c + 1) * BANK], start=True, stop=True)
                    mm.then_inc(scored, 1)
                    if r == FIRST:
                        pe.wait_ge(qk_loaded[1 - u], LOADS * (i + 1 + u))
                    maxima(1 - u, done_by[r], done_by[r + 1], 2 * i + u + 1)
                    if r == LAST:
                        turn_maxima(2 * i + u + 1)
                    if g >= LAG:
                        weigh(g - LAG, i)
                for g in range(BODY - LAG, BODY):
                    weigh(g, i)

        @block.vector
        def _(dve):
            def take(n0, n1, pair):
                for n in range(n0, n1):
                    t, c = n // CH % T, n % CH
                    due = UNITS * pair + n + 1
                    if not isinstance(due, int):
                        dve.compute_val(due)
                    dve.wait_ge(mbias_loaded, 16 * T)
                    dve.wait_ge(mx_scored, due)
                    nc.vector.tensor_tensor_reduce(out=mx_ps[:, n % 2, :], in0=mx_ps[:, n % 2, :],
                                                   in1=mbias[:, t, c * BANK:(c + 1) * BANK], scale=1.0, scalar=-3.0e38,
                                                   op0=ALU.add, op1=ALU.max,
                                                   accum_out=mx[:, n // CH, c:c + 1]).then_inc(mx_taken, 1)

            def row_maxima(pair):
                dve.wait_ge(mx_taken, UNITS * (pair + 1) + 2)
                nc.vector.tensor_reduce(mrow[:], mx[:], AX.X, ALU.max).then_inc(rows_done, 1)

            def shifts(pair):
                dve.wait_ge(rows_turned, pair + 1)
                dve.wait_ge(shift_placed, 32 * pair)
                nc.vector.tensor_scalar(mshift[:], mx_ps[0:2 * T, 0, 0:P], -1.0 / SHIFT_UNIT, None, ALU.mult).then_inc(shift_ready, 1)

            def mask(g, i):
                if g in mine:
                    c, jt = g // T % CH, g % T
                    dve.wait_ge(exp_done, BODY * i + g + 1 + 2)
                    nc.vector.tensor_tensor(w[:, g % PB], w[:, g % PB],
                                            keep["mask_t"][:, jt, c * BANK:(c + 1) * BANK].unsqueeze(1).to_broadcast([P, 2, BANK]),
                                            ALU.mult).then_inc(masked_dve, 1)

            dve.sem_inc(mx_taken, 2)
            for u in range(2):
                for a in range(2):
                    nc.vector.memset(ks[u][a][K:K + 1, :], SHIFT_UNIT).then_inc(units_ready, 1)
            dve.wait_ge(mbias_loaded, 16 * T)
            take(0, UNITS, 0)
            row_maxima(0)
            shifts(0)
            with dve.Fori(0, B) as i:
                for g in range(BODY):
                    u, r = g // STEPS, g % STEPS
                    if g >= 1:
                        mask(g - 1, i)
                    take(done_by[r], done_by[r + 1], 2 * i + u + 1)
                    if r == LAST:
                        row_maxima(2 * i + u + 1)
                    if r == LAST + 1:
                        shifts(2 * i + u + 1)
                mask(BODY - 1, i)

        @block.scalar
        def _(act):
            def keep_rows(c, i):
                act.wait_ge(weighed, BODY * i + (c + 1) * T + PB)
                act.wait_ge(o_stored[c % 2], 64 * (CH * i + c // 2))
                for a in range(2):
                    rows = slice(2 * HD * a, 2 * HD * a + HD + 1)
                    ins = nc.scalar.copy(oe[rows, c % 2, :], o_ps[rows, c % 2, :])
                ins.then_inc(o_kept, 1)

            act.sem_inc(exp_done, 2)
            act.sem_inc(o_kept, 2)
            with act.Fori(0, B) as i:
                for g in range(BODY):
                    act.wait_ge(scored, BODY * i + g + 1)
                    act.wait_ge(weighed, BODY * i + g + 1)
                    nc.scalar.activation(w[:, g % PB], sc_ps[:, g % 2], ACT.Exp, scale=SCALE).then_inc(exp_done, 1)
                    if g >= T + LAG and (g - LAG) % T == 0:
                        keep_rows((g - LAG) // T - 1, i)
                keep_rows(2 * CH - 1, i)

        @block.gpsimd
        def _(pool):
            with pool.Fori(0, B) as i:
                for g in range(BODY):
                    if g in mine:
                        continue
                    c, jt = g // T % CH, g % T
                    pool.wait_ge(exp_done, BODY * i + g + 1 + 2)
                    nc.gpsimd.tensor_tensor(w[:, g % PB], w[:, g % PB],
                                            keep["mask_t"][:, jt, c * BANK:(c + 1) * BANK].unsqueeze(1).to_broadcast([P, 2, BANK]),
                                            ALU.mult).then_inc(masked_pool, 1)


def nodes2(nc, io, keep):
    with ExitStack() as stack:
        s = Scope(nc, stack, "p2")
        ot = s.sb("ot", [P, N])
        sums = s.sb("sums", [HEADS, N])
        rz = s.sb("rz", [HEADS, N])
        sel = s.sb("sel", [HEADS, HEADS, HD])
        x1 = s.sb("x1", [P, T, F])
        x1b = s.sb("x1b", [P, T, F])
        x2 = s.sb("x2", [P, T, F])
        hn = s.sb("hn", [P, T, F])
        hT = s.sb("hT", [P, N])
        g = s.sb("g", [P, T, 2, F], F16)
        own = s.sb("own", [P, T, F])
        wo = s.sb("wo", [P, F])
        wns = s.sb("wns", [P, 2 * F])
        bo, bs, bn = s.sb("bo", [P, F]), s.sb("bs", [P, F]), s.sb("bn", [P, F])
        bias = s.sb("bias", [P, T, F])
        st = s.sb("st", [P, T, 6])
        tmp = s.sb("tmp", [P, 4, T])
        rstd, shift, minus_half = s.sb("rstd", [P, T]), s.sb("shift", [P, T]), s.sb("minus_half", [P, T])
        rep_ps = s.ps("rep_ps", [P, 2, BANK])
        y_ps = s.ps("y_ps", [P, 2, BANK])
        tp_ps = s.ps("tp_ps", [P, 2, BANK])
        g_ps = s.ps("g_ps", [P, 2, 2, 2 * F])
        weights_in, consts_ready, sel_ready, bias_ready = (s.sem("weights_in"), s.sem("consts_ready"), s.sem("sel_ready"),
                                                           s.sem("bias_ready"))
        heads_loaded, x1_loaded = s.sem("heads_loaded"), s.sem("x1_loaded")
        rz_done, spread, divided, y_done, x1b_done, x2_done = (s.sem("rz_done"), s.sem("spread"), s.sem("divided"), s.sem("y_done"),
                                                               s.sem("x1b_done"), s.sem("x2_done"))
        chain, rooted, normed, turned, hT_kept = s.sem("chain"), s.sem("rooted"), s.sem("normed"), s.sem("turned"), s.sem("hT_kept")
        g_done, hi_done, lo_done, own_done = s.sem("g_done"), s.sem("hi_done"), s.sem("lo_done"), s.sem("own_done")
        x2_stored, g_stored, own_stored = s.sem("x2_stored"), s.sem("g_stored"), s.sem("own_stored")
        block = s.block()
        CHAIN = NORM_STEPS + 1
        PAIRS = T // 2

        @block.sync
        def _(sp):
            sp.dma_start(wo[:], io["L1_gnn_W_o"][:]).then_inc(weights_in, 16)
            sp.dma_start(wns[:, 0:F], io["L2_gnn_W_neigh"][:]).then_inc(weights_in, 16)
            sp.dma_start(wns[:, F:2 * F], io["L2_gnn_W_self"][:]).then_inc(weights_in, 16)
            for buf, m in ((bo, "L1_gnn_b_o"), (bs, "L2_gnn_b_self"), (bn, "L2_gnn_b_neigh")):
                sp.dma_start(buf[:], io[m][0:1, :].partition_broadcast(P)).then_inc(weights_in, 16)
            with sp.Fori(0, B) as b:
                sp.wait_ge(x1b_done, b)
                sp.dma_start(flat(x1[:]), node_tiles(io["x1"], b)).then_inc(x1_loaded, 16)
                sp.wait_ge(rz_done, b)
                sp.dma_start(sums[:], io["sums"][bass.ds(b, 1)].rearrange("one p n -> p (one n)")).then_inc(heads_loaded, 16)
                sp.wait_ge(y_done, CH * b)
                sp.dma_start(ot[:], io["heads_t"][bass.ds(b, 1)].rearrange("one p n -> p (one n)")).then_inc(heads_loaded, 16)

        @block.gpsimd
        def _(pool):
            nc.gpsimd.memset(minus_half[:], -0.5).then_inc(consts_ready, 1)
            nc.gpsimd.memset(sel[:], 1.0).then_inc(sel_ready, 1)
            pool.wait_ge(sel_ready, 1)
            nc.gpsimd.affine_select(out=sel[:], in_=sel[:], compare_op=ALU.is_equal, fill=0.0, base=0,
                                    pattern=[[-1, HEADS], [0, HD]], channel_multiplier=1).then_inc(consts_ready, 1)
            pool.wait_ge(weights_in, 16 * 6)
            pool.wait_ge(consts_ready, 2)

            def first(b):
                pool.wait_ge(x1_loaded, 16 * (b + 1))
                pool.wait_ge(x2_done, CH * b)
                nc.gpsimd.tensor_tensor(x1b[:], x1[:], bo[:].unsqueeze(1).to_broadcast([P, T, F]), ALU.add).then_inc(x1b_done, 1)

            def root_and_store(b):
                norm_root(nc, pool, tmp, minus_half[:], rstd[:], chain, b * CHAIN + NORM_STEPS, rooted)
                pool.dma_start(node_tiles(io["x2"], b), flat(x2[:])).then_inc(x2_stored, 16)

            def second(b):
                pool.wait_ge(lo_done, PAIRS * (b + 1))
                pool.wait_ge(hi_done, PAIRS * (b + 1))
                pool.dma_start(io["g"][bass.ds(b, 1)].rearrange("one p n -> p (one n)"),
                               g[:].rearrange("p t k f -> p (t k f)")).then_inc(g_stored, 16)
                pool.wait_ge(own_done, PAIRS * (b + 1))
                pool.dma_start(io["own"][bass.ds(b, 1)].rearrange("one p n -> p (one n)"),
                               own[:].rearrange("p t f -> p (t f)")).then_inc(own_stored, 16)

            first(0)
            root_and_store(0)
            with pool.Fori(0, B - 1) as b:
                first(b + 1)
                second(b)
                root_and_store(b + 1)
            second(B - 1)
            pool.wait_ge(x2_stored, 16 * B)
            pool.wait_ge(g_stored, 16 * B)
            pool.wait_ge(own_stored, 16 * B)

        @block.vector
        def _(dve):
            def divide(b):
                dve.wait_ge(heads_loaded, 32 * (b + 1))
                dve.wait_ge(spread, CH * b)
                nc.vector.reciprocal(rz[:], sums[:]).then_inc(rz_done, 1)
                for q in range(CH):
                    dve.wait_ge(spread, CH * b + q + 1)
                    nc.vector.tensor_tensor(ot[:, q * BANK:(q + 1) * BANK], ot[:, q * BANK:(q + 1) * BANK], rep_ps[:, q % 2, :],
                                            ALU.mult).then_inc(divided, 1)

            def first(b):
                dve.wait_ge(x1b_done, b + 1)
                dve.wait_ge(x2_stored, 16 * b)
                dve.wait_ge(normed, b)
                for q in range(CH):
                    dve.wait_ge(y_done, CH * b + q + 1)
                    nc.vector.tensor_tensor(x2[:, 4 * q:4 * q + 4, :], y_ps[:, q % 2, :].rearrange("p (t f) -> p t f", f=F),
                                            x1b[:, 4 * q:4 * q + 4, :], ALU.add).then_inc(x2_done, 1)
                dve.wait_ge(x2_done, CH * (b + 1))
                for t in range(T):
                    last = nc.vector.bn_stats(st[:, t, :], x2[:, t, :])
                last.then_inc(chain, 1)
                dve.wait_ge(chain, b * CHAIN + 1)
                norm_stats(nc, dve, st, tmp, rstd[:], shift[:], chain, b * CHAIN + 1, rooted, b + 1)

            def second(b):
                dve.wait_ge(g_stored, 16 * b)
                dve.wait_ge(own_stored, 16 * b)
                for q in range(PAIRS):
                    tiles = slice(2 * q, 2 * q + 2)
                    dve.wait_ge(hi_done, PAIRS * b + q + 1)
                    nc.vector.tensor_tensor(g[:, tiles, 1, :], g_ps[:, q % 2, :, 0:F], g[:, tiles, 0, :], ALU.subtract).then_inc(lo_done, 1)
                    nc.vector.tensor_tensor(own[:, tiles, :], g_ps[:, q % 2, :, F:2 * F], bias[:, tiles, :], ALU.add).then_inc(own_done, 1)

            dve.sem_inc(divided, 2)
            dve.wait_ge(weights_in, 16 * 6)
            for t in range(T):
                last = nc.vector.scalar_tensor_tensor(out=bias[:, t, :], in0=bn[:], scalar=keep["has_deg"][:, t:t + 1], in1=bs[:],
                                                      op0=ALU.mult, op1=ALU.add)
            last.then_inc(bias_ready, 1)
            dve.wait_ge(bias_ready, 1)
            divide(0)
            first(0)
            with dve.Fori(0, B - 1) as b:
                divide(b + 1)
                second(b)
                first(b + 1)
            second(B - 1)

        @block.scalar
        def _(act):
            def first(b):
                act.wait_ge(chain, (b + 1) * CHAIN)
                act.wait_ge(turned, CH * b)
                for t in range(T):
                    last = nc.scalar.activation(hn[:, t, :], x2[:, t, :], ACT.Relu, bias=shift[:, t:t + 1], scale=rstd[:, t:t + 1])
                last.then_inc(normed, 1)

            def second(b):
                act.wait_ge(g_stored, 16 * b)
                for q in range(CH):
                    act.wait_ge(turned, CH * b + q + 1)
                    nc.scalar.copy(hT[:, q * BANK:(q + 1) * BANK], tp_ps[:, q % 2, :]).then_inc(hT_kept, 1)
                    for r in (2 * q, 2 * q + 1):
                        act.wait_ge(g_done, PAIRS * b + r + 1)
                        nc.scalar.copy(g[:, 2 * r:2 * r + 2, 0, :], g_ps[:, r % 2, :, 0:F]).then_inc(hi_done, 1)

            act.sem_inc(hT_kept, 2)
            first(0)
            with act.Fori(0, B - 1) as b:
                second(b)
                first(b + 1)
            second(B - 1)

        @block.tensor
        def _(pe):
            def divide(b):
                pe.wait_ge(rz_done, b + 1)
                for q in range(CH):
                    pe.wait_ge(divided, CH * b + q + 1)
                    nc.tensor.matmul(rep_ps[:, q % 2, :], sel[:].rearrange("k h d -> k (h d)"), rz[:, q * BANK:(q + 1) * BANK],
                                     start=True, stop=True).then_inc(spread, 1)

            def first(b):
                for q in range(CH):
                    pe.wait_ge(divided, CH * b + q + 3)
                    pe.wait_ge(x2_done, CH * b + max(q - 1, 0))
                    for t in range(4 * q, 4 * q + 4):
                        mm = nc.tensor.matmul(y_ps[:, q % 2, (t % 4) * P:(t % 4 + 1) * P], ot[:, t * P:(t + 1) * P], wo[:],
                                              start=True, stop=True)
                    mm.then_inc(y_done, 1)

            def second(b):
                pe.wait_ge(normed, b + 1)
                for q in range(CH):
                    pe.wait_ge(hT_kept, CH * b + q + 1)
                    for t in range(4 * q, 4 * q + 4):
                        mm = nc.tensor.transpose(tp_ps[:, q % 2, (t % 4) * P:(t % 4 + 1) * P], hn[:, t, :], keep["ident"][:])
                    mm.then_inc(turned, 1)
                    pe.wait_ge(hT_kept, CH * b + q + 3)
                    for r in (2 * q, 2 * q + 1):
                        pe.wait_ge(own_done, PAIRS * b + max(r - 1, 0))
                        for t in (2 * r, 2 * r + 1):
                            mm = nc.tensor.matmul(g_ps[:, r % 2, t % 2, :], hT[:, t * P:(t + 1) * P], wns[:], start=True, stop=True)
                        mm.then_inc(g_done, 1)

            pe.wait_ge(weights_in, 16 * 6)
            pe.wait_ge(consts_ready, 2)
            divide(0)
            first(0)
            with pe.Fori(0, B - 1) as b:
                divide(b + 1)
                second(b)
                first(b + 1)
            second(B - 1)


def neighbours(nc, io, keep):
    SLOTS = 4
    with ExitStack() as stack:
        s = Scope(nc, stack, "p3")
        g = s.sb("g", [P, 2, T, 2 * F], F16)
        own = s.sb("own", [P, 2, T, F])
        x2 = s.sb("x2", [P, 2, T, F])
        part = s.sb("part", [P, T, F])
        x3 = s.sb("x3", [P, T, F])
        hn = s.sb("hn", [P, T, F])
        hT = s.sb("hT", [P, N])
        h = s.sb("h", [P, T, F + 1])
        w = s.sb("w", [P, F + 2])
        w_rows = s.sb("w_rows", [P, F])
        a_cols = s.sb("a_cols", [P, 2])
        st = s.sb("st", [P, T, 6])
        tmp = s.sb("tmp", [P, 4, T])
        rstd, shift, minus_half = s.sb("rstd", [P, T]), s.sb("shift", [P, T]), s.sb("minus_half", [P, T])
        dots = s.sb("dots", [P, T, 2])
        sum_ps = s.ps("sum_ps", [P, SLOTS, BANK])
        tp_ps = s.ps("tp_ps", [P, 2, BANK])
        h_ps = s.ps("h_ps", [P, 2, BANK])
        THREES = [range(t, min(t + 3, T)) for t in range(0, T, 3)]
        TH = len(THREES)
        weights_in, consts_ready, wa_done, w_ready = s.sem("weights_in"), s.sem("consts_ready"), s.sem("wa_done"), s.sem("w_ready")
        g_loaded, own_loaded, x2_loaded = s.sem("g_loaded"), s.sem("own_loaded"), s.sem("x2_loaded")
        summed, part_done, used, x3_done, x3_stored = (s.sem("summed"), s.sem("part_done"), s.sem("used"), s.sem("x3_done"),
                                                       s.sem("x3_stored"))
        chain, rooted, normed, turned, hT_kept = s.sem("chain"), s.sem("rooted"), s.sem("normed"), s.sem("turned"), s.sem("hT_kept")
        h_done, h_kept, dots_kept, h_stored = s.sem("h_done"), s.sem("h_kept"), s.sem("dots_kept"), s.sem("h_stored")
        block = s.block()
        CHAIN = NORM_STEPS + 1

        def of(buf, b):
            return buf[:, bass.ds(b % 2, 1)]

        @block.sync
        def _(sp):
            sp.dma_start(w[:, 0:F], io["L3_gnn_W_t"][:]).then_inc(weights_in, 16)
            sp.dma_start(w_rows[:], io["L3_gnn_W"][:]).then_inc(weights_in, 16)
            sp.dma_start(a_cols[:], io["L3_gnn_a"][:]).then_inc(weights_in, 16)

            def load(b):
                sp.dma_start(of(g, b).rearrange("p one t f -> p (one t f)"),
                             io["g"][bass.ds(b, 1)].rearrange("one p n -> p (one n)")).then_inc(g_loaded, 16)
                sp.dma_start(of(own, b).rearrange("p one t f -> p (one t f)"),
                             io["own"][bass.ds(b, 1)].rearrange("one p n -> p (one n)")).then_inc(own_loaded, 16)
                sp.dma_start(of(x2, b).rearrange("p one t f -> p (one t f)"), node_tiles(io["x2"], b)).then_inc(x2_loaded, 16)

            def loaded(b):
                for sem in (g_loaded, own_loaded, x2_loaded):
                    sp.wait_ge(sem, 16 * (b + 1))

            load(0)
            loaded(0)
            load(1)
            with sp.Fori(0, B - 2) as b:
                loaded(b + 1)
                sp.wait_ge(summed, T * (b + 1))
                sp.wait_ge(x3_done, b + 1)
                load(b + 2)

        @block.gpsimd
        def _(pool):
            nc.gpsimd.memset(minus_half[:], -0.5).then_inc(consts_ready, 1)
            nc.gpsimd.memset(h[:, :, F:F + 1], 1.0).then_inc(consts_ready, 1)
            pool.wait_ge(consts_ready, 2)
            with pool.Fori(0, B) as b:
                norm_root(nc, pool, tmp, minus_half[:], rstd[:], chain, b * CHAIN + NORM_STEPS, rooted)
                pool.dma_start(node_tiles(io["x3"], b), flat(x3[:])).then_inc(x3_stored, 16)
                pool.wait_ge(h_kept, TH * (b + 1))
                pool.dma_start(io["h_nodes"][bass.ds(b, 1)].rearrange("one p t f -> p (one t) f"), h[:]).then_inc(h_stored, 16)
            pool.wait_ge(x3_stored, 16 * B)
            pool.wait_ge(h_stored, 16 * B)

        @block.vector
        def _(dve):
            def first(b):
                dve.wait_ge(own_loaded, 16 * (b + 1))
                for t in range(T):
                    dve.wait_ge(summed, T * b + t + 1)
                    nc.vector.scalar_tensor_tensor(out=part[:, t, :], in0=sum_ps[:, t % SLOTS, 0:F], scalar=keep["rdeg"][:, t:t + 1],
                                                   in1=of(own, b)[:, 0, t, :], op0=ALU.mult, op1=ALU.add).then_inc(part_done, 1)
                    dve.wait_ge(part_done, T * b + t + 1)
                    nc.vector.scalar_tensor_tensor(out=part[:, t, :], in0=sum_ps[:, t % SLOTS, F:2 * F], scalar=keep["rdeg"][:, t:t + 1],
                                                   in1=part[:, t, :], op0=ALU.mult, op1=ALU.add).then_inc(used, 1)
                dve.wait_ge(used, T * (b + 1) + SLOTS)
                dve.wait_ge(x2_loaded, 16 * (b + 1))
                dve.wait_ge(x3_stored, 16 * b)
                dve.wait_ge(normed, b)
                nc.vector.scalar_tensor_tensor(out=x3[:], in0=part[:], scalar=0.0, in1=of(x2, b)[:, 0], op0=ALU.max,
                                               op1=ALU.add).then_inc(x3_done, 1)

            def stats(b):
                dve.wait_ge(x3_done, b + 1)
                for t in range(T):
                    last = nc.vector.bn_stats(st[:, t, :], x3[:, t, :])
                last.then_inc(chain, 1)
                dve.wait_ge(chain, b * CHAIN + 1)
                norm_stats(nc, dve, st, tmp, rstd[:], shift[:], chain, b * CHAIN + 1, rooted, b + 1)

            def scores(b):
                for n, tiles in enumerate(THREES):
                    dve.wait_ge(h_kept, TH * b + n + 1)
                    m = len(tiles)
                    nc.vector.tensor_copy(dots[:, tiles[0]:tiles[0] + m, :],
                                          h_ps[:, n % 2, 0:m * (F + 2)].rearrange("p (t f) -> p t f", f=F + 2)[:, :, F:F + 2]).then_inc(dots_kept, 1)
                dve.wait_ge(dots_kept, TH * (b + 1))
                for k, m in enumerate(("s1", "s2")):
                    nc.vector.tensor_copy(keep[m][:, bass.ds(b, 1), :], dots[:, :, k:k + 1].rearrange("p t one -> p one t"))

            dve.sem_inc(used, SLOTS)
            dve.wait_ge(wa_done, 1)
            nc.vector.tensor_copy(w[:, F:F + 2], h_ps[:, 0, 0:2]).then_inc(w_ready, 1)
            first(0)
            with dve.Fori(0, B - 1) as b:
                stats(b)
                first(b + 1)
                scores(b)
            stats(B - 1)
            scores(B - 1)

        @block.scalar
        def _(act):
            act.sem_inc(hT_kept, 2)
            with act.Fori(0, B) as b:
                act.wait_ge(chain, (b + 1) * CHAIN)
                act.wait_ge(turned, CH * b)
                for t in range(T):
                    last = nc.scalar.activation(hn[:, t, :], x3[:, t, :], ACT.Relu, bias=shift[:, t:t + 1], scale=rstd[:, t:t + 1])
                last.then_inc(normed, 1)
                for q in range(CH):
                    act.wait_ge(turned, CH * b + q + 1)
                    nc.scalar.copy(hT[:, q * BANK:(q + 1) * BANK], tp_ps[:, q % 2, :]).then_inc(hT_kept, 1)
                act.wait_ge(h_stored, 16 * b)
                act.wait_ge(consts_ready, 2)
                for n, tiles in enumerate(THREES):
                    act.wait_ge(h_done, TH * b + n + 1)
                    m = len(tiles)
                    nc.scalar.copy(h[:, tiles[0]:tiles[0] + m, 0:F],
                                   h_ps[:, n % 2, 0:m * (F + 2)].rearrange("p (t f) -> p t f", f=F + 2)[:, :, 0:F]).then_inc(h_kept, 1)

        @block.tensor
        def _(pe):
            def first(b):
                pe.wait_ge(g_loaded, 16 * (b + 1))
                for it in range(T):
                    pe.wait_ge(used, T * b + it + 1)
                    for jt in range(T):
                        mm = nc.tensor.matmul(sum_ps[:, it % SLOTS, 0:2 * F], keep["mask_t"][:, jt, it * P:(it + 1) * P],
                                              of(g, b)[:, 0, jt, :], start=(jt == 0), stop=(jt == T - 1))
                    mm.then_inc(summed, 1)

            def second(b):
                pe.wait_ge(normed, b + 1)
                for q in range(CH):
                    pe.wait_ge(hT_kept, CH * b + q + 1)
                    for t in range(4 * q, 4 * q + 4):
                        mm = nc.tensor.transpose(tp_ps[:, q % 2, (t % 4) * P:(t % 4 + 1) * P], hn[:, t, :], keep["ident"][:])
                    mm.then_inc(turned, 1)
                pe.wait_ge(hT_kept, CH * (b + 1) + 2)
                for n, tiles in enumerate(THREES):
                    pe.wait_ge(h_kept, TH * b + max(n - 1, 0))
                    pe.wait_ge(dots_kept, TH * b + max(n - 1, 0))
                    for k, t in enumerate(tiles):
                        mm = nc.tensor.matmul(h_ps[:, n % 2, k * (F + 2):(k + 1) * (F + 2)], hT[:, t * P:(t + 1) * P], w[:],
                                              start=True, stop=True)
                    mm.then_inc(h_done, 1)

            pe.wait_ge(weights_in, 16 * 3)
            nc.tensor.matmul(h_ps[:, 0, 0:2], w_rows[:], a_cols[:], start=True, stop=True).then_inc(wa_done, 1)
            first(0)
            pe.wait_ge(w_ready, 1)
            with pe.Fori(0, B - 1) as b:
                first(b + 1)
                second(b)
            second(B - 1)


_SHAPES = {"h_nodes": ((B, P, T, F + 1), F32), "mask_bias": ((N, N), BF16), "u_rows": ((B, N), F32), "v_rows": ((B, N), F32),
           "x1": ((B, N, F), F32),
           "q_hi": ((B, P, N), F16), "q_lo": ((B, P, N), F16), "k_hi": ((B, P, N), F16), "k_lo": ((B, P, N), F16),
           "v": ((B, 2, P, T * 2 * (HD + 1)), F32), "x2": ((B, N, F), F32), "x3": ((B, N, F), F32), "g": ((B, P, T * 2 * F), F16), "own": ((B, P, T * F), F32),
           "shifts": ((2 * T, P), F16), "heads_t": ((B, P, N), F32), "sums": ((B, HEADS, N), F32)}
PHASES = [
    masks_and_nodes0,
    lambda nc, io, keep: row_shifts(nc, io, keep, "l0", True),
    lambda nc, io, keep: gat_attention(nc, io, keep, "g0", io["x"], io["x1"], True),
    nodes1,
    head_attention,
    nodes2,
    neighbours,
    lambda nc, io, keep: row_shifts(nc, io, keep, "l3", False),
    lambda nc, io, keep: gat_attention(nc, io, keep, "g3", io["x3"], io["out"], False),
]

CLEAR_BEFORE = (5,)


def build(nc, io, upto=99):
    for name, (shape, dtype) in _SHAPES.items():
        io[name] = nc.dram_tensor(name, shape, dtype, kind="Internal").ap()
    with ExitStack() as stack:
        s = Scope(nc, stack, "keep")
        keep = {"mask_t": s.sb("mask_t", [P, T, N], BF16), "ident": s.sb("ident", [P, P]),
                "ident16": s.sb("ident16", [P, P], BF16)}
        for name in ("s1", "s2", "u", "v", "s2_08", "s2_02"):
            keep[name] = s.sb(name, [P, B, T])
        keep["rdeg"], keep["has_deg"] = s.sb("rdeg", [P, T]), s.sb("has_deg", [P, T])
        Scope.used_sems.clear()
        for k, phase in enumerate(PHASES[:upto]):
            if k in CLEAR_BEFORE:
                clear_semaphores(nc)
            phase(nc, io, keep)


def kernel(**inputs):
    import numpy as _np
    import concourse.bacc as _bacc
    from concourse import mybir as _mybir
    from concourse.bass_utils import run_bass_kernel_spmd as _run

    laid = {name: _np.asarray(a) for name, a in inputs.items()}
    for name in ("L0_gnn_ln_gamma", "L0_gnn_ln_beta", "L1_gnn_b_o", "L2_gnn_b_self", "L2_gnn_b_neigh"):
        laid[name] = laid[name].reshape(1, F)
    for name in ("L0_gnn_node_weights", "L0_gnn_node_bias"):
        laid[name] = laid[name].reshape(P, T)
    laid["L0_gnn_a"] = laid["L0_gnn_a"].reshape(2, F)
    laid["L3_gnn_a"] = laid["L3_gnn_a"].reshape(2, F).T
    laid["L3_gnn_W_t"] = laid["L3_gnn_W"].T
    nc = _bacc.Bacc("TRN2", target_bir_lowering=False, num_devices=1)
    arrays, io = {}, {}
    for name, a in laid.items():
        arrays[f"in_{name}"] = a = _np.ascontiguousarray(a)
        io[name] = nc.dram_tensor(f"in_{name}", a.shape, _mybir.dt.from_np(a.dtype), kind="ExternalInput").ap()
    io["out"] = nc.dram_tensor("out_0", (B, N, F), F32, kind="ExternalOutput").ap()
    build(nc, io)
    r = _run(nc, [arrays], core_ids=[0])
    return r.results[0]["out_0"]
```

```python
from contextlib import ExitStack

import concourse.bass as bass
from concourse import mybir

ALU = mybir.AluOpType
ACT = mybir.ActivationFunctionType
AX = mybir.AxisListType
F32 = mybir.dt.float32
F16 = mybir.dt.float16
BF16 = mybir.dt.bfloat16
I32 = mybir.dt.int32

P = 128
B = 8
N = 2048
F = 128
T = N // P
HEADS = 4
HD = F // HEADS
BANK = 512
CH = N // BANK
LN_EPS = 1e-5
SLOPE = 0.2
LEVELS = 64
MASKED = 1.0e30
SHIFT_UNIT = 1024.0


class Scope:

    used_sems = []

    def __init__(self, nc, stack, name):
        self.nc, self.stack, self.name = nc, stack, name

    def sb(self, name, shape, dtype=F32):
        return self.stack.enter_context(self.nc.sbuf_tensor(f"{self.name}_{name}", shape, dtype))

    def ps(self, name, shape, dtype=F32):
        return self.stack.enter_context(self.nc.psum_tensor(f"{self.name}_{name}", shape, dtype))

    def sem(self, name):
        sem = self.nc.alloc_semaphore(name=f"{self.name}_{name}")
        self.used_sems.append(sem)
        return sem

    def block(self):
        return self.stack.enter_context(self.nc.Block())


def clear_semaphores(nc):
    nc.clear_and_free_semaphores(list(Scope.used_sems))
    Scope.used_sems.clear()
    nc.all_engine_barrier()


def node_tiles(dram, b):
    return dram[bass.ds(b, 1)].rearrange("one (p t) f -> p (one t f)", p=P)


def flat(buf):
    return buf.rearrange("p t f -> p (t f)")


def norm_stats(nc, dve, st, tmp, done, base):
    mean2, diff, ssq, var = (tmp[:, k, :] for k in range(4))
    nc.vector.tensor_tensor(mean2, st[:, :, 1], st[:, :, 4], ALU.add).then_inc(done, 1)
    nc.vector.tensor_tensor(diff, st[:, :, 1], st[:, :, 4], ALU.subtract).then_inc(done, 1)
    nc.vector.tensor_tensor(ssq, st[:, :, 2], st[:, :, 5], ALU.add).then_inc(done, 1)
    dve.wait_ge(done, base + 2)
    nc.vector.scalar_tensor_tensor(out=diff, in0=diff, scalar=0.25, in1=diff,
                                   op0=ALU.mult, op1=ALU.mult).then_inc(done, 1)
    dve.wait_ge(done, base + 3)
    nc.vector.tensor_scalar(ssq, ssq, 1.0 / F, LN_EPS, ALU.mult, ALU.add).then_inc(done, 1)
    dve.wait_ge(done, base + 5)
    nc.vector.tensor_tensor(var, ssq, diff, ALU.add).then_inc(done, 1)


def norm_shift(nc, dve, tmp, rstd, shift, done, rooted, roots):
    dve.wait_ge(rooted, roots)
    nc.vector.scalar_tensor_tensor(out=shift, in0=tmp[:, 0, :], scalar=-0.5, in1=rstd,
                                   op0=ALU.mult, op1=ALU.mult).then_inc(done, 1)


def norm_root(nc, pool, tmp, minus_half, rstd, done, value, rooted):
    pool.wait_ge(done, value)
    nc.gpsimd.tensor_tensor(rstd, tmp[:, 3, :], minus_half, ALU.pow).then_inc(rooted, 1)


NORM_STEPS = 7


def masks_and_nodes0(nc, io, keep):
    with ExitStack() as stack:
        s = Scope(nc, stack, "p0")
        adj_in = s.sb("adj_in", [P, 2, N], I32)
        m01 = s.sb("m01", [P, 2, N], BF16)
        mbias = s.sb("mbias", [P, 2, N], BF16)
        x = s.sb("x", [P, T, F])
        hn = s.sb("hn", [P, T, F])
        hT = s.sb("hT", [P, N])
        h0 = s.sb("h0", [P, T, F])
        h1 = s.sb("h1", [P, T, F])
        h = s.sb("h", [P, T, F + 1])
        w = s.sb("w", [P, F])
        gamma = s.sb("gamma", [P, F])
        beta = s.sb("beta", [P, F])
        a12 = s.sb("a12", [P, 2, F])
        nw = s.sb("nw", [P, T])
        nw1 = s.sb("nw1", [P, T])
        nb = s.sb("nb", [P, T])
        st_x, st_h = s.sb("st_x", [P, T, 6]), s.sb("st_h", [P, T, 6])
        tmp_x, tmp_h = s.sb("tmp_x", [P, 4, T]), s.sb("tmp_h", [P, 4, T])
        rstd_x, shift_x = s.sb("rstd_x", [P, T]), s.sb("shift_x", [P, T])
        rstd_h, shift_h = s.sb("rstd_h", [P, T]), s.sb("shift_h", [P, T])
        dots = s.sb("dots", [P, 2, T])
        products = s.sb("products", [P, T, F])
        minus_half = s.sb("minus_half", [P, T])
        mt_ps = s.ps("mt_ps", [P, 2, T, P], BF16)
        tp_ps = s.ps("tp_ps", [P, 2, BANK])
        pj_ps = s.ps("pj_ps", [P, 2, BANK])

        weights_in, ident_zero, ident_ready = s.sem("weights_in"), s.sem("ident_zero"), s.sem("ident_ready")
        adj_loaded, x_loaded = [s.sem(f"adj_loaded{k}") for k in range(2)], s.sem("x_loaded")
        m01_ready, mbias_ready = s.sem("m01_ready"), s.sem("mbias_ready")
        mbias_stored = [s.sem(f"mbias_stored{k}") for k in range(2)]
        mt_turned, mt_kept = s.sem("mt_turned"), s.sem("mt_kept")
        ones_ready, nw1_ready = s.sem("ones_ready"), s.sem("nw1_ready")
        chain_x, rooted_x, chain_h, rooted_h = s.sem("chain_x"), s.sem("rooted_x"), s.sem("chain_h"), s.sem("rooted_h")
        x_normed, x_scaled, h_turned, hT_kept = s.sem("x_normed"), s.sem("x_scaled"), s.sem("h_turned"), s.sem("hT_kept")
        projected, h0_kept, h0_normed = s.sem("projected"), s.sem("h0_kept"), s.sem("h0_normed")
        gamma_done, h_ready, dots_done, h_stored = s.sem("gamma_done"), s.sem("h_ready"), s.sem("dots_done"), s.sem("h_stored")
        scores_kept = s.sem("scores_kept")
        block = s.block()
        CHAIN = NORM_STEPS + 1

        @block.sync
        def _(sp):
            def load_x(b):
                sp.dma_start(flat(x[:]), node_tiles(io["x"], b)).then_inc(x_loaded, 16)

            def load_adj(b, k):
                rows = io["adj"].rearrange("(p t) j -> p t j", t=T)[:, bass.ds(2 * b + k, 1), :]
                sp.dma_start(adj_in[:, k, :], rows.rearrange("p one j -> p (one j)")).then_inc(adj_loaded[k], 16)

            def store_mbias(b):
                for k in range(2):
                    sp.wait_ge(mbias_ready, 2 * b + k + 1)
                    sp.dma_start(io["mask_bias"][bass.ds((2 * b + k) * P, P), :], mbias[:, k, :]).then_inc(mbias_stored[k], 16)

            def store_h(b):
                sp.wait_ge(h_ready, b + 1)
                sp.dma_start(io["h_nodes"][bass.ds(b, 1)].rearrange("one p t f -> p (one t f)"), flat(h[:])).then_inc(h_stored, 16)

            load_x(0)
            load_adj(0, 0)
            load_adj(0, 1)
            sp.dma_start(w[:], io["L0_gnn_W"][:]).then_inc(weights_in, 16)
            sp.dma_start(gamma[:], io["L0_gnn_ln_gamma"][0:1, :].partition_broadcast(P)).then_inc(weights_in, 16)
            sp.dma_start(beta[:], io["L0_gnn_ln_beta"][0:1, :].partition_broadcast(P)).then_inc(weights_in, 16)
            for k in range(2):
                sp.dma_start(a12[:, k, :], io["L0_gnn_a"][k:k + 1, :].partition_broadcast(P)).then_inc(weights_in, 16)
            sp.dma_start(nw[:], io["L0_gnn_node_weights"][:]).then_inc(weights_in, 16)
            sp.dma_start(nb[:], io["L0_gnn_node_bias"][:]).then_inc(weights_in, 16)

            def following(b):
                sp.wait_ge(x_normed, b + 1)
                load_x(b + 1)
                for k in range(2):
                    sp.wait_ge(m01_ready, 2 * b + k + 1)
                    load_adj(b + 1, k)
                store_mbias(b)

            following(0)
            with sp.Fori(0, B - 2) as j:
                following(j + 1)
                store_h(j)
            store_mbias(B - 1)
            store_h(B - 2)
            store_h(B - 1)
            for k in range(2):
                sp.wait_ge(mbias_stored[k], 16 * B)
            sp.wait_ge(h_stored, 16 * B)

        @block.gpsimd
        def _(pool):
            def root_x(b):
                norm_root(nc, pool, tmp_x, minus_half[:], rstd_x[:], chain_x, b * CHAIN + NORM_STEPS, rooted_x)

            def root_h(b):
                norm_root(nc, pool, tmp_h, minus_half[:], rstd_h[:], chain_h, b * CHAIN + NORM_STEPS, rooted_h)

            def affine(b):
                pool.wait_ge(h0_normed, b + 1)
                nc.gpsimd.tensor_tensor(h1[:], h1[:], gamma[:].unsqueeze(1).to_broadcast([P, T, F]), ALU.mult).then_inc(gamma_done, 1)
                pool.wait_ge(gamma_done, b + 1)
                pool.wait_ge(h_stored, 16 * b)
                pool.wait_ge(dots_done, 2 * b)
                nc.gpsimd.tensor_tensor(h[:, :, 0:F], h1[:], beta[:].unsqueeze(1).to_broadcast([P, T, F]),
                                        ALU.add).then_inc(h_ready, 1)

            nc.gpsimd.memset(minus_half[:], -0.5).then_inc(ident_zero, 1)
            nc.gpsimd.memset(keep["ident"][:], 0.0).then_inc(ident_zero, 1)
            nc.gpsimd.memset(keep["ident16"][:], 0.0).then_inc(ident_zero, 1)
            nc.gpsimd.memset(h[:, :, F:F + 1], 1.0).then_inc(ident_zero, 1)
            pool.wait_ge(ident_zero, 4)
            for m in (keep["ident"], keep["ident16"]):
                nc.gpsimd.affine_select(out=m[:], in_=m[:], compare_op=ALU.not_equal, fill=1.0, base=0,
                                        pattern=[[-1, P]], channel_multiplier=1).then_inc(ident_ready, 1)
            root_x(0)
            pool.wait_ge(weights_in, 16 * 7)
            root_x(1)
            root_h(0)
            affine(0)
            with pool.Fori(0, B - 2) as j:
                root_x(j + 2)
                root_h(j + 1)
                affine(j + 1)
            root_h(B - 1)
            affine(B - 1)

        @block.vector
        def _(dve):
            def masks(b):
                for k in range(2):
                    dve.wait_ge(adj_loaded[k], 16 * (b + 1))
                    dve.wait_ge(mt_turned, 2 * b + k + 1)
                    nc.vector.tensor_scalar(m01[:, k, :].rearrange("p (t q) -> p t q", q=P),
                                            adj_in[:, k, :].rearrange("p (q t) -> p t q", t=T), 0, None, ALU.is_gt).then_inc(m01_ready, 1)
                for k in range(2):
                    dve.wait_ge(m01_ready, 2 * b + k + 1)
                    dve.wait_ge(mbias_stored[k], 16 * b)
                    nc.vector.tensor_scalar(mbias[:, k, :], m01[:, k, :], MASKED, -MASKED,
                                            ALU.mult, ALU.add).then_inc(mbias_ready, 1)

            def stats_x(b):
                dve.wait_ge(x_loaded, 16 * (b + 1))
                for t in range(T):
                    last = nc.vector.bn_stats(st_x[:, t, :], x[:, t, :])
                last.then_inc(chain_x, 1)
                dve.wait_ge(chain_x, b * CHAIN + 1)
                norm_stats(nc, dve, st_x, tmp_x, chain_x, b * CHAIN + 1)

            def shift_of_x(b):
                norm_shift(nc, dve, tmp_x, rstd_x[:], shift_x[:], chain_x, rooted_x, b + 1)

            def scale_x(b):
                dve.wait_ge(x_normed, b + 1)
                for t in range(T):
                    last = nc.vector.tensor_scalar(hn[:, t, :], hn[:, t, :], nw1[:, t:t + 1], nb[:, t:t + 1], ALU.mult, ALU.add)
                last.then_inc(x_scaled, 1)

            def stats_h(b):
                dve.wait_ge(h0_kept, CH * (b + 1) + 2)
                for t in range(T):
                    last = nc.vector.bn_stats(st_h[:, t, :], h0[:, t, :])
                last.then_inc(chain_h, 1)
                dve.wait_ge(chain_h, b * CHAIN + 1)
                norm_stats(nc, dve, st_h, tmp_h, chain_h, b * CHAIN + 1)

            def norm_h(b):
                norm_shift(nc, dve, tmp_h, rstd_h[:], shift_h[:], chain_h, rooted_h, b + 1)
                dve.wait_ge(chain_h, (b + 1) * CHAIN)
                dve.wait_ge(h_ready, b)
                for t in range(T):
                    last = nc.vector.tensor_scalar(h1[:, t, :], h0[:, t, :], rstd_h[:, t:t + 1], shift_h[:, t:t + 1], ALU.mult, ALU.add)
                last.then_inc(h0_normed, 1)

            def scores(b):
                dve.wait_ge(h_ready, b + 1)
                dve.wait_ge(scores_kept, 2 * b)
                for k in range(2):
                    for t in range(T):
                        last = nc.vector.tensor_tensor_reduce(
                            out=products[:, t, :], in0=h[:, t, 0:F], in1=a12[:, k, :], scale=1.0, scalar=0.0,
                            op0=ALU.mult, op1=ALU.add, accum_out=dots[:, k, t:t + 1])
                    last.then_inc(dots_done, 1)
                    dve.wait_ge(dots_done, 2 * b + k + 1)
                nc.vector.tensor_copy(keep["s1"][:, bass.ds(b, 1), :], dots[:, 0:1, :]).then_inc(scores_kept, 1)
                nc.vector.tensor_copy(keep["s2"][:, bass.ds(b, 1), :], dots[:, 1:2, :]).then_inc(scores_kept, 1)

            stats_x(0)
            masks(0)
            shift_of_x(0)
            dve.wait_ge(weights_in, 16 * 7)
            nc.vector.tensor_scalar(nw1[:], nw[:], 1.0, None, ALU.add).then_inc(nw1_ready, 1)
            dve.wait_ge(nw1_ready, 1)
            scale_x(0)
            stats_x(1)
            masks(1)
            shift_of_x(1)
            stats_h(0)
            norm_h(0)
            scale_x(1)
            with dve.Fori(0, B - 2) as j:
                stats_x(j + 2)
                masks(j + 2)
                shift_of_x(j + 2)
                stats_h(j + 1)
                scores(j)
                norm_h(j + 1)
                scale_x(j + 2)
            stats_h(B - 1)
            scores(B - 2)
            norm_h(B - 1)
            scores(B - 1)

        @block.scalar
        def _(act):
            def keep_masks(b):
                for k in range(2):
                    act.wait_ge(mt_turned, 2 * b + k + 3)
                    nc.scalar.activation(keep["mask_t"][:, :, bass.ds((2 * b + k) * P, P)], mt_ps[:, k], ACT.Copy).then_inc(mt_kept, 1)

            def norm_x(b):
                act.wait_ge(chain_x, (b + 1) * CHAIN)
                act.wait_ge(h_turned, CH * b)
                for t in range(T):
                    last = nc.scalar.activation(hn[:, t, :], x[:, t, :], ACT.Relu, bias=shift_x[:, t:t + 1],
                                                scale=rstd_x[:, t:t + 1])
                last.then_inc(x_normed, 1)

            def keep_h0(b):
                act.wait_ge(h0_normed, b)
                for q in range(CH):
                    act.wait_ge(h_turned, CH * b + q + 1)
                    nc.scalar.copy(hT[:, q * BANK:(q + 1) * BANK], tp_ps[:, q % 2, :]).then_inc(hT_kept, 1)
                    act.wait_ge(projected, CH * b + q + 1)
                    nc.scalar.copy(h0[:, 4 * q:4 * q + 4, :],
                                   pj_ps[:, q % 2, :].rearrange("p (t f) -> p t f", f=F)).then_inc(h0_kept, 1)

            act.sem_inc(mt_kept, 2)
            act.sem_inc(hT_kept, 2)
            act.sem_inc(h0_kept, 2)
            norm_x(0)
            keep_masks(0)
            with act.Fori(0, B - 1) as j:
                keep_h0(j)
                norm_x(j + 1)
                keep_masks(j + 1)
            keep_h0(B - 1)

        @block.tensor
        def _(pe):
            def turn_masks(b):
                for k in range(2):
                    pe.wait_ge(m01_ready, 2 * b + k + 1)
                    pe.wait_ge(mt_kept, 2 * b + k + 1)
                    for t in range(T):
                        mm = nc.tensor.transpose(mt_ps[:, k, t, :], m01[:, k, t * P:(t + 1) * P], keep["ident16"][:])
                    mm.then_inc(mt_turned, 1)

            def project(b):
                pe.wait_ge(x_scaled, b + 1)
                for q in range(CH):
                    pe.wait_ge(hT_kept, CH * b + q + 1)
                    for t in range(4 * q, 4 * q + 4):
                        mm = nc.tensor.transpose(tp_ps[:, q % 2, (t % 4) * P:(t % 4 + 1) * P], hn[:, t, :], keep["ident"][:])
                    mm.then_inc(h_turned, 1)
                    pe.wait_ge(hT_kept, CH * b + q + 3)
                    pe.wait_ge(h0_kept, CH * b + q + 1)
                    for t in range(4 * q, 4 * q + 4):
                        mm = nc.tensor.matmul(pj_ps[:, q % 2, (t % 4) * P:(t % 4 + 1) * P], hT[:, t * P:(t + 1) * P],
                                              w[:], start=True, stop=True)
                    mm.then_inc(projected, 1)

            pe.sem_inc(mt_turned, 2)
            pe.wait_ge(ident_ready, 2)
            pe.wait_ge(weights_in, 16 * 7)
            turn_masks(0)
            with pe.Fori(0, B - 1) as j:
                project(j)
                turn_masks(j + 1)
            project(B - 1)

def row_shifts(nc, io, keep, name, first):
    with ExitStack() as stack:
        s = Scope(nc, stack, name)
        ext = s.sb("ext", [P, 2 * B])
        ext_col = s.sb("ext_col", [2 * B, 1])
        ext_diag = s.sb("ext_diag", [2 * B, 2 * B])
        ones = s.sb("ones", [2 * B, P])
        ext_all = s.sb("ext_all", [P, 2 * B])
        step = s.sb("step", [P, B])
        lev_i = s.sb("lev_i", [P, LEVELS], I32)
        lev = s.sb("lev", [P, LEVELS])
        rank = s.sb("rank", [P, B, LEVELS], BF16)
        tau = s.sb("tau", [P, B, LEVELS])
        above = s.sb("above", [P, T, B * LEVELS], BF16)
        hit = s.sb("hit", [P, 2, B * LEVELS], BF16)
        top = s.sb("top", [P, B, T])
        lk = s.sb("lk", [P, B, T])
        deg = s.sb("deg", [P, T])
        rows = s.sb("rows", [P, 2, P])
        ext_ps = s.ps("ext_ps", [2 * B, P])
        all_ps = s.ps("all_ps", [P, 2 * B])
        cnt_ps = s.ps("cnt_ps", [P, 4, BANK])
        rows_ps = s.ps("rows_ps", [P, 2, P])
        levels_in, step_done = s.sem("levels_in"), s.sem("step_done")
        ext_done, ext_turned, diag_done, spread = s.sem("ext_done"), s.sem("ext_turned"), s.sem("diag_done"), s.sem("spread")
        above_done, counted, hit_done, top_done = s.sem("above_done"), s.sem("counted"), s.sem("hit_done"), s.sem("top_done")
        shifts_done, rows_turned, rows_kept, rows_stored = (s.sem("shifts_done"), s.sem("rows_turned"), s.sem("rows_kept"),
                                                            s.sem("rows_stored"))
        block = s.block()
        s1, s2 = keep["s1"], keep["s2"]

        @block.gpsimd
        def _(pool):
            nc.gpsimd.memset(ones[:], 1.0).then_inc(levels_in, 1)
            nc.gpsimd.iota(lev_i[:], pattern=[[1, LEVELS]], base=0, channel_multiplier=0).then_inc(levels_in, 1)

        @block.vector
        def _(dve):
            nc.vector.tensor_reduce(ext[:, 0:B], s2[:], AX.X, ALU.max).then_inc(ext_done, 1)
            nc.vector.tensor_reduce(ext[:, B:2 * B], s2[:], AX.X, ALU.min, negate=True).then_inc(ext_done, 1)
            nc.vector.tensor_scalar(keep["s2_08"][:], s2[:], 1.0 - SLOPE, None, ALU.mult)
            nc.vector.tensor_scalar(keep["s2_02"][:], s2[:], SLOPE, None, ALU.mult)
            dve.wait_ge(levels_in, 2)
            nc.vector.tensor_copy(lev[:], lev_i[:]).then_inc(step_done, 1)
            dve.wait_ge(step_done, 1)
            nc.vector.tensor_scalar(rank[:], lev[:].unsqueeze(1).to_broadcast([P, B, LEVELS]), 1.0, None, ALU.add).then_inc(step_done, 1)
            dve.wait_ge(ext_turned, 1)
            nc.vector.tensor_reduce(ext_col[:], ext_ps[:], AX.X, ALU.max).then_inc(diag_done, 1)
            dve.wait_ge(diag_done, 1)
            nc.vector.tensor_scalar(ext_diag[:], keep["ident"][0:2 * B, 0:2 * B], ext_col[:, 0:1], None, ALU.mult).then_inc(diag_done, 1)
            dve.wait_ge(spread, 1)
            nc.vector.tensor_copy(ext_all[:], all_ps[:]).then_inc(step_done, 1)
            dve.wait_ge(step_done, 3)
            nc.vector.tensor_tensor(step[:], ext_all[:, 0:B], ext_all[:, B:2 * B], ALU.add).then_inc(step_done, 1)
            dve.wait_ge(step_done, 4)
            nc.vector.tensor_scalar(step[:], step[:], 1.0 / (LEVELS - 1), None, ALU.mult).then_inc(step_done, 1)
            dve.wait_ge(step_done, 5)
            for b in range(B):
                last = nc.vector.tensor_scalar(tau[:, b, :], lev[:], step[:, b:b + 1], ext_all[:, B + b:B + b + 1],
                                               ALU.mult, ALU.subtract)
            last.then_inc(step_done, 1)
            dve.wait_ge(step_done, 6)
            for t in range(T):
                nc.vector.tensor_tensor(above[:, t, :].rearrange("p (b l) -> p b l", l=LEVELS),
                                        s2[:, :, t:t + 1].to_broadcast([P, B, LEVELS]), tau[:], ALU.is_ge).then_inc(above_done, 1)
            for t in range(T):
                dve.wait_ge(counted, t + 1)
                if first:
                    nc.vector.tensor_copy(deg[:, t:t + 1], cnt_ps[:, t % 4, 0:1])
                if t >= 2:
                    dve.wait_ge(top_done, t - 1)
                nc.vector.scalar_tensor_tensor(out=hit[:, t % 2, :], in0=cnt_ps[:, t % 4, :], scalar=0.0,
                                               in1=rank[:].rearrange("p b l -> p (b l)"), op0=ALU.is_gt, op1=ALU.mult).then_inc(hit_done, 1)
                dve.wait_ge(hit_done, t + 1)
                nc.vector.tensor_reduce(top[:, :, t], hit[:, t % 2, :].rearrange("p (b l) -> p b l", l=LEVELS),
                                        AX.X, ALU.max).then_inc(top_done, 1)
            by_batch = [P, B, T]
            dve.wait_ge(top_done, T)
            nc.vector.tensor_scalar(top[:], top[:], -1.0, None, ALU.add).then_inc(shifts_done, 1)
            dve.wait_ge(shifts_done, 1)
            nc.vector.tensor_tensor(top[:], top[:], step[:].unsqueeze(2).to_broadcast(by_batch), ALU.mult).then_inc(shifts_done, 1)
            dve.wait_ge(shifts_done, 2)
            nc.vector.tensor_tensor(top[:], top[:], ext_all[:, B:2 * B].unsqueeze(2).to_broadcast(by_batch),
                                    ALU.subtract).then_inc(shifts_done, 1)
            dve.wait_ge(shifts_done, 3)
            nc.vector.tensor_tensor(top[:], top[:], s1[:], ALU.add).then_inc(shifts_done, 1)
            dve.wait_ge(shifts_done, 4)
            nc.vector.scalar_tensor_tensor(out=lk[:], in0=top[:], scalar=SLOPE, in1=top[:], op0=ALU.mult, op1=ALU.max).then_inc(shifts_done, 1)
            dve.wait_ge(shifts_done, 5)
            nc.vector.tensor_tensor(keep["u"][:], s1[:], lk[:], ALU.subtract).then_inc(shifts_done, 1)
            nc.vector.scalar_tensor_tensor(out=keep["v"][:], in0=s1[:], scalar=SLOPE, in1=lk[:], op0=ALU.mult,
                                           op1=ALU.subtract).then_inc(shifts_done, 1)
            if first:
                nc.vector.tensor_scalar(keep["has_deg"][:], deg[:], 0.0, None, ALU.is_gt).then_inc(shifts_done, 1)
                nc.vector.tensor_scalar(deg[:], deg[:], 1.0, None, ALU.max).then_inc(shifts_done, 1)
                dve.wait_ge(shifts_done, 9)
                nc.vector.reciprocal(keep["rdeg"][:], deg[:]).then_inc(shifts_done, 1)
            dve.wait_ge(rows_turned, 1)
            nc.vector.tensor_copy(rows[:], rows_ps[:]).then_inc(rows_kept, 1)

        @block.tensor
        def _(pe):
            pe.wait_ge(ext_done, 2)
            nc.tensor.transpose(ext_ps[:], ext[:], keep["ident"][:]).then_inc(ext_turned, 1)
            pe.wait_ge(levels_in, 2)
            pe.wait_ge(diag_done, 2)
            nc.tensor.matmul(all_ps[:], ones[:], ext_diag[:], start=True, stop=True).then_inc(spread, 1)
            for it in range(T):
                if it >= 4:
                    pe.wait_ge(hit_done, it - 3)
                for jt in range(T):
                    if it == 0:
                        pe.wait_ge(above_done, jt + 1)
                    mm = nc.tensor.matmul(cnt_ps[:, it % 4, :], keep["mask_t"][:, jt, it * P:(it + 1) * P], above[:, jt, :],
                                          start=(jt == 0), stop=(jt == T - 1))
                mm.then_inc(counted, 1)
            pe.wait_ge(shifts_done, 7)
            for k, m in enumerate(("u", "v")):
                mm = nc.tensor.transpose(rows_ps[:, k, :], keep[m][:].rearrange("p b t -> p (b t)"), keep["ident"][:])
            mm.then_inc(rows_turned, 1)

        @block.sync
        def _(sp):
            sp.wait_ge(rows_kept, 1)
            for k, m in enumerate(("u_rows", "v_rows")):
                sp.dma_start(io[m].rearrange("b (t p) -> (b t) p", p=P), rows[:, k, :]).then_inc(rows_stored, 16)
            sp.wait_ge(rows_stored, 32)


def gat_attention(nc, io, keep, name, x_in, x_out, residual_elu):
    HALF = N // 2
    IT = HALF // P
    STEPS = 4 * T
    ZB, PB = 4, 8
    mine = [g for g in range(STEPS) if g % T in (2, 5, 8)]
    FIN = (10, 12, 14)
    STAGES = 3 if residual_elu else 1
    with ExitStack() as stack:
        s = Scope(nc, stack, name)
        h = s.sb("h", [P, 2, T, F + 1])
        x = s.sb("x", [P, 2, T, F])
        urow = s.sb("urow", [P, 2, N])
        vrow = s.sb("vrow", [P, 2, N])
        s2_02 = s.sb("s2_02", [P, 2, T])
        z = s.sb("z", [P, ZB, HALF])
        w = s.sb("w", [P, PB, HALF])
        rz = s.sb("rz", [P, IT])
        y = s.sb("y", [P, IT, F])
        e = s.sb("e", [P, IT, F])
        o = s.sb("o", [P, IT, F])
        acc = s.ps("acc", [P, 2, 3, BANK])
        h_loaded, x_loaded = [s.sem(f"h_loaded{k}") for k in range(2)], [s.sem(f"x_loaded{k}") for k in range(2)]
        rows_loaded = [s.sem(f"rows_loaded{k}") for k in range(2)]
        z_ready, exp_done, masked_pool, masked_dve = s.sem("z_ready"), s.sem("exp_done"), s.sem("masked_pool"), s.sem("masked_dve")
        weighed, drained = s.sem("weighed"), s.sem("drained")
        rz_done, y_ready, e_ready, o_ready, o_stored, r_done = (s.sem("rz_done"), s.sem("y_ready"), s.sem("e_ready"),
                                                                s.sem("o_ready"), [s.sem(f"o_stored{k}") for k in range(2)], s.sem("r_done"))
        block = s.block()

        def tile(half, it):
            return acc[:, half, it // 3, (it % 3) * (F + 1):(it % 3 + 1) * (F + 1)]

        def half_rows(dram, b, half):
            return node_tiles(dram, b)[:, half * IT * F:(half + 1) * IT * F]

        @block.sync
        def _(sp):
            def load(b, k):
                for rows, m in ((urow, "u_rows"), (vrow, "v_rows")):
                    sp.dma_start(rows[:, k, :], io[m][bass.ds(b, 1), :].partition_broadcast(P)).then_inc(rows_loaded[k], 16)
                sp.dma_start(h[:, k], io["h_nodes"][bass.ds(b, 1)].rearrange("one p t f -> p (one t) f")).then_inc(h_loaded[k], 16)
                sp.dma_start(flat(x[:, k]), node_tiles(x_in, b)).then_inc(x_loaded[k], 16)

            def store(b, half, n):
                if residual_elu:
                    sp.wait_ge(o_ready, n + 1)
                else:
                    sp.wait_ge(drained, n + 2)
                sp.dma_start(half_rows(x_out, b, half), flat(o[:])).then_inc(o_stored[half], 16)

            load(0, 0)
            load(1, 1)
            with sp.Fori(0, B // 2) as i:
                with sp.If(i > 0):
                    store(nc.s_assert_within(2 * i - 1, 0, B - 1, skip_runtime_bounds_check_because="only where i > 0"), 1, 4 * i)
                    load(2 * i + 1, 1)
                store(2 * i, 0, 4 * i + 1)
                store(2 * i, 1, 4 * i + 2)
                with sp.If(i < B // 2 - 1):
                    load(nc.s_assert_within(2 * i + 2, 0, B - 1, skip_runtime_bounds_check_because="only before the last i"), 0)
                store(2 * i + 1, 0, 4 * i + 3)
            store(B - 1, 1, 2 * B)
            for half in range(2):
                sp.wait_ge(o_stored[half], 16 * B)

        @block.vector
        def _(dve):
            def stored_before(half, stores):
                dve.wait_ge(o_stored[1 - half], 16 * stores)

            def finish(k, half, n, stores, loads):
                dve.wait_ge(weighed, T * (n + 1) + PB)
                dve.wait_ge(h_loaded[k], 16 * loads)
                dve.wait_ge(x_loaded[k], 16 * loads)
                sums = acc[:, half, :, 0:3 * (F + 1)].rearrange("p k (i f) -> p k i f", f=F + 1)[:, :, :, F]
                nc.vector.reciprocal(rz[:, 0:6].rearrange("p (k i) -> p k i", i=3), sums[:, 0:2, :])
                nc.vector.reciprocal(rz[:, 6:8], sums[:, 2, 0:2]).then_inc(rz_done, 1)
                dve.wait_ge(rz_done, n + 1)
                if not residual_elu:
                    stored_before(half, stores)
                for it in range(IT):
                    add = h[:, k, half * IT + it, 0:F] if residual_elu else x[:, k, half * IT + it, :]
                    last = nc.vector.scalar_tensor_tensor(out=(y if residual_elu else o)[:, it, :], in0=tile(half, it)[:, 0:F],
                                                          scalar=rz[:, it:it + 1], in1=add, op0=ALU.mult, op1=ALU.add)
                last.then_inc(drained, 1)

            def add_x(k, half, n, stores):
                dve.wait_ge(drained, n + 1 + 2)
                stored_before(half, stores)
                nc.vector.scalar_tensor_tensor(out=o[:], in0=y[:], scalar=0.0, in1=x[:, k, half * IT:(half + 1) * IT, :],
                                               op0=ALU.max, op1=ALU.add).then_inc(r_done, 1)

            def add_elu(n):
                dve.wait_ge(r_done, n + 1)
                dve.wait_ge(e_ready, 2 * n + 3)
                nc.vector.tensor_tensor(o[:], o[:], e[:], ALU.subtract).then_inc(o_ready, 1)

            def finish_stage(stage, k, half, n, stores, loads):
                if stage == 0:
                    finish(k, half, n, stores, loads)
                elif stage == 1:
                    add_x(k, half, n, stores)
                else:
                    add_elu(n)

            dve.sem_inc(drained, 2)
            dve.sem_inc(o_ready, 1)
            with dve.Fori(0, B // 2) as i:
                for g in range(STEPS):
                    k, half, jt = g // (2 * T), g // T % 2, g % T
                    b = 2 * i + k
                    if g % (2 * T) == 0:
                        dve.wait_ge(rows_loaded[k], 32 * (i + 1))
                    dve.wait_ge(exp_done, STEPS * i + g + 1)
                    if g % (2 * T) == 0:
                        nc.vector.tensor_copy(s2_02[:, k:k + 1, :], keep["s2_02"][:, bass.ds(b, 1), :])
                    rows = slice(half * HALF, (half + 1) * HALF)
                    nc.vector.scalar_tensor_tensor(out=z[:, g % ZB, :], in0=urow[:, k, rows], scalar=keep["s2_08"][:, bass.ds(b, 1), jt],
                                                   in1=vrow[:, k, rows], op0=ALU.add, op1=ALU.max).then_inc(z_ready, 1)
                    if g - 1 in mine:
                        dve.wait_ge(exp_done, STEPS * i + g + ZB)
                        q = (g - 1) % PB
                        m_half, m_jt = (g - 1) // T % 2, (g - 1) % T
                        nc.vector.tensor_tensor(w[:, q, :], w[:, q, :], keep["mask_t"][:, m_jt, m_half * HALF:(m_half + 1) * HALF],
                                                ALU.mult).then_inc(masked_dve, 1)
                    if g % T in FIN[:STAGES]:
                        stage = FIN.index(g % T)
                        n = g // T - 1
                        if n >= 0:
                            finish_stage(stage, n // 2, n % 2, 4 * i + n, 2 * i + (n + 1) // 2, i + 1)
                        else:
                            with dve.If(i > 0):
                                finish_stage(stage, 1, 1, 4 * i - 1, 2 * i, i)
            for stage in range(STAGES):
                finish_stage(stage, 1, 1, 2 * B - 1, B, B // 2)

        @block.scalar
        def _(act):
            def exp_y(n):
                act.wait_ge(drained, n + 1 + 2)
                if residual_elu:
                    act.wait_ge(o_ready, n + 1)
                    nc.scalar.activation(e[:], y[:], ACT.Exp).then_inc(e_ready, 1)
                    act.wait_ge(e_ready, 2 * n + 2)
                    nc.scalar.activation(e[:], e[:], ACT.Relu, bias=1.0, scale=-1.0).then_inc(e_ready, 1)

            act.sem_inc(e_ready, 1)
            act.sem_inc(exp_done, ZB)
            with act.Fori(0, B // 2) as i:
                for g in range(STEPS):
                    k, jt = g // (2 * T), g % T
                    act.wait_ge(z_ready, STEPS * i + g + 1)
                    act.wait_ge(weighed, STEPS * i + g + 1)
                    nc.scalar.activation(w[:, g % PB, :], z[:, g % ZB, :], ACT.Exp,
                                         bias=s2_02[:, k, jt:jt + 1]).then_inc(exp_done, 1)
                    if g % T == FIN[0] + 1 and residual_elu:
                        n = g // T - 1
                        if n >= 0:
                            exp_y(4 * i + n)
                        else:
                            with act.If(i > 0):
                                exp_y(4 * i - 1)
            if residual_elu:
                exp_y(2 * B - 1)

        @block.gpsimd
        def _(pool):
            with pool.Fori(0, B // 2) as i:
                for g in range(STEPS):
                    if g in mine:
                        continue
                    half, jt = g // T % 2, g % T
                    pool.wait_ge(exp_done, STEPS * i + g + 1 + ZB)
                    nc.gpsimd.tensor_tensor(w[:, g % PB, :], w[:, g % PB, :], keep["mask_t"][:, jt, half * HALF:(half + 1) * HALF],
                                            ALU.mult).then_inc(masked_pool, 1)

        @block.tensor
        def _(pe):
            pe.sem_inc(weighed, PB)
            with pe.Fori(0, B // 2) as i:
                for g in range(STEPS):
                    k, half, jt = g // (2 * T), g // T % 2, g % T
                    if g % (2 * T) == 0:
                        pe.wait_ge(h_loaded[k], 16 * (i + 1))
                    if jt == 0:
                        pe.wait_ge(drained, 4 * i + g // T + 1)
                    if g in mine:
                        pe.wait_ge(masked_dve, len(mine) * i + mine.index(g) + 1)
                    else:
                        pe.wait_ge(masked_pool, (STEPS - len(mine)) * i + g - sum(m < g for m in mine) + 1)
                    for it in range(IT):
                        mm = nc.tensor.matmul(tile(half, it), w[:, g % PB, it * P:(it + 1) * P], h[:, k, jt, :],
                                              start=(jt == 0 and it % 3 == 0), stop=(jt == T - 1), skip_group_check=True)
                    mm.then_inc(weighed, 1)


def nodes1(nc, io, keep):
    with ExitStack() as stack:
        s = Scope(nc, stack, "p1")
        x = [s.sb(f"x{k}", [P, T, F]) for k in range(2)]
        hn = s.sb("hn", [P, T, F])
        hT = s.sb("hT", [P, N])
        wqk = [s.sb("wq", [P, F]), s.sb("wk", [P, F])]
        wv = s.sb("wv", [P, F])
        hi = [[s.sb(f"{m}_hi{k}", [P, N], F16) for m in "qk"] for k in range(2)]
        lo = [[s.sb(f"{m}_lo{k}", [P, N], F16) for m in "qk"] for k in range(2)]
        v = [s.sb(f"v{k}", [P, 2, T, 2, HD + 1]) for k in range(2)]
        st = s.sb("st", [P, T, 6])
        tmp = s.sb("tmp", [P, 4, T])
        rstd, shift, minus_half = s.sb("rstd", [P, T]), s.sb("shift", [P, T]), s.sb("minus_half", [P, T])
        tp_ps = s.ps("tp_ps", [P, 2, BANK])
        qk_ps = s.ps("qk_ps", [P, 4, BANK])
        v_ps = s.ps("v_ps", [P, 2, BANK])
        weights_in, consts_ready, x_loaded = s.sem("weights_in"), s.sem("consts_ready"), [s.sem(f"x_loaded{k}") for k in range(2)]
        chain, rooted, normed, turned, hT_kept = s.sem("chain"), s.sem("rooted"), s.sem("normed"), s.sem("turned"), s.sem("hT_kept")
        qk_done, hi_done, lo_done, v_done, v_kept = (s.sem("qk_done"), s.sem("hi_done"), s.sem("lo_done"), s.sem("v_done"),
                                                     s.sem("v_kept"))
        stored = [s.sem(f"stored{k}") for k in range(2)]
        block = s.block()
        CHAIN = NORM_STEPS + 1
        QK = 2 * CH

        def turns(eng, first, turn, last):
            first()
            with eng.Fori(0, B // 2 - 1) as i:
                turn(2 * i, 0, i)
                turn(2 * i + 1, 1, i)
            turn(B - 2, 0, B // 2 - 1)
            last(B - 1, 1, B // 2 - 1)

        def last_two(i):
            return isinstance(i, int) and i == B // 2 - 1

        @block.sync
        def _(sp):
            def load(b, k):
                sp.dma_start(flat(x[k][:]), node_tiles(io["x1"], b)).then_inc(x_loaded[k], 16)

            def store(b, k, i):
                sp.wait_ge(hi_done, QK * (b + 1))
                sp.wait_ge(lo_done, QK * (b + 1))
                for part, names in ((hi[k], ("q_hi", "k_hi")), (lo[k], ("q_lo", "k_lo"))):
                    for buf, m in zip(part, names):
                        sp.dma_start(io[m][bass.ds(b, 1)].rearrange("one p n -> p (one n)"), buf[:]).then_inc(stored[k], 16)
                sp.wait_ge(v_kept, CH * (b + 1) + 2)
                sp.dma_start(io["v"][bass.ds(b, 1)].rearrange("one g p n -> p (one g) n"),
                             v[k][:].rearrange("p g t a d -> p g (t a d)")).then_inc(stored[k], 16)

            def first():
                load(0, 0)
                load(1, 1)
                for buf, m in ((wqk[0], "L1_gnn_W_q"), (wqk[1], "L1_gnn_W_k"), (wv, "L1_gnn_W_v")):
                    sp.dma_start(buf[:], io[m][:]).then_inc(weights_in, 16)

            def turn(b, k, i):
                if not last_two(i):
                    sp.wait_ge(normed, CH * (b + 1))
                    load(b + 2, k)
                store(b, k, i)

            turns(sp, first, turn, store)
            for k in range(2):
                sp.wait_ge(stored[k], 80 * B // 2)

        @block.gpsimd
        def _(pool):
            nc.gpsimd.memset(minus_half[:], -0.5).then_inc(consts_ready, 1)
            for k in range(2):
                nc.gpsimd.memset(v[k][:], 1.0).then_inc(consts_ready, 1)
            pool.wait_ge(consts_ready, 3)
            with pool.Fori(0, B) as b:
                norm_root(nc, pool, tmp, minus_half[:], rstd[:], chain, b * CHAIN + NORM_STEPS, rooted)

        @block.vector
        def _(dve):
            def stats(b, k, i):
                dve.wait_ge(x_loaded[k], 16 * (i + 1))
                for t in range(T):
                    last = nc.vector.bn_stats(st[:, t, :], x[k][:, t, :])
                last.then_inc(chain, 1)
                dve.wait_ge(chain, b * CHAIN + 1)
                dve.wait_ge(normed, CH * b)
                norm_stats(nc, dve, st, tmp, chain, b * CHAIN + 1)

            def shifts(b):
                norm_shift(nc, dve, tmp, rstd[:], shift[:], chain, rooted, b + 1)

            def split(b, k, i, q):
                for a in range(2):
                    c = 2 * q + a
                    dve.wait_ge(hi_done, QK * b + c + 1)
                    nc.vector.tensor_tensor(lo[k][a][:, q * BANK:(q + 1) * BANK], qk_ps[:, c % 4, :],
                                            hi[k][a][:, q * BANK:(q + 1) * BANK], ALU.subtract).then_inc(lo_done, 1)
                dve.wait_ge(v_done, CH * b + q + 1)
                for g in range(2):
                    ins = nc.vector.tensor_copy(v[k][:, g, 4 * q:4 * q + 4, :, 0:HD],
                                                v_ps[:, q % 2, :].rearrange("p (t g a d) -> p g t a d", g=2, a=2, d=HD)[:, g])
                ins.then_inc(v_kept, 1)

            def first():
                stats(0, 0, 0)
                shifts(0)

            def turn(b, k, i, more=True):
                if more:
                    stats(b + 1, 1 - k, i + k)
                dve.wait_ge(stored[k], 80 * i)
                split(b, k, i, 0)
                if more:
                    shifts(b + 1)
                for q in range(1, CH):
                    split(b, k, i, q)

            dve.sem_inc(v_kept, 2)
            dve.wait_ge(consts_ready, 3)
            turns(dve, first, turn, lambda b, k, i: turn(b, k, i, False))

        @block.scalar
        def _(act):
            def norm(b, k, q):
                if q == 0:
                    act.wait_ge(chain, (b + 1) * CHAIN)
                for t in range(4 * q, 4 * q + 4):
                    last = nc.scalar.activation(hn[:, t, :], x[k][:, t, :], ACT.Relu, bias=shift[:, t:t + 1], scale=rstd[:, t:t + 1])
                last.then_inc(normed, 1)

            def first():
                for q in range(CH):
                    norm(0, 0, q)

            def turn(b, k, i, more=True):
                act.wait_ge(stored[k], 80 * i)
                for q in range(CH):
                    act.wait_ge(turned, CH * b + q + 1)
                    nc.scalar.copy(hT[:, q * BANK:(q + 1) * BANK], tp_ps[:, q % 2, :]).then_inc(hT_kept, 1)
                    if q >= 1 and more:
                        norm(b + 1, 1 - k, q - 1)
                    for a in range(2):
                        c = 2 * q + a
                        act.wait_ge(qk_done, QK * b + c + 1)
                        nc.scalar.copy(hi[k][a][:, q * BANK:(q + 1) * BANK], qk_ps[:, c % 4, :]).then_inc(hi_done, 1)
                if more:
                    norm(b + 1, 1 - k, CH - 1)

            act.sem_inc(hT_kept, 2)
            turns(act, first, turn, lambda b, k, i: turn(b, k, i, False))

        @block.tensor
        def _(pe):
            def turn_nodes(b, q):
                pe.wait_ge(normed, CH * b + q + 1)
                pe.wait_ge(hT_kept, CH * b + q + 1)
                for t in range(4 * q, 4 * q + 4):
                    mm = nc.tensor.transpose(tp_ps[:, q % 2, (t % 4) * P:(t % 4 + 1) * P], hn[:, t, :], keep["ident"][:])
                mm.then_inc(turned, 1)

            def batch(b):
                turn_nodes(b, 0)
                for q in range(CH):
                    if q + 1 < CH:
                        turn_nodes(b, q + 1)
                    pe.wait_ge(hT_kept, CH * b + q + 3)
                    for a in range(2):
                        c = 2 * q + a
                        pe.wait_ge(lo_done, QK * b + max(c - 3, 0))
                        nc.tensor.matmul(qk_ps[:, c % 4, :], wqk[a][:], hT[:, q * BANK:(q + 1) * BANK], start=True,
                                         stop=True).then_inc(qk_done, 1)
                    pe.wait_ge(v_kept, CH * b + q + 1)
                    for t in range(4 * q, 4 * q + 4):
                        mm = nc.tensor.matmul(v_ps[:, q % 2, (t % 4) * P:(t % 4 + 1) * P], hT[:, t * P:(t + 1) * P], wv[:],
                                              start=True, stop=True)
                    mm.then_inc(v_done, 1)

            pe.wait_ge(weights_in, 16 * 3)
            with pe.Fori(0, B) as b:
                batch(b)


def head_attention(nc, io, keep):
    SCALE = float(HD) ** -0.5
    K = 3 * HD
    STEPS = CH * T
    BODY = 2 * STEPS
    UNITS = 2 * T * CH
    FIRST, LAST = 4, 59
    PB, LAG = 4, 3
    SB, MB = 3, 3
    done_by = [0] * (STEPS + 1)
    for g in range(STEPS):
        done_by[g + 1] = min(UNITS, max(0, (g + 1 - FIRST) * UNITS // (LAST - FIRST)))
    mine = [g for g in range(BODY) if not FIRST <= g % STEPS < LAST or g % 5 == 3]
    with ExitStack() as stack:
        s = Scope(nc, stack, "a1")
        mbias = s.sb("mbias", [P, T, N], BF16)
        qs = [[s.sb(f"qs{u}{a}", [K + 1, N], F16) for a in range(2)] for u in range(2)]
        ks = [[s.sb(f"ks{u}{a}", [K + 1, N], F16) for a in range(2)] for u in range(2)]
        v = [s.sb(f"v{u}", [P, T, 2, HD + 1]) for u in range(2)]
        w = s.sb("w", [P, PB, 2, BANK])
        mx = s.sb("mx", [P, 2 * T, CH])
        mrow = s.sb("mrow", [P, 2 * T])
        mshift = s.sb("mshift", [2 * T, P], F16)
        oe = s.sb("oe", [2 * (HD * 2), 2, BANK])
        sc_ps = s.ps("sc_ps", [P, SB, BANK])
        mx_ps = s.ps("mx_ps", [P, MB, BANK])
        o_ps = s.ps("o_ps", [P, 2, BANK])
        mbias_loaded, units_ready = s.sem("mbias_loaded"), s.sem("units_ready")
        qk_loaded, v_loaded = [s.sem(f"qk_loaded{u}") for u in range(2)], [s.sem(f"v_loaded{u}") for u in range(2)]
        scored, exp_done, masked_pool, masked_dve, weighed = (s.sem("scored"), s.sem("exp_done"), s.sem("masked_pool"),
                                                              s.sem("masked_dve"), s.sem("weighed"))
        mx_scored, mx_taken, rows_done, rows_turned = s.sem("mx_scored"), s.sem("mx_taken"), s.sem("rows_done"), s.sem("rows_turned")
        shift_ready, shift_stored, shift_placed = s.sem("shift_ready"), s.sem("shift_stored"), s.sem("shift_placed")
        o_kept, o_stored = s.sem("o_kept"), [s.sem(f"o_stored{k}") for k in range(2)]
        block = s.block()

        def load(sp, b, u):
            for a in range(2):
                head = slice((2 * u + a) * HD, (2 * u + a + 1) * HD)
                for row, m in ((0, "k_hi"), (1, "k_lo"), (2, "k_hi")):
                    sp.dma_start(ks[u][a][row * HD:(row + 1) * HD, :],
                                 io[m][bass.ds(b, 1), head, :].rearrange("one p n -> p (one n)")).then_inc(qk_loaded[u], 16)
                for row, m in ((0, "q_hi"), (1, "q_hi"), (2, "q_lo")):
                    sp.dma_start(qs[u][a][row * HD:(row + 1) * HD, :],
                                 io[m][bass.ds(b, 1), head, :].rearrange("one p n -> p (one n)")).then_inc(qk_loaded[u], 16)

        def load_v(sp, b, u):
            sp.dma_start(v[u][:].rearrange("p t a d -> p (t a d)"),
                         io["v"][bass.ds(b, 1), u].rearrange("one p n -> p (one n)")).then_inc(v_loaded[u], 16)

        LOADS = 16 * 12

        def place_shift(sp, pair, u):
            sp.wait_ge(shift_ready, pair + 1)
            sp.dma_start(io["shifts"][:], mshift[:]).then_inc(shift_stored, 16)
            sp.wait_ge(shift_stored, 16 * (pair + 1))
            for a in range(2):
                sp.dma_start(qs[u][a][K:K + 1, :],
                             io["shifts"][a * T:(a + 1) * T, :].rearrange("(o t) p -> o (t p)", o=1)).then_inc(shift_placed, 16)

        @block.sync
        def _(sp):
            load(sp, 0, 0)
            load_v(sp, 0, 0)
            for t in range(T):
                sp.dma_start(mbias[:, t, :], io["mask_bias"][t * P:(t + 1) * P, :]).then_inc(mbias_loaded, 16)
            load(sp, 0, 1)
            load_v(sp, 0, 1)
            place_shift(sp, 0, 0)

            def store(b, c):
                sp.wait_ge(o_kept, 2 * CH * b + c + 1 + 2)
                u, rows = c // CH, slice(c % CH * BANK, (c % CH + 1) * BANK)
                for a in range(2):
                    head = 2 * u + a
                    sp.dma_start(io["heads_t"][bass.ds(b, 1), head * HD:(head + 1) * HD, rows].rearrange("one p n -> p (one n)"),
                                 oe[2 * HD * a:2 * HD * a + HD, c % 2, :]).then_inc(o_stored[c % 2], 16)
                    sp.dma_start(io["sums"][bass.ds(b, 1), head:head + 1, rows].rearrange("one p n -> p (one n)"),
                                 oe[2 * HD * a + HD:2 * HD * a + HD + 1, c % 2, :]).then_inc(o_stored[c % 2], 16)

            with sp.Fori(0, B) as b:
                following = (b + 1) % B
                for c in range(CH - 1):
                    store(b, c)
                place_shift(sp, 2 * b + 1, 1)
                sp.wait_ge(scored, 2 * (BODY * b + STEPS))
                load(sp, following, 0)
                store(b, CH - 1)
                sp.wait_ge(weighed, BODY * b + STEPS + PB)
                load_v(sp, following, 0)
                for c in range(CH, 2 * CH - 1):
                    store(b, c)
                place_shift(sp, 2 * b + 2, 0)
                sp.wait_ge(scored, 2 * BODY * (b + 1))
                load(sp, following, 1)
                store(b, 2 * CH - 1)
                sp.wait_ge(weighed, BODY * (b + 1) + PB)
                load_v(sp, following, 1)
            for u in range(2):
                sp.wait_ge(qk_loaded[u], LOADS * (B + 1))
                sp.wait_ge(v_loaded[u], 16 * (B + 1))
                sp.wait_ge(o_stored[u], 64 * CH * B)
            sp.wait_ge(shift_placed, 32 * (2 * B + 1))

        @block.tensor
        def _(pe):
            def maxima(u, n0, n1, pair):
                for n in range(n0, n1):
                    a, t, c = n // (T * CH), n // CH % T, n % CH
                    if n == 0:
                        pe.wait_ge(shift_ready, pair)
                    pe.wait_ge(mx_taken, UNITS * pair + n + 1)
                    nc.tensor.matmul(mx_ps[:, n % MB, :], qs[u][a][0:K, t * P:(t + 1) * P], ks[u][a][0:K, c * BANK:(c + 1) * BANK],
                                     start=True, stop=True).then_inc(mx_scored, 1)

            def turn_maxima(pair):
                pe.wait_ge(rows_done, pair + 1)
                nc.tensor.transpose(mx_ps[0:2 * T, 0, 0:P], mrow[:], keep["ident"][:]).then_inc(rows_turned, 1)

            def weigh(g, i):
                u, c, jt = g // STEPS, g // T, g % T
                if jt == 0:
                    pe.wait_ge(o_kept, 2 * CH * i + c + 1)
                if g % STEPS == 0:
                    pe.wait_ge(v_loaded[u], 16 * (i + 1))
                if g in mine:
                    pe.wait_ge(masked_dve, len(mine) * i + mine.index(g) + 1)
                else:
                    pe.wait_ge(masked_pool, (BODY - len(mine)) * i + g - sum(m < g for m in mine) + 1)
                for a in range(2):
                    mm = nc.tensor.matmul(o_ps[2 * HD * a:2 * HD * a + HD + 1, c % 2, :], v[u][:, jt, a, :], w[:, g % PB, a, :],
                                          start=(jt == 0), stop=(jt == T - 1))
                mm.then_inc(weighed, 1)

            pe.sem_inc(weighed, PB)
            pe.wait_ge(qk_loaded[0], LOADS)
            maxima(0, 0, UNITS, 0)
            turn_maxima(0)
            pe.wait_ge(units_ready, 4)
            with pe.Fori(0, B) as i:
                for g in range(BODY):
                    u, r = g // STEPS, g % STEPS
                    c, jt = r // T, r % T
                    if r == 0:
                        pe.wait_ge(shift_placed, 32 * (2 * i + u + 1))
                    for a in range(2):
                        n = 2 * g + a
                        pe.wait_ge(exp_done, 2 * BODY * i + (n + 1 if n else SB))
                        nc.tensor.matmul(sc_ps[:, n % SB, :], ks[u][a][:, jt * P:(jt + 1) * P],
                                         qs[u][a][:, c * BANK:(c + 1) * BANK], start=True, stop=True).then_inc(scored, 1)
                    if r == FIRST:
                        pe.wait_ge(qk_loaded[1 - u], LOADS * (i + 1 + u))
                    half = (done_by[r] + done_by[r + 1]) // 2
                    maxima(1 - u, done_by[r], half, 2 * i + u + 1)
                    if g >= LAG:
                        weigh(g - LAG, i)
                    maxima(1 - u, half, done_by[r + 1], 2 * i + u + 1)
                    if r == LAST:
                        turn_maxima(2 * i + u + 1)
                for g in range(BODY - LAG, BODY):
                    weigh(g, i)

        @block.vector
        def _(dve):
            def take(n0, n1, pair):
                for n in range(n0, n1):
                    t, c = n // CH % T, n % CH
                    due = UNITS * pair + n + 1
                    if not isinstance(due, int):
                        dve.compute_val(due)
                    dve.wait_ge(mbias_loaded, 16 * T)
                    dve.wait_ge(mx_scored, due)
                    nc.vector.tensor_tensor_reduce(out=mx_ps[:, n % MB, :], in0=mx_ps[:, n % MB, :],
                                                   in1=mbias[:, t, c * BANK:(c + 1) * BANK], scale=1.0, scalar=-3.0e38,
                                                   op0=ALU.add, op1=ALU.max,
                                                   accum_out=mx[:, n // CH, c:c + 1]).then_inc(mx_taken, 1)

            def row_maxima(pair):
                dve.wait_ge(mx_taken, UNITS * (pair + 1) + MB)
                nc.vector.tensor_reduce(mrow[:], mx[:], AX.X, ALU.max).then_inc(rows_done, 1)

            def shifts(pair):
                dve.wait_ge(rows_turned, pair + 1)
                dve.wait_ge(shift_placed, 32 * pair)
                nc.vector.tensor_scalar(mshift[:], mx_ps[0:2 * T, 0, 0:P], -1.0 / SHIFT_UNIT, None, ALU.mult).then_inc(shift_ready, 1)

            def mask(g, i):
                if g in mine:
                    c, jt = g // T % CH, g % T
                    dve.wait_ge(exp_done, 2 * (BODY * i + g + 1) + SB)
                    nc.vector.tensor_tensor(w[:, g % PB], w[:, g % PB],
                                            keep["mask_t"][:, jt, c * BANK:(c + 1) * BANK].unsqueeze(1).to_broadcast([P, 2, BANK]),
                                            ALU.mult).then_inc(masked_dve, 1)

            dve.sem_inc(mx_taken, MB)
            for u in range(2):
                for a in range(2):
                    nc.vector.memset(ks[u][a][K:K + 1, :], SHIFT_UNIT).then_inc(units_ready, 1)
            dve.wait_ge(mbias_loaded, 16 * T)
            take(0, UNITS, 0)
            row_maxima(0)
            shifts(0)
            with dve.Fori(0, B) as i:
                for g in range(BODY):
                    u, r = g // STEPS, g % STEPS
                    if g >= 1:
                        mask(g - 1, i)
                    take(done_by[r], done_by[r + 1], 2 * i + u + 1)
                    if r == LAST:
                        row_maxima(2 * i + u + 1)
                    if r == LAST + 1:
                        shifts(2 * i + u + 1)
                mask(BODY - 1, i)

        @block.scalar
        def _(act):
            def keep_rows(c, i):
                act.wait_ge(weighed, BODY * i + (c + 1) * T + PB)
                act.wait_ge(o_stored[c % 2], 64 * (CH * i + c // 2))
                for a in range(2):
                    rows = slice(2 * HD * a, 2 * HD * a + HD + 1)
                    ins = nc.scalar.copy(oe[rows, c % 2, :], o_ps[rows, c % 2, :])
                ins.then_inc(o_kept, 1)

            act.sem_inc(exp_done, SB)
            act.sem_inc(o_kept, 2)
            with act.Fori(0, B) as i:
                for g in range(BODY):
                    act.wait_ge(weighed, BODY * i + g + 1)
                    for a in range(2):
                        n = 2 * g + a
                        act.wait_ge(scored, 2 * BODY * i + n + 1)
                        nc.scalar.activation(w[:, g % PB, a], sc_ps[:, n % SB], ACT.Exp, scale=SCALE).then_inc(exp_done, 1)
                    if g >= T + LAG and (g - LAG) % T == 0:
                        keep_rows((g - LAG) // T - 1, i)
                keep_rows(2 * CH - 1, i)

        @block.gpsimd
        def _(pool):
            with pool.Fori(0, B) as i:
                for g in range(BODY):
                    if g in mine:
                        continue
                    c, jt = g // T % CH, g % T
                    pool.wait_ge(exp_done, 2 * (BODY * i + g + 1) + SB)
                    nc.gpsimd.tensor_tensor(w[:, g % PB], w[:, g % PB],
                                            keep["mask_t"][:, jt, c * BANK:(c + 1) * BANK].unsqueeze(1).to_broadcast([P, 2, BANK]),
                                            ALU.mult).then_inc(masked_pool, 1)


def nodes2(nc, io, keep):
    with ExitStack() as stack:
        s = Scope(nc, stack, "p2")
        ot = s.sb("ot", [P, N])
        all_sums = s.sb("all_sums", [P, BANK])
        rz = s.sb("rz", [HEADS, N])
        sel = s.sb("sel", [HEADS, HEADS, HD])
        x1 = s.sb("x1", [P, T, F])
        x1b = s.sb("x1b", [P, T, F])
        x2 = s.sb("x2", [P, T, F])
        hn = s.sb("hn", [P, T, F])
        hT = s.sb("hT", [P, N])
        g = s.sb("g", [P, T, 2, F], F16)
        own = s.sb("own", [P, T, F])
        wo = s.sb("wo", [P, F])
        wns = s.sb("wns", [P, 2 * F])
        bo, bs, bn = s.sb("bo", [P, F]), s.sb("bs", [P, F]), s.sb("bn", [P, F])
        bias = s.sb("bias", [P, T, F])
        st = s.sb("st", [P, T, 6])
        tmp = s.sb("tmp", [P, 4, T])
        rstd, shift, minus_half = s.sb("rstd", [P, T]), s.sb("shift", [P, T]), s.sb("minus_half", [P, T])
        rep_ps = s.ps("rep_ps", [P, 2, BANK])
        y_ps = s.ps("y_ps", [P, 2, BANK])
        tp_ps = s.ps("tp_ps", [P, 2, BANK])
        g_ps = s.ps("g_ps", [P, 2, 2, 2 * F])
        weights_in, consts_ready, sel_ready, bias_ready = (s.sem("weights_in"), s.sem("consts_ready"), s.sem("sel_ready"),
                                                           s.sem("bias_ready"))
        heads_loaded, x1_loaded = s.sem("heads_loaded"), s.sem("x1_loaded")
        spread, divided, y_done, x1b_done, x2_done = (s.sem("spread"), s.sem("divided"), s.sem("y_done"),
                                                               s.sem("x1b_done"), s.sem("x2_done"))
        chain, rooted, normed, turned, hT_kept = s.sem("chain"), s.sem("rooted"), s.sem("normed"), s.sem("turned"), s.sem("hT_kept")
        g_done, hi_done, lo_done, own_done = s.sem("g_done"), s.sem("hi_done"), s.sem("lo_done"), s.sem("own_done")
        x2_stored, g_stored, own_stored = s.sem("x2_stored"), s.sem("g_stored"), s.sem("own_stored")
        sums_loaded, rz_done, rz_stored = s.sem("sums_loaded"), s.sem("rz_done"), s.sem("rz_stored")
        block = s.block()
        CHAIN = NORM_STEPS + 1
        PAIRS = T // 2

        @block.sync
        def _(sp):
            sp.dma_start(wo[:], io["L1_gnn_W_o"][:]).then_inc(weights_in, 16)
            sp.dma_start(wns[:, 0:F], io["L2_gnn_W_neigh"][:]).then_inc(weights_in, 16)
            sp.dma_start(wns[:, F:2 * F], io["L2_gnn_W_self"][:]).then_inc(weights_in, 16)
            for buf, m in ((bo, "L1_gnn_b_o"), (bs, "L2_gnn_b_self"), (bn, "L2_gnn_b_neigh")):
                sp.dma_start(buf[:], io[m][0:1, :].partition_broadcast(P)).then_inc(weights_in, 16)
            def load(b):
                sp.wait_ge(x1b_done, b)
                sp.dma_start(flat(x1[:]), node_tiles(io["x1"], b)).then_inc(x1_loaded, 16)
                sp.wait_ge(spread, CH * b)
                sp.dma_start(rz[:], io["sums"][bass.ds(b, 1)].rearrange("one p n -> p (one n)")).then_inc(heads_loaded, 16)
                sp.wait_ge(y_done, CH * b)
                sp.dma_start(ot[:], io["heads_t"][bass.ds(b, 1)].rearrange("one p n -> p (one n)")).then_inc(heads_loaded, 16)

            def store_x2(b):
                sp.wait_ge(x2_done, CH * (b + 1))
                sp.dma_start(node_tiles(io["x2"], b), flat(x2[:])).then_inc(x2_stored, 16)

            def store(b):
                sp.wait_ge(lo_done, PAIRS * (b + 1))
                sp.wait_ge(hi_done, PAIRS * (b + 1))
                sp.dma_start(io["g"][bass.ds(b, 1)].rearrange("one p n -> p (one n)"),
                             g[:].rearrange("p t k f -> p (t k f)")).then_inc(g_stored, 16)
                sp.wait_ge(own_done, PAIRS * (b + 1))
                sp.dma_start(io["own"][bass.ds(b, 1)].rearrange("one p n -> p (one n)"), flat(own[:])).then_inc(own_stored, 16)

            across = io["sums"].rearrange("b h (c n) -> (b h c) n", n=BANK)
            sp.dma_start(all_sums[:], across).then_inc(sums_loaded, 16)
            sp.wait_ge(rz_done, 1)
            sp.dma_start(across, all_sums[:]).then_inc(rz_stored, 16)
            sp.wait_ge(rz_stored, 16)
            load(0)
            load(1)
            store_x2(0)
            with sp.Fori(0, B - 2) as b:
                load(b + 2)
                store_x2(b + 1)
                store(b)
            store_x2(B - 1)
            store(B - 2)
            store(B - 1)
            sp.wait_ge(x2_stored, 16 * B)
            sp.wait_ge(g_stored, 16 * B)
            sp.wait_ge(own_stored, 16 * B)

        @block.gpsimd
        def _(pool):
            nc.gpsimd.memset(minus_half[:], -0.5).then_inc(consts_ready, 1)
            nc.gpsimd.memset(sel[:], 1.0).then_inc(sel_ready, 1)
            pool.wait_ge(sel_ready, 1)
            nc.gpsimd.affine_select(out=sel[:], in_=sel[:], compare_op=ALU.is_equal, fill=0.0, base=0,
                                    pattern=[[-1, HEADS], [0, HD]], channel_multiplier=1).then_inc(consts_ready, 1)
            pool.wait_ge(weights_in, 16 * 6)
            pool.wait_ge(consts_ready, 2)

            def first(b):
                pool.wait_ge(x1_loaded, 16 * (b + 1))
                pool.wait_ge(x2_done, CH * b)
                nc.gpsimd.tensor_tensor(x1b[:], x1[:], bo[:].unsqueeze(1).to_broadcast([P, T, F]), ALU.add).then_inc(x1b_done, 1)

            def root(b):
                norm_root(nc, pool, tmp, minus_half[:], rstd[:], chain, b * CHAIN + NORM_STEPS, rooted)

            first(0)
            root(0)
            with pool.Fori(0, B - 1) as b:
                first(b + 1)
                root(b + 1)

        @block.vector
        def _(dve):
            def divide(b):
                dve.wait_ge(heads_loaded, 32 * (b + 1))
                for q in range(CH):
                    dve.wait_ge(spread, CH * b + q + 1)
                    nc.vector.tensor_tensor(ot[:, q * BANK:(q + 1) * BANK], ot[:, q * BANK:(q + 1) * BANK], rep_ps[:, q % 2, :],
                                            ALU.mult).then_inc(divided, 1)

            def first(b):
                dve.wait_ge(x1b_done, b + 1)
                dve.wait_ge(x2_stored, 16 * b)
                dve.wait_ge(normed, b)
                for q in range(CH):
                    dve.wait_ge(y_done, CH * b + q + 1)
                    nc.vector.tensor_tensor(x2[:, 4 * q:4 * q + 4, :], y_ps[:, q % 2, :].rearrange("p (t f) -> p t f", f=F),
                                            x1b[:, 4 * q:4 * q + 4, :], ALU.add).then_inc(x2_done, 1)
                dve.wait_ge(x2_done, CH * (b + 1))
                for t in range(T):
                    last = nc.vector.bn_stats(st[:, t, :], x2[:, t, :])
                last.then_inc(chain, 1)
                dve.wait_ge(chain, b * CHAIN + 1)
                norm_stats(nc, dve, st, tmp, chain, b * CHAIN + 1)

            def shifts(b):
                norm_shift(nc, dve, tmp, rstd[:], shift[:], chain, rooted, b + 1)

            def second(b, part):
                if part == 0:
                    dve.wait_ge(g_stored, 16 * b)
                    dve.wait_ge(own_stored, 16 * b)
                for q in range(part * PAIRS // 2, (part + 1) * PAIRS // 2):
                    tiles = slice(2 * q, 2 * q + 2)
                    dve.wait_ge(hi_done, PAIRS * b + q + 1)
                    nc.vector.tensor_tensor(g[:, tiles, 1, :], g_ps[:, q % 2, :, 0:F], g[:, tiles, 0, :], ALU.subtract).then_inc(lo_done, 1)
                    nc.vector.tensor_tensor(own[:, tiles, :], g_ps[:, q % 2, :, F:2 * F], bias[:, tiles, :], ALU.add).then_inc(own_done, 1)

            dve.sem_inc(divided, 2)
            dve.wait_ge(sums_loaded, 16)
            nc.vector.reciprocal(all_sums[:], all_sums[:]).then_inc(rz_done, 1)
            dve.wait_ge(weights_in, 16 * 6)
            for t in range(T):
                last = nc.vector.scalar_tensor_tensor(out=bias[:, t, :], in0=bn[:], scalar=keep["has_deg"][:, t:t + 1], in1=bs[:],
                                                      op0=ALU.mult, op1=ALU.add)
            last.then_inc(bias_ready, 1)
            dve.wait_ge(bias_ready, 1)
            divide(0)
            first(0)
            shifts(0)
            with dve.Fori(0, B - 1) as b:
                divide(b + 1)
                first(b + 1)
                second(b, 0)
                shifts(b + 1)
                second(b, 1)
            second(B - 1, 0)
            second(B - 1, 1)

        @block.scalar
        def _(act):
            def first(b):
                act.wait_ge(chain, (b + 1) * CHAIN)
                act.wait_ge(turned, CH * b)
                for t in range(T):
                    last = nc.scalar.activation(hn[:, t, :], x2[:, t, :], ACT.Relu, bias=shift[:, t:t + 1], scale=rstd[:, t:t + 1])
                last.then_inc(normed, 1)

            def second(b):
                act.wait_ge(g_stored, 16 * b)
                for q in range(CH):
                    act.wait_ge(turned, CH * b + q + 1)
                    nc.scalar.copy(hT[:, q * BANK:(q + 1) * BANK], tp_ps[:, q % 2, :]).then_inc(hT_kept, 1)
                    for r in (2 * q, 2 * q + 1):
                        act.wait_ge(g_done, PAIRS * b + r + 1)
                        nc.scalar.copy(g[:, 2 * r:2 * r + 2, 0, :], g_ps[:, r % 2, :, 0:F]).then_inc(hi_done, 1)

            act.sem_inc(hT_kept, 2)
            first(0)
            with act.Fori(0, B - 1) as b:
                second(b)
                first(b + 1)
            second(B - 1)

        @block.tensor
        def _(pe):
            def divide(b):
                pe.wait_ge(heads_loaded, 32 * (b + 1))
                for q in range(CH):
                    pe.wait_ge(divided, CH * b + q + 1)
                    nc.tensor.matmul(rep_ps[:, q % 2, :], sel[:].rearrange("k h d -> k (h d)"), rz[:, q * BANK:(q + 1) * BANK],
                                     start=True, stop=True).then_inc(spread, 1)

            def first(b):
                for q in range(CH):
                    pe.wait_ge(divided, CH * b + q + 3)
                    pe.wait_ge(x2_done, CH * b + max(q - 1, 0))
                    for t in range(4 * q, 4 * q + 4):
                        mm = nc.tensor.matmul(y_ps[:, q % 2, (t % 4) * P:(t % 4 + 1) * P], ot[:, t * P:(t + 1) * P], wo[:],
                                              start=True, stop=True)
                    mm.then_inc(y_done, 1)

            def second(b):
                pe.wait_ge(normed, b + 1)
                for q in range(CH):
                    pe.wait_ge(hT_kept, CH * b + q + 1)
                    for t in range(4 * q, 4 * q + 4):
                        mm = nc.tensor.transpose(tp_ps[:, q % 2, (t % 4) * P:(t % 4 + 1) * P], hn[:, t, :], keep["ident"][:])
                    mm.then_inc(turned, 1)
                    pe.wait_ge(hT_kept, CH * b + q + 3)
                    for r in (2 * q, 2 * q + 1):
                        pe.wait_ge(own_done, PAIRS * b + max(r - 1, 0))
                        for t in (2 * r, 2 * r + 1):
                            mm = nc.tensor.matmul(g_ps[:, r % 2, t % 2, :], hT[:, t * P:(t + 1) * P], wns[:], start=True, stop=True)
                        mm.then_inc(g_done, 1)

            pe.wait_ge(weights_in, 16 * 6)
            pe.wait_ge(consts_ready, 2)
            divide(0)
            first(0)
            with pe.Fori(0, B - 1) as b:
                divide(b + 1)
                first(b + 1)
                second(b)
            second(B - 1)


def neighbours(nc, io, keep):
    SLOTS = 4
    with ExitStack() as stack:
        s = Scope(nc, stack, "p3")
        g = s.sb("g", [P, 2, T, 2 * F], F16)
        own = s.sb("own", [P, 2, T, F])
        x2 = s.sb("x2", [P, 2, T, F])
        part = s.sb("part", [P, T, F])
        x3 = s.sb("x3", [P, T, F])
        hn = s.sb("hn", [P, T, F])
        hT = s.sb("hT", [P, N])
        h = s.sb("h", [P, T, F + 1])
        w = s.sb("w", [P, F + 2])
        w_rows = s.sb("w_rows", [P, F])
        a_cols = s.sb("a_cols", [P, 2])
        st = s.sb("st", [P, T, 6])
        tmp = s.sb("tmp", [P, 4, T])
        rstd, shift, minus_half = s.sb("rstd", [P, T]), s.sb("shift", [P, T]), s.sb("minus_half", [P, T])
        dots = s.sb("dots", [P, T, 2])
        sum_ps = s.ps("sum_ps", [P, SLOTS, BANK])
        tp_ps = s.ps("tp_ps", [P, 2, BANK])
        h_ps = s.ps("h_ps", [P, 2, BANK])
        THREES = [range(t, min(t + 3, T)) for t in range(0, T, 3)]
        TH = len(THREES)
        weights_in, consts_ready, wa_done, w_ready = s.sem("weights_in"), s.sem("consts_ready"), s.sem("wa_done"), s.sem("w_ready")
        g_loaded, own_loaded, x2_loaded = s.sem("g_loaded"), s.sem("own_loaded"), s.sem("x2_loaded")
        summed, part_done, used, x3_done, x3_stored = (s.sem("summed"), s.sem("part_done"), s.sem("used"), s.sem("x3_done"),
                                                       s.sem("x3_stored"))
        chain, rooted, normed, turned, hT_kept = s.sem("chain"), s.sem("rooted"), s.sem("normed"), s.sem("turned"), s.sem("hT_kept")
        h_done, h_kept, dots_kept, h_stored = s.sem("h_done"), s.sem("h_kept"), s.sem("dots_kept"), s.sem("h_stored")
        block = s.block()
        CHAIN = NORM_STEPS + 1

        def of(buf, b):
            return buf[:, bass.ds(b % 2, 1)]

        @block.sync
        def _(sp):
            sp.dma_start(w[:, 0:F], io["L3_gnn_W_t"][:]).then_inc(weights_in, 16)
            sp.dma_start(w_rows[:], io["L3_gnn_W"][:]).then_inc(weights_in, 16)
            sp.dma_start(a_cols[:], io["L3_gnn_a"][:]).then_inc(weights_in, 16)

            def load(b):
                sp.dma_start(of(g, b).rearrange("p one t f -> p (one t f)"),
                             io["g"][bass.ds(b, 1)].rearrange("one p n -> p (one n)")).then_inc(g_loaded, 16)
                sp.dma_start(of(own, b).rearrange("p one t f -> p (one t f)"),
                             io["own"][bass.ds(b, 1)].rearrange("one p n -> p (one n)")).then_inc(own_loaded, 16)
                sp.dma_start(of(x2, b).rearrange("p one t f -> p (one t f)"), node_tiles(io["x2"], b)).then_inc(x2_loaded, 16)

            def loaded(b):
                for sem in (g_loaded, own_loaded, x2_loaded):
                    sp.wait_ge(sem, 16 * (b + 1))

            load(0)
            loaded(0)
            load(1)
            with sp.Fori(0, B - 2) as b:
                loaded(b + 1)
                sp.wait_ge(summed, T * (b + 1))
                sp.wait_ge(x3_done, b + 1)
                load(b + 2)

        @block.gpsimd
        def _(pool):
            nc.gpsimd.memset(minus_half[:], -0.5).then_inc(consts_ready, 1)
            nc.gpsimd.memset(h[:, :, F:F + 1], 1.0).then_inc(consts_ready, 1)
            pool.wait_ge(consts_ready, 2)
            with pool.Fori(0, B) as b:
                norm_root(nc, pool, tmp, minus_half[:], rstd[:], chain, b * CHAIN + NORM_STEPS, rooted)
                pool.dma_start(node_tiles(io["x3"], b), flat(x3[:])).then_inc(x3_stored, 16)
                pool.wait_ge(h_kept, TH * (b + 1))
                pool.dma_start(io["h_nodes"][bass.ds(b, 1)].rearrange("one p t f -> p (one t) f"), h[:]).then_inc(h_stored, 16)
            pool.wait_ge(x3_stored, 16 * B)
            pool.wait_ge(h_stored, 16 * B)

        @block.vector
        def _(dve):
            def first(b):
                dve.wait_ge(own_loaded, 16 * (b + 1))
                for t in range(T):
                    dve.wait_ge(summed, T * b + t + 1)
                    nc.vector.scalar_tensor_tensor(out=part[:, t, :], in0=sum_ps[:, t % SLOTS, 0:F], scalar=keep["rdeg"][:, t:t + 1],
                                                   in1=of(own, b)[:, 0, t, :], op0=ALU.mult, op1=ALU.add).then_inc(part_done, 1)
                    dve.wait_ge(part_done, T * b + t + 1)
                    nc.vector.scalar_tensor_tensor(out=part[:, t, :], in0=sum_ps[:, t % SLOTS, F:2 * F], scalar=keep["rdeg"][:, t:t + 1],
                                                   in1=part[:, t, :], op0=ALU.mult, op1=ALU.add).then_inc(used, 1)
                dve.wait_ge(used, T * (b + 1) + SLOTS)
                dve.wait_ge(x2_loaded, 16 * (b + 1))
                dve.wait_ge(x3_stored, 16 * b)
                dve.wait_ge(normed, b)
                nc.vector.scalar_tensor_tensor(out=x3[:], in0=part[:], scalar=0.0, in1=of(x2, b)[:, 0], op0=ALU.max,
                                               op1=ALU.add).then_inc(x3_done, 1)

            def stats(b):
                dve.wait_ge(x3_done, b + 1)
                for t in range(T):
                    last = nc.vector.bn_stats(st[:, t, :], x3[:, t, :])
                last.then_inc(chain, 1)
                dve.wait_ge(chain, b * CHAIN + 1)
                norm_stats(nc, dve, st, tmp, chain, b * CHAIN + 1)
                norm_shift(nc, dve, tmp, rstd[:], shift[:], chain, rooted, b + 1)

            def scores(b):
                for n, tiles in enumerate(THREES):
                    dve.wait_ge(h_kept, TH * b + n + 1)
                    m = len(tiles)
                    nc.vector.tensor_copy(dots[:, tiles[0]:tiles[0] + m, :],
                                          h_ps[:, n % 2, 0:m * (F + 2)].rearrange("p (t f) -> p t f", f=F + 2)[:, :, F:F + 2]).then_inc(dots_kept, 1)
                dve.wait_ge(dots_kept, TH * (b + 1))
                for k, m in enumerate(("s1", "s2")):
                    nc.vector.tensor_copy(keep[m][:, bass.ds(b, 1), :], dots[:, :, k:k + 1].rearrange("p t one -> p one t"))

            dve.sem_inc(used, SLOTS)
            dve.wait_ge(wa_done, 1)
            nc.vector.tensor_copy(w[:, F:F + 2], h_ps[:, 0, 0:2]).then_inc(w_ready, 1)
            first(0)
            with dve.Fori(0, B - 1) as b:
                stats(b)
                first(b + 1)
                scores(b)
            stats(B - 1)
            scores(B - 1)

        @block.scalar
        def _(act):
            act.sem_inc(hT_kept, 2)
            with act.Fori(0, B) as b:
                act.wait_ge(chain, (b + 1) * CHAIN)
                act.wait_ge(turned, CH * b)
                for t in range(T):
                    last = nc.scalar.activation(hn[:, t, :], x3[:, t, :], ACT.Relu, bias=shift[:, t:t + 1], scale=rstd[:, t:t + 1])
                last.then_inc(normed, 1)
                for q in range(CH):
                    act.wait_ge(turned, CH * b + q + 1)
                    nc.scalar.copy(hT[:, q * BANK:(q + 1) * BANK], tp_ps[:, q % 2, :]).then_inc(hT_kept, 1)
                act.wait_ge(h_stored, 16 * b)
                act.wait_ge(consts_ready, 2)
                for n, tiles in enumerate(THREES):
                    act.wait_ge(h_done, TH * b + n + 1)
                    m = len(tiles)
                    nc.scalar.copy(h[:, tiles[0]:tiles[0] + m, 0:F],
                                   h_ps[:, n % 2, 0:m * (F + 2)].rearrange("p (t f) -> p t f", f=F + 2)[:, :, 0:F]).then_inc(h_kept, 1)

        @block.tensor
        def _(pe):
            def first(b):
                pe.wait_ge(g_loaded, 16 * (b + 1))
                for it in range(T):
                    pe.wait_ge(used, T * b + it + 1)
                    for jt in range(T):
                        mm = nc.tensor.matmul(sum_ps[:, it % SLOTS, 0:2 * F], keep["mask_t"][:, jt, it * P:(it + 1) * P],
                                              of(g, b)[:, 0, jt, :], start=(jt == 0), stop=(jt == T - 1))
                    mm.then_inc(summed, 1)

            def second(b):
                pe.wait_ge(normed, b + 1)
                for q in range(CH):
                    pe.wait_ge(hT_kept, CH * b + q + 1)
                    for t in range(4 * q, 4 * q + 4):
                        mm = nc.tensor.transpose(tp_ps[:, q % 2, (t % 4) * P:(t % 4 + 1) * P], hn[:, t, :], keep["ident"][:])
                    mm.then_inc(turned, 1)
                pe.wait_ge(hT_kept, CH * (b + 1) + 2)
                for n, tiles in enumerate(THREES):
                    pe.wait_ge(h_kept, TH * b + max(n - 1, 0))
                    pe.wait_ge(dots_kept, TH * b + max(n - 1, 0))
                    for k, t in enumerate(tiles):
                        mm = nc.tensor.matmul(h_ps[:, n % 2, k * (F + 2):(k + 1) * (F + 2)], hT[:, t * P:(t + 1) * P], w[:],
                                              start=True, stop=True)
                    mm.then_inc(h_done, 1)

            pe.wait_ge(weights_in, 16 * 3)
            nc.tensor.matmul(h_ps[:, 0, 0:2], w_rows[:], a_cols[:], start=True, stop=True).then_inc(wa_done, 1)
            first(0)
            pe.wait_ge(w_ready, 1)
            with pe.Fori(0, B - 1) as b:
                first(b + 1)
                second(b)
            second(B - 1)


_SHAPES = {"h_nodes": ((B, P, T, F + 1), F32), "mask_bias": ((N, N), BF16), "u_rows": ((B, N), F32), "v_rows": ((B, N), F32),
           "x1": ((B, N, F), F32),
           "q_hi": ((B, P, N), F16), "q_lo": ((B, P, N), F16), "k_hi": ((B, P, N), F16), "k_lo": ((B, P, N), F16),
           "v": ((B, 2, P, T * 2 * (HD + 1)), F32), "x2": ((B, N, F), F32), "x3": ((B, N, F), F32), "g": ((B, P, T * 2 * F), F16), "own": ((B, P, T * F), F32),
           "shifts": ((2 * T, P), F16), "heads_t": ((B, P, N), F32), "sums": ((B, HEADS, N), F32)}
PHASES = [
    masks_and_nodes0,
    lambda nc, io, keep: row_shifts(nc, io, keep, "l0", True),
    lambda nc, io, keep: gat_attention(nc, io, keep, "g0", io["x"], io["x1"], True),
    nodes1,
    head_attention,
    nodes2,
    neighbours,
    lambda nc, io, keep: row_shifts(nc, io, keep, "l3", False),
    lambda nc, io, keep: gat_attention(nc, io, keep, "g3", io["x3"], io["out"], False),
]

CLEAR_BEFORE = (5,)


def build(nc, io, upto=99):
    for name, (shape, dtype) in _SHAPES.items():
        io[name] = nc.dram_tensor(name, shape, dtype, kind="Internal").ap()
    with ExitStack() as stack:
        s = Scope(nc, stack, "keep")
        keep = {"mask_t": s.sb("mask_t", [P, T, N], BF16), "ident": s.sb("ident", [P, P]),
                "ident16": s.sb("ident16", [P, P], BF16)}
        for name in ("s1", "s2", "u", "v", "s2_08", "s2_02"):
            keep[name] = s.sb(name, [P, B, T])
        keep["rdeg"], keep["has_deg"] = s.sb("rdeg", [P, T]), s.sb("has_deg", [P, T])
        Scope.used_sems.clear()
        for k, phase in enumerate(PHASES[:upto]):
            if k in CLEAR_BEFORE:
                clear_semaphores(nc)
            phase(nc, io, keep)


def kernel(**inputs):
    import numpy as _np
    import concourse.bacc as _bacc
    from concourse import mybir as _mybir
    from concourse.bass_utils import run_bass_kernel_spmd as _run

    laid = {name: _np.asarray(a) for name, a in inputs.items()}
    for name in ("L0_gnn_ln_gamma", "L0_gnn_ln_beta", "L1_gnn_b_o", "L2_gnn_b_self", "L2_gnn_b_neigh"):
        laid[name] = laid[name].reshape(1, F)
    for name in ("L0_gnn_node_weights", "L0_gnn_node_bias"):
        laid[name] = laid[name].reshape(P, T)
    laid["L0_gnn_a"] = laid["L0_gnn_a"].reshape(2, F)
    laid["L3_gnn_a"] = laid["L3_gnn_a"].reshape(2, F).T
    laid["L3_gnn_W_t"] = laid["L3_gnn_W"].T
    nc = _bacc.Bacc("TRN2", target_bir_lowering=False, num_devices=1)
    arrays, io = {}, {}
    for name, a in laid.items():
        arrays[f"in_{name}"] = a = _np.ascontiguousarray(a)
        io[name] = nc.dram_tensor(f"in_{name}", a.shape, _mybir.dt.from_np(a.dtype), kind="ExternalInput").ap()
    io["out"] = nc.dram_tensor("out_0", (B, N, F), F32, kind="ExternalOutput").ap()
    build(nc, io)
    r = _run(nc, [arrays], core_ids=[0])
    return r.results[0]["out_0"]
```

```python
from contextlib import ExitStack

import concourse.bass as bass
from concourse import mybir

ALU = mybir.AluOpType
ACT = mybir.ActivationFunctionType
AX = mybir.AxisListType
F32 = mybir.dt.float32
F16 = mybir.dt.float16
BF16 = mybir.dt.bfloat16
I32 = mybir.dt.int32

P = 128
B = 8
N = 2048
F = 128
T = N // P
HEADS = 4
HD = F // HEADS
BANK = 512
CH = N // BANK
LN_EPS = 1e-5
SLOPE = 0.2
LEVELS = 32
MASKED = 1.0e30
SHIFT_UNIT = 1024.0


class Scope:

    used_sems = []

    def __init__(self, nc, stack, name):
        self.nc, self.stack, self.name = nc, stack, name

    def sb(self, name, shape, dtype=F32):
        return self.stack.enter_context(self.nc.sbuf_tensor(f"{self.name}_{name}", shape, dtype))

    def ps(self, name, shape, dtype=F32):
        return self.stack.enter_context(self.nc.psum_tensor(f"{self.name}_{name}", shape, dtype))

    def sem(self, name):
        sem = self.nc.alloc_semaphore(name=f"{self.name}_{name}")
        self.used_sems.append(sem)
        return sem

    def block(self):
        return self.stack.enter_context(self.nc.Block())


def clear_semaphores(nc):
    nc.clear_and_free_semaphores(list(Scope.used_sems))
    Scope.used_sems.clear()
    nc.all_engine_barrier()


def node_tiles(dram, b):
    return dram[bass.ds(b, 1)].rearrange("one (p t) f -> p (one t f)", p=P)


def flat(buf):
    return buf.rearrange("p t f -> p (t f)")


def norm_stats(nc, dve, st, tmp, done, base):
    mean2, diff, ssq, var = (tmp[:, k, :] for k in range(4))
    nc.vector.tensor_tensor(mean2, st[:, :, 1], st[:, :, 4], ALU.add).then_inc(done, 1)
    nc.vector.tensor_tensor(diff, st[:, :, 1], st[:, :, 4], ALU.subtract).then_inc(done, 1)
    nc.vector.tensor_tensor(ssq, st[:, :, 2], st[:, :, 5], ALU.add).then_inc(done, 1)
    dve.wait_ge(done, base + 2)
    nc.vector.scalar_tensor_tensor(out=diff, in0=diff, scalar=0.25, in1=diff,
                                   op0=ALU.mult, op1=ALU.mult).then_inc(done, 1)
    dve.wait_ge(done, base + 3)
    nc.vector.tensor_scalar(ssq, ssq, 1.0 / F, LN_EPS, ALU.mult, ALU.add).then_inc(done, 1)
    dve.wait_ge(done, base + 5)
    nc.vector.tensor_tensor(var, ssq, diff, ALU.add).then_inc(done, 1)


def norm_shift(nc, dve, tmp, rstd, shift, done, rooted, roots):
    dve.wait_ge(rooted, roots)
    nc.vector.scalar_tensor_tensor(out=shift, in0=tmp[:, 0, :], scalar=-0.5, in1=rstd,
                                   op0=ALU.mult, op1=ALU.mult).then_inc(done, 1)


def norm_root(nc, pool, tmp, minus_half, rstd, done, value, rooted):
    pool.wait_ge(done, value)
    nc.gpsimd.tensor_tensor(rstd, tmp[:, 3, :], minus_half, ALU.pow).then_inc(rooted, 1)


NORM_STEPS = 7


def masks_and_nodes0(nc, io, keep):
    with ExitStack() as stack:
        s = Scope(nc, stack, "p0")
        adj_in = s.sb("adj_in", [P, 2, N], I32)
        m01 = s.sb("m01", [P, 2, N], BF16)
        mbias = s.sb("mbias", [P, 2, N], BF16)
        x = s.sb("x", [P, T, F])
        hn = s.sb("hn", [P, T, F])
        hT = s.sb("hT", [P, N])
        h0 = s.sb("h0", [P, T, F])
        h1 = s.sb("h1", [P, T, F])
        h = s.sb("h", [P, T, F + 1])
        w = s.sb("w", [P, F])
        gamma = s.sb("gamma", [P, F])
        beta = s.sb("beta", [P, F])
        a12 = s.sb("a12", [P, 2, F])
        nw = s.sb("nw", [P, T])
        nw1 = s.sb("nw1", [P, T])
        nb = s.sb("nb", [P, T])
        st_x, st_h = s.sb("st_x", [P, T, 6]), s.sb("st_h", [P, T, 6])
        tmp_x, tmp_h = s.sb("tmp_x", [P, 4, T]), s.sb("tmp_h", [P, 4, T])
        rstd_x, shift_x = s.sb("rstd_x", [P, T]), s.sb("shift_x", [P, T])
        rstd_h, shift_h = s.sb("rstd_h", [P, T]), s.sb("shift_h", [P, T])
        dots = s.sb("dots", [P, 2, T])
        products = s.sb("products", [P, T, F])
        minus_half = s.sb("minus_half", [P, T])
        mt_ps = s.ps("mt_ps", [P, 2, T, P], BF16)
        tp_ps = s.ps("tp_ps", [P, 2, BANK])
        pj_ps = s.ps("pj_ps", [P, 2, BANK])

        weights_in, ident_zero, ident_ready = s.sem("weights_in"), s.sem("ident_zero"), s.sem("ident_ready")
        adj_loaded, x_loaded = [s.sem(f"adj_loaded{k}") for k in range(2)], s.sem("x_loaded")
        m01_ready, mbias_ready = s.sem("m01_ready"), s.sem("mbias_ready")
        mbias_stored = [s.sem(f"mbias_stored{k}") for k in range(2)]
        mt_turned, mt_kept = s.sem("mt_turned"), s.sem("mt_kept")
        nw1_ready = s.sem("nw1_ready")
        chain_x, rooted_x, chain_h, rooted_h = s.sem("chain_x"), s.sem("rooted_x"), s.sem("chain_h"), s.sem("rooted_h")
        x_normed, x_scaled, h_turned, hT_kept = s.sem("x_normed"), s.sem("x_scaled"), s.sem("h_turned"), s.sem("hT_kept")
        projected, h0_kept, h0_normed = s.sem("projected"), s.sem("h0_kept"), s.sem("h0_normed")
        gamma_done, h_ready, dots_done, h_stored = s.sem("gamma_done"), s.sem("h_ready"), s.sem("dots_done"), s.sem("h_stored")
        scores_kept = s.sem("scores_kept")
        block = s.block()
        CHAIN = NORM_STEPS + 1

        @block.sync
        def _(sp):
            def load_x(b):
                sp.dma_start(flat(x[:]), node_tiles(io["x"], b)).then_inc(x_loaded, 16)

            def load_adj(b, k):
                rows = io["adj"].rearrange("(p t) j -> p t j", t=T)[:, bass.ds(2 * b + k, 1), :]
                sp.dma_start(adj_in[:, k, :], rows.rearrange("p one j -> p (one j)")).then_inc(adj_loaded[k], 16)

            def store_mbias(b):
                for k in range(2):
                    sp.wait_ge(mbias_ready, 2 * b + k + 1)
                    sp.dma_start(io["mask_bias"][bass.ds((2 * b + k) * P, P), :], mbias[:, k, :]).then_inc(mbias_stored[k], 16)

            def store_h(b):
                sp.wait_ge(h_ready, b + 1)
                sp.dma_start(io["h_nodes"][bass.ds(b, 1)].rearrange("one p t f -> p (one t f)"), flat(h[:])).then_inc(h_stored, 16)

            load_x(0)
            load_adj(0, 0)
            load_adj(0, 1)
            sp.dma_start(w[:], io["L0_gnn_W"][:]).then_inc(weights_in, 16)
            sp.dma_start(gamma[:], io["L0_gnn_ln_gamma"][0:1, :].partition_broadcast(P)).then_inc(weights_in, 16)
            sp.dma_start(beta[:], io["L0_gnn_ln_beta"][0:1, :].partition_broadcast(P)).then_inc(weights_in, 16)
            for k in range(2):
                sp.dma_start(a12[:, k, :], io["L0_gnn_a"][k:k + 1, :].partition_broadcast(P)).then_inc(weights_in, 16)
            sp.dma_start(nw[:], io["L0_gnn_node_weights"][:]).then_inc(weights_in, 16)
            sp.dma_start(nb[:], io["L0_gnn_node_bias"][:]).then_inc(weights_in, 16)

            def following(b):
                sp.wait_ge(x_normed, b + 1)
                load_x(b + 1)
                for k in range(2):
                    sp.wait_ge(m01_ready, 2 * b + k + 1)
                    load_adj(b + 1, k)
                store_mbias(b)

            following(0)
            with sp.Fori(0, B - 2) as j:
                following(j + 1)
                store_h(j)
            store_mbias(B - 1)
            store_h(B - 2)
            store_h(B - 1)
            for k in range(2):
                sp.wait_ge(mbias_stored[k], 16 * B)
            sp.wait_ge(h_stored, 16 * B)

        @block.gpsimd
        def _(pool):
            def root_x(b):
                norm_root(nc, pool, tmp_x, minus_half[:], rstd_x[:], chain_x, b * CHAIN + NORM_STEPS, rooted_x)

            def root_h(b):
                norm_root(nc, pool, tmp_h, minus_half[:], rstd_h[:], chain_h, b * CHAIN + NORM_STEPS, rooted_h)

            def affine(b):
                pool.wait_ge(h0_normed, b + 1)
                nc.gpsimd.tensor_tensor(h1[:], h1[:], gamma[:].unsqueeze(1).to_broadcast([P, T, F]), ALU.mult).then_inc(gamma_done, 1)
                pool.wait_ge(gamma_done, b + 1)
                pool.wait_ge(h_stored, 16 * b)
                pool.wait_ge(dots_done, 2 * b)
                nc.gpsimd.tensor_tensor(h[:, :, 0:F], h1[:], beta[:].unsqueeze(1).to_broadcast([P, T, F]),
                                        ALU.add).then_inc(h_ready, 1)

            nc.gpsimd.memset(minus_half[:], -0.5).then_inc(ident_zero, 1)
            nc.gpsimd.memset(keep["ident"][:], 0.0).then_inc(ident_zero, 1)
            nc.gpsimd.memset(keep["ident16"][:], 0.0).then_inc(ident_zero, 1)
            nc.gpsimd.memset(h[:, :, F:F + 1], 1.0).then_inc(ident_zero, 1)
            pool.wait_ge(ident_zero, 4)
            for m in (keep["ident"], keep["ident16"]):
                nc.gpsimd.affine_select(out=m[:], in_=m[:], compare_op=ALU.not_equal, fill=1.0, base=0,
                                        pattern=[[-1, P]], channel_multiplier=1).then_inc(ident_ready, 1)
            root_x(0)
            pool.wait_ge(weights_in, 16 * 7)
            root_x(1)
            root_h(0)
            affine(0)
            with pool.Fori(0, B - 2) as j:
                root_x(j + 2)
                root_h(j + 1)
                affine(j + 1)
            root_h(B - 1)
            affine(B - 1)

        @block.vector
        def _(dve):
            def masks(b):
                for k in range(2):
                    dve.wait_ge(adj_loaded[k], 16 * (b + 1))
                    dve.wait_ge(mt_turned, 2 * b + k + 1)
                    nc.vector.tensor_scalar(m01[:, k, :].rearrange("p (t q) -> p t q", q=P),
                                            adj_in[:, k, :].rearrange("p (q t) -> p t q", t=T), 0, None, ALU.is_gt).then_inc(m01_ready, 1)
                for k in range(2):
                    dve.wait_ge(m01_ready, 2 * b + k + 1)
                    dve.wait_ge(mbias_stored[k], 16 * b)
                    nc.vector.tensor_scalar(mbias[:, k, :], m01[:, k, :], MASKED, -MASKED,
                                            ALU.mult, ALU.add).then_inc(mbias_ready, 1)

            def stats_x(b):
                dve.wait_ge(x_loaded, 16 * (b + 1))
                for t in range(T):
                    last = nc.vector.bn_stats(st_x[:, t, :], x[:, t, :])
                last.then_inc(chain_x, 1)
                dve.wait_ge(chain_x, b * CHAIN + 1)
                norm_stats(nc, dve, st_x, tmp_x, chain_x, b * CHAIN + 1)

            def shift_of_x(b):
                norm_shift(nc, dve, tmp_x, rstd_x[:], shift_x[:], chain_x, rooted_x, b + 1)

            def scale_x(b):
                dve.wait_ge(x_normed, b + 1)
                for t in range(T):
                    ins = nc.vector.tensor_scalar(hn[:, t, :], hn[:, t, :], nw1[:, t:t + 1], nb[:, t:t + 1], ALU.mult, ALU.add)
                    if t % 4 == 3:
                        ins.then_inc(x_scaled, 1)

            def stats_h(b):
                dve.wait_ge(h0_kept, CH * (b + 1) + 2)
                for t in range(T):
                    last = nc.vector.bn_stats(st_h[:, t, :], h0[:, t, :])
                last.then_inc(chain_h, 1)
                dve.wait_ge(chain_h, b * CHAIN + 1)
                norm_stats(nc, dve, st_h, tmp_h, chain_h, b * CHAIN + 1)

            def norm_h(b):
                norm_shift(nc, dve, tmp_h, rstd_h[:], shift_h[:], chain_h, rooted_h, b + 1)
                dve.wait_ge(chain_h, (b + 1) * CHAIN)
                dve.wait_ge(h_ready, b)
                for t in range(T):
                    last = nc.vector.tensor_scalar(h1[:, t, :], h0[:, t, :], rstd_h[:, t:t + 1], shift_h[:, t:t + 1], ALU.mult, ALU.add)
                last.then_inc(h0_normed, 1)

            def scores(b):
                dve.wait_ge(h_ready, b + 1)
                dve.wait_ge(scores_kept, 2 * b)
                for k in range(2):
                    for t in range(T):
                        last = nc.vector.tensor_tensor_reduce(
                            out=products[:, t, :], in0=h[:, t, 0:F], in1=a12[:, k, :], scale=1.0, scalar=0.0,
                            op0=ALU.mult, op1=ALU.add, accum_out=dots[:, k, t:t + 1])
                    last.then_inc(dots_done, 1)
                    dve.wait_ge(dots_done, 2 * b + k + 1)
                nc.vector.tensor_copy(keep["s1"][:, bass.ds(b, 1), :], dots[:, 0:1, :]).then_inc(scores_kept, 1)
                nc.vector.tensor_copy(keep["s2"][:, bass.ds(b, 1), :], dots[:, 1:2, :]).then_inc(scores_kept, 1)

            stats_x(0)
            masks(0)
            shift_of_x(0)
            dve.wait_ge(weights_in, 16 * 7)
            nc.vector.tensor_scalar(nw1[:], nw[:], 1.0, None, ALU.add).then_inc(nw1_ready, 1)
            dve.wait_ge(nw1_ready, 1)
            scale_x(0)
            stats_x(1)
            masks(1)
            shift_of_x(1)
            stats_h(0)
            norm_h(0)
            scale_x(1)
            with dve.Fori(0, B - 2) as j:
                stats_x(j + 2)
                masks(j + 2)
                shift_of_x(j + 2)
                stats_h(j + 1)
                scores(j)
                norm_h(j + 1)
                scale_x(j + 2)
            stats_h(B - 1)
            scores(B - 2)
            norm_h(B - 1)
            scores(B - 1)

        @block.scalar
        def _(act):
            def keep_masks(b):
                for k in range(2):
                    act.wait_ge(mt_turned, 2 * b + k + 3)
                    nc.scalar.activation(keep["mask_t"][:, :, bass.ds((2 * b + k) * P, P)], mt_ps[:, k], ACT.Copy).then_inc(mt_kept, 1)

            def norm_x(b):
                act.wait_ge(chain_x, (b + 1) * CHAIN)
                act.wait_ge(h_turned, CH * b)
                for t in range(T):
                    last = nc.scalar.activation(hn[:, t, :], x[:, t, :], ACT.Relu, bias=shift_x[:, t:t + 1],
                                                scale=rstd_x[:, t:t + 1])
                last.then_inc(x_normed, 1)

            def keep_hT(b, q):
                act.wait_ge(h_turned, CH * b + q + 1)
                nc.scalar.copy(hT[:, q * BANK:(q + 1) * BANK], tp_ps[:, q % 2, :]).then_inc(hT_kept, 1)

            def keep_h0(b):
                act.wait_ge(h0_normed, b)
                keep_hT(b, 0)
                for q in range(CH):
                    if q + 1 < CH:
                        keep_hT(b, q + 1)
                    act.wait_ge(projected, CH * b + q + 1)
                    nc.scalar.copy(h0[:, 4 * q:4 * q + 4, :],
                                   pj_ps[:, q % 2, :].rearrange("p (t f) -> p t f", f=F)).then_inc(h0_kept, 1)

            act.sem_inc(mt_kept, 2)
            act.sem_inc(hT_kept, 2)
            act.sem_inc(h0_kept, 2)
            norm_x(0)
            keep_masks(0)
            with act.Fori(0, B - 1) as j:
                keep_h0(j)
                norm_x(j + 1)
                keep_masks(j + 1)
            keep_h0(B - 1)

        @block.tensor
        def _(pe):
            def turn_masks(b):
                for k in range(2):
                    pe.wait_ge(m01_ready, 2 * b + k + 1)
                    pe.wait_ge(mt_kept, 2 * b + k + 1)
                    for t in range(T):
                        mm = nc.tensor.transpose(mt_ps[:, k, t, :], m01[:, k, t * P:(t + 1) * P], keep["ident16"][:])
                    mm.then_inc(mt_turned, 1)

            def turn_nodes(b, q):
                pe.wait_ge(x_scaled, CH * b + q + 1)
                pe.wait_ge(hT_kept, CH * b + q + 1)
                for t in range(4 * q, 4 * q + 4):
                    mm = nc.tensor.transpose(tp_ps[:, q % 2, (t % 4) * P:(t % 4 + 1) * P], hn[:, t, :], keep["ident"][:])
                mm.then_inc(h_turned, 1)

            def project(b):
                turn_nodes(b, 0)
                for q in range(CH):
                    if q + 1 < CH:
                        turn_nodes(b, q + 1)
                    pe.wait_ge(hT_kept, CH * b + q + 3)
                    pe.wait_ge(h0_kept, CH * b + q + 1)
                    for t in range(4 * q, 4 * q + 4):
                        mm = nc.tensor.matmul(pj_ps[:, q % 2, (t % 4) * P:(t % 4 + 1) * P], hT[:, t * P:(t + 1) * P],
                                              w[:], start=True, stop=True)
                    mm.then_inc(projected, 1)

            pe.sem_inc(mt_turned, 2)
            pe.wait_ge(ident_ready, 2)
            pe.wait_ge(weights_in, 16 * 7)
            turn_masks(0)
            with pe.Fori(0, B - 1) as j:
                project(j)
                turn_masks(j + 1)
            project(B - 1)

def row_shifts(nc, io, keep, name, first):
    with ExitStack() as stack:
        s = Scope(nc, stack, name)
        ext = s.sb("ext", [P, 2 * B])
        ext_col = s.sb("ext_col", [2 * B, 1])
        ext_diag = s.sb("ext_diag", [2 * B, 2 * B])
        ones = s.sb("ones", [2 * B, P])
        ext_all = s.sb("ext_all", [P, 2 * B])
        step = s.sb("step", [P, B])
        lev_i = s.sb("lev_i", [P, LEVELS], I32)
        lev = s.sb("lev", [P, LEVELS])
        rank = s.sb("rank", [P, B, LEVELS], BF16)
        tau = s.sb("tau", [P, B, LEVELS])
        above = s.sb("above", [P, T, B * LEVELS], BF16)
        hit = s.sb("hit", [P, 2, B * LEVELS], BF16)
        top = s.sb("top", [P, B, T])
        lk = s.sb("lk", [P, B, T])
        deg = s.sb("deg", [P, T])
        rows = s.sb("rows", [P, 2, P])
        ext_ps = s.ps("ext_ps", [2 * B, P])
        all_ps = s.ps("all_ps", [P, 2 * B])
        cnt_ps = s.ps("cnt_ps", [P, 4, BANK])
        rows_ps = s.ps("rows_ps", [P, 2, P])
        levels_in, step_done = s.sem("levels_in"), s.sem("step_done")
        ext_done, ext_turned, diag_done, spread = s.sem("ext_done"), s.sem("ext_turned"), s.sem("diag_done"), s.sem("spread")
        above_done, counted, hit_done, top_done = s.sem("above_done"), s.sem("counted"), s.sem("hit_done"), s.sem("top_done")
        shifts_done, rows_turned, rows_kept, rows_stored = (s.sem("shifts_done"), s.sem("rows_turned"), s.sem("rows_kept"),
                                                            s.sem("rows_stored"))
        block = s.block()
        s1, s2 = keep["s1"], keep["s2"]

        @block.gpsimd
        def _(pool):
            nc.gpsimd.memset(ones[:], 1.0).then_inc(levels_in, 1)
            nc.gpsimd.iota(lev_i[:], pattern=[[1, LEVELS]], base=0, channel_multiplier=0).then_inc(levels_in, 1)

        @block.vector
        def _(dve):
            nc.vector.tensor_reduce(ext[:, 0:B], s2[:], AX.X, ALU.max).then_inc(ext_done, 1)
            nc.vector.tensor_reduce(ext[:, B:2 * B], s2[:], AX.X, ALU.min, negate=True).then_inc(ext_done, 1)
            nc.vector.tensor_scalar(keep["s2_08"][:], s2[:], 1.0 - SLOPE, None, ALU.mult)
            nc.vector.tensor_scalar(keep["s2_02"][:], s2[:], SLOPE, None, ALU.mult)
            dve.wait_ge(levels_in, 2)
            nc.vector.tensor_copy(lev[:], lev_i[:]).then_inc(step_done, 1)
            dve.wait_ge(step_done, 1)
            nc.vector.tensor_scalar(rank[:], lev[:].unsqueeze(1).to_broadcast([P, B, LEVELS]), 1.0, None, ALU.add).then_inc(step_done, 1)
            dve.wait_ge(ext_turned, 1)
            nc.vector.tensor_reduce(ext_col[:], ext_ps[:], AX.X, ALU.max).then_inc(diag_done, 1)
            dve.wait_ge(diag_done, 1)
            nc.vector.tensor_scalar(ext_diag[:], keep["ident"][0:2 * B, 0:2 * B], ext_col[:, 0:1], None, ALU.mult).then_inc(diag_done, 1)
            dve.wait_ge(spread, 1)
            nc.vector.tensor_copy(ext_all[:], all_ps[:]).then_inc(step_done, 1)
            dve.wait_ge(step_done, 3)
            nc.vector.tensor_tensor(step[:], ext_all[:, 0:B], ext_all[:, B:2 * B], ALU.add).then_inc(step_done, 1)
            dve.wait_ge(step_done, 4)
            nc.vector.tensor_scalar(step[:], step[:], 1.0 / (LEVELS - 1), None, ALU.mult).then_inc(step_done, 1)
            dve.wait_ge(step_done, 5)
            for b in range(B):
                last = nc.vector.tensor_scalar(tau[:, b, :], lev[:], step[:, b:b + 1], ext_all[:, B + b:B + b + 1],
                                               ALU.mult, ALU.subtract)
            last.then_inc(step_done, 1)
            dve.wait_ge(step_done, 6)
            for t in range(T):
                nc.vector.tensor_tensor(above[:, t, :].rearrange("p (b l) -> p b l", l=LEVELS),
                                        s2[:, :, t:t + 1].to_broadcast([P, B, LEVELS]), tau[:], ALU.is_ge).then_inc(above_done, 1)
            for t in range(T):
                dve.wait_ge(counted, t + 1)
                if first:
                    nc.vector.tensor_copy(deg[:, t:t + 1], cnt_ps[:, t % 4, 0:1])
                if t >= 2:
                    dve.wait_ge(top_done, t - 1)
                nc.vector.scalar_tensor_tensor(out=hit[:, t % 2, :], in0=cnt_ps[:, t % 4, 0:B * LEVELS], scalar=0.0,
                                               in1=rank[:].rearrange("p b l -> p (b l)"), op0=ALU.is_gt, op1=ALU.mult).then_inc(hit_done, 1)
                dve.wait_ge(hit_done, t + 1)
                nc.vector.tensor_reduce(top[:, :, t], hit[:, t % 2, :].rearrange("p (b l) -> p b l", l=LEVELS),
                                        AX.X, ALU.max).then_inc(top_done, 1)
            by_batch = [P, B, T]
            dve.wait_ge(top_done, T)
            nc.vector.tensor_scalar(top[:], top[:], -1.0, None, ALU.add).then_inc(shifts_done, 1)
            dve.wait_ge(shifts_done, 1)
            nc.vector.tensor_tensor(top[:], top[:], step[:].unsqueeze(2).to_broadcast(by_batch), ALU.mult).then_inc(shifts_done, 1)
            dve.wait_ge(shifts_done, 2)
            nc.vector.tensor_tensor(top[:], top[:], ext_all[:, B:2 * B].unsqueeze(2).to_broadcast(by_batch),
                                    ALU.subtract).then_inc(shifts_done, 1)
            dve.wait_ge(shifts_done, 3)
            nc.vector.tensor_tensor(top[:], top[:], s1[:], ALU.add).then_inc(shifts_done, 1)
            dve.wait_ge(shifts_done, 4)
            nc.vector.scalar_tensor_tensor(out=lk[:], in0=top[:], scalar=SLOPE, in1=top[:], op0=ALU.mult, op1=ALU.max).then_inc(shifts_done, 1)
            dve.wait_ge(shifts_done, 5)
            nc.vector.tensor_tensor(keep["u"][:], s1[:], lk[:], ALU.subtract).then_inc(shifts_done, 1)
            nc.vector.scalar_tensor_tensor(out=keep["v"][:], in0=s1[:], scalar=SLOPE, in1=lk[:], op0=ALU.mult,
                                           op1=ALU.subtract).then_inc(shifts_done, 1)
            if first:
                nc.vector.tensor_scalar(keep["has_deg"][:], deg[:], 0.0, None, ALU.is_gt).then_inc(shifts_done, 1)
                nc.vector.tensor_scalar(deg[:], deg[:], 1.0, None, ALU.max).then_inc(shifts_done, 1)
                dve.wait_ge(shifts_done, 9)
                nc.vector.reciprocal(keep["rdeg"][:], deg[:]).then_inc(shifts_done, 1)
            dve.wait_ge(rows_turned, 1)
            nc.vector.tensor_copy(rows[:], rows_ps[:]).then_inc(rows_kept, 1)

        @block.tensor
        def _(pe):
            pe.wait_ge(ext_done, 2)
            nc.tensor.transpose(ext_ps[:], ext[:], keep["ident"][:]).then_inc(ext_turned, 1)
            pe.wait_ge(levels_in, 2)
            pe.wait_ge(diag_done, 2)
            nc.tensor.matmul(all_ps[:], ones[:], ext_diag[:], start=True, stop=True).then_inc(spread, 1)
            for it in range(T):
                if it >= 4:
                    pe.wait_ge(hit_done, it - 3)
                for jt in range(T):
                    if it == 0:
                        pe.wait_ge(above_done, jt + 1)
                    mm = nc.tensor.matmul(cnt_ps[:, it % 4, 0:B * LEVELS], keep["mask_t"][:, jt, it * P:(it + 1) * P], above[:, jt, :],
                                          start=(jt == 0), stop=(jt == T - 1))
                mm.then_inc(counted, 1)
            pe.wait_ge(shifts_done, 7)
            for k, m in enumerate(("u", "v")):
                mm = nc.tensor.transpose(rows_ps[:, k, :], keep[m][:].rearrange("p b t -> p (b t)"), keep["ident"][:])
            mm.then_inc(rows_turned, 1)

        @block.sync
        def _(sp):
            sp.wait_ge(rows_kept, 1)
            for k, m in enumerate(("u_rows", "v_rows")):
                sp.dma_start(io[m].rearrange("b (t p) -> (b t) p", p=P), rows[:, k, :]).then_inc(rows_stored, 16)
            sp.wait_ge(rows_stored, 32)


def gat_attention(nc, io, keep, name, x_in, x_out, residual_elu):
    HALF = N // 2
    IT = HALF // P
    STEPS = 4 * T
    ZB, PB = 4, 8
    mine = [g for g in range(STEPS) if g % T in (2, 5, 8)]
    FIN = (10, 12, 14)
    STAGES = 3 if residual_elu else 1
    with ExitStack() as stack:
        s = Scope(nc, stack, name)
        h = s.sb("h", [P, 2, T, F + 1])
        x = s.sb("x", [P, 2, T, F])
        urow = s.sb("urow", [P, 2, N])
        vrow = s.sb("vrow", [P, 2, N])
        s2_02 = s.sb("s2_02", [P, 2, T])
        z = s.sb("z", [P, ZB, HALF])
        w = s.sb("w", [P, PB, HALF])
        rz = s.sb("rz", [P, IT])
        y = s.sb("y", [P, IT, F])
        e = s.sb("e", [P, IT, F])
        o = s.sb("o", [P, IT, F])
        acc = s.ps("acc", [P, 2, 3, BANK])
        h_loaded, x_loaded = [s.sem(f"h_loaded{k}") for k in range(2)], [s.sem(f"x_loaded{k}") for k in range(2)]
        rows_loaded = [[s.sem(f"rows_loaded{k}{half}") for half in range(2)] for k in range(2)]
        z_ready, exp_done, masked_pool, masked_dve = s.sem("z_ready"), s.sem("exp_done"), s.sem("masked_pool"), s.sem("masked_dve")
        weighed, drained = s.sem("weighed"), s.sem("drained")
        rz_done, e_ready, o_ready, r_done = s.sem("rz_done"), s.sem("e_ready"), s.sem("o_ready"), s.sem("r_done")
        o_stored = [s.sem(f"o_stored{half}") for half in range(2)]
        block = s.block()

        def tile(half, it):
            return acc[:, half, it // 3, (it % 3) * (F + 1):(it % 3 + 1) * (F + 1)]

        def half_rows(dram, b, half):
            return node_tiles(dram, b)[:, half * IT * F:(half + 1) * IT * F]

        @block.sync
        def _(sp):
            def load(b, k):
                for half in range(2):
                    cols = slice(half * HALF, (half + 1) * HALF)
                    for rows, m in ((urow, "u_rows"), (vrow, "v_rows")):
                        sp.dma_start(rows[:, k, cols], io[m][bass.ds(b, 1), cols].partition_broadcast(P)).then_inc(rows_loaded[k][half], 16)
                sp.dma_start(h[:, k], io["h_nodes"][bass.ds(b, 1)].rearrange("one p t f -> p (one t) f")).then_inc(h_loaded[k], 16)
                sp.dma_start(flat(x[:, k]), node_tiles(x_in, b)).then_inc(x_loaded[k], 16)

            def store(b, half, n):
                if residual_elu:
                    sp.wait_ge(o_ready, n + 1)
                else:
                    sp.wait_ge(drained, n + 2)
                sp.dma_start(half_rows(x_out, b, half), flat(o[:])).then_inc(o_stored[half], 16)

            load(0, 0)
            load(1, 1)
            with sp.Fori(0, B // 2) as i:
                with sp.If(i > 0):
                    store(nc.s_assert_within(2 * i - 1, 0, B - 1, skip_runtime_bounds_check_because="only where i > 0"), 1, 4 * i)
                    load(2 * i + 1, 1)
                store(2 * i, 0, 4 * i + 1)
                store(2 * i, 1, 4 * i + 2)
                with sp.If(i < B // 2 - 1):
                    load(nc.s_assert_within(2 * i + 2, 0, B - 1, skip_runtime_bounds_check_because="only before the last i"), 0)
                store(2 * i + 1, 0, 4 * i + 3)
            store(B - 1, 1, 2 * B)
            for half in range(2):
                sp.wait_ge(o_stored[half], 16 * B)

        @block.vector
        def _(dve):
            def stored_before(half, stores):
                dve.wait_ge(o_stored[1 - half], 16 * stores)

            def finish(k, half, n, stores, loads):
                dve.wait_ge(weighed, T * (n + 1) + PB)
                dve.wait_ge(h_loaded[k], 16 * loads)
                dve.wait_ge(x_loaded[k], 16 * loads)
                sums = acc[:, half, :, 0:3 * (F + 1)].rearrange("p k (i f) -> p k i f", f=F + 1)[:, :, :, F]
                nc.vector.reciprocal(rz[:, 0:6].rearrange("p (k i) -> p k i", i=3), sums[:, 0:2, :])
                nc.vector.reciprocal(rz[:, 6:8], sums[:, 2, 0:2]).then_inc(rz_done, 1)
                dve.wait_ge(rz_done, n + 1)
                if not residual_elu:
                    stored_before(half, stores)
                for it in range(IT):
                    add = h[:, k, half * IT + it, 0:F] if residual_elu else x[:, k, half * IT + it, :]
                    last = nc.vector.scalar_tensor_tensor(out=(y if residual_elu else o)[:, it, :], in0=tile(half, it)[:, 0:F],
                                                          scalar=rz[:, it:it + 1], in1=add, op0=ALU.mult, op1=ALU.add)
                last.then_inc(drained, 1)

            def add_x(k, half, n, stores):
                dve.wait_ge(drained, n + 1 + 2)
                stored_before(half, stores)
                nc.vector.scalar_tensor_tensor(out=o[:], in0=y[:], scalar=0.0, in1=x[:, k, half * IT:(half + 1) * IT, :],
                                               op0=ALU.max, op1=ALU.add).then_inc(r_done, 1)

            def add_elu(n):
                dve.wait_ge(r_done, n + 1)
                dve.wait_ge(e_ready, 2 * n + 3)
                nc.vector.tensor_tensor(o[:], o[:], e[:], ALU.subtract).then_inc(o_ready, 1)

            def finish_stage(stage, k, half, n, stores, loads):
                if stage == 0:
                    finish(k, half, n, stores, loads)
                elif stage == 1:
                    add_x(k, half, n, stores)
                else:
                    add_elu(n)

            dve.sem_inc(drained, 2)
            dve.sem_inc(o_ready, 1)
            with dve.Fori(0, B // 2) as i:
                for g in range(STEPS):
                    k, half, jt = g // (2 * T), g // T % 2, g % T
                    b = 2 * i + k
                    if jt == 0:
                        dve.wait_ge(rows_loaded[k][half], 32 * (i + 1))
                    dve.wait_ge(exp_done, STEPS * i + g + 1)
                    if g % (2 * T) == 0:
                        nc.vector.tensor_copy(s2_02[:, k:k + 1, :], keep["s2_02"][:, bass.ds(b, 1), :])
                    rows = slice(half * HALF, (half + 1) * HALF)
                    nc.vector.scalar_tensor_tensor(out=z[:, g % ZB, :], in0=urow[:, k, rows], scalar=keep["s2_08"][:, bass.ds(b, 1), jt],
                                                   in1=vrow[:, k, rows], op0=ALU.add, op1=ALU.max).then_inc(z_ready, 1)
                    if g - 1 in mine:
                        dve.wait_ge(exp_done, STEPS * i + g + ZB)
                        q = (g - 1) % PB
                        m_half, m_jt = (g - 1) // T % 2, (g - 1) % T
                        nc.vector.tensor_tensor(w[:, q, :], w[:, q, :], keep["mask_t"][:, m_jt, m_half * HALF:(m_half + 1) * HALF],
                                                ALU.mult).then_inc(masked_dve, 1)
                    if g % T in FIN[:STAGES]:
                        stage = FIN.index(g % T)
                        n = g // T - 1
                        if n >= 0:
                            finish_stage(stage, n // 2, n % 2, 4 * i + n, 2 * i + (n + 1) // 2, i + 1)
                        else:
                            with dve.If(i > 0):
                                finish_stage(stage, 1, 1, 4 * i - 1, 2 * i, i)
            for stage in range(STAGES):
                finish_stage(stage, 1, 1, 2 * B - 1, B, B // 2)

        @block.scalar
        def _(act):
            def exp_y(n):
                act.wait_ge(drained, n + 1 + 2)
                if residual_elu:
                    act.wait_ge(o_ready, n + 1)
                    nc.scalar.activation(e[:], y[:], ACT.Exp).then_inc(e_ready, 1)
                    act.wait_ge(e_ready, 2 * n + 2)
                    nc.scalar.activation(e[:], e[:], ACT.Relu, bias=1.0, scale=-1.0).then_inc(e_ready, 1)

            act.sem_inc(e_ready, 1)
            act.sem_inc(exp_done, ZB)
            with act.Fori(0, B // 2) as i:
                for g in range(STEPS):
                    k, jt = g // (2 * T), g % T
                    act.wait_ge(z_ready, STEPS * i + g + 1)
                    act.wait_ge(weighed, STEPS * i + g + 1)
                    nc.scalar.activation(w[:, g % PB, :], z[:, g % ZB, :], ACT.Exp,
                                         bias=s2_02[:, k, jt:jt + 1]).then_inc(exp_done, 1)
                    if g % T == FIN[0] + 1 and residual_elu:
                        n = g // T - 1
                        if n >= 0:
                            exp_y(4 * i + n)
                        else:
                            with act.If(i > 0):
                                exp_y(4 * i - 1)
            if residual_elu:
                exp_y(2 * B - 1)

        @block.gpsimd
        def _(pool):
            with pool.Fori(0, B // 2) as i:
                for g in range(STEPS):
                    if g in mine:
                        continue
                    half, jt = g // T % 2, g % T
                    pool.wait_ge(exp_done, STEPS * i + g + 1 + ZB)
                    nc.gpsimd.tensor_tensor(w[:, g % PB, :], w[:, g % PB, :], keep["mask_t"][:, jt, half * HALF:(half + 1) * HALF],
                                            ALU.mult).then_inc(masked_pool, 1)

        @block.tensor
        def _(pe):
            pe.sem_inc(weighed, PB)
            with pe.Fori(0, B // 2) as i:
                for g in range(STEPS):
                    k, half, jt = g // (2 * T), g // T % 2, g % T
                    if g % (2 * T) == 0:
                        pe.wait_ge(h_loaded[k], 16 * (i + 1))
                    if jt == 0:
                        pe.wait_ge(drained, 4 * i + g // T + 1)
                    if g in mine:
                        pe.wait_ge(masked_dve, len(mine) * i + mine.index(g) + 1)
                    else:
                        pe.wait_ge(masked_pool, (STEPS - len(mine)) * i + g - sum(m < g for m in mine) + 1)
                    for it in range(IT):
                        mm = nc.tensor.matmul(tile(half, it), w[:, g % PB, it * P:(it + 1) * P], h[:, k, jt, :],
                                              start=(jt == 0 and it % 3 == 0), stop=(jt == T - 1), skip_group_check=True)
                    mm.then_inc(weighed, 1)


def nodes1(nc, io, keep):
    with ExitStack() as stack:
        s = Scope(nc, stack, "p1")
        x = [s.sb(f"x{k}", [P, T, F]) for k in range(2)]
        hn = s.sb("hn", [P, T, F])
        hT = s.sb("hT", [P, N])
        wqk = [s.sb("wq", [P, F]), s.sb("wk", [P, F])]
        wv = s.sb("wv", [P, F])
        hi = [[s.sb(f"{m}_hi{k}", [P, N], F16) for m in "qk"] for k in range(2)]
        lo = [[s.sb(f"{m}_lo{k}", [P, N], F16) for m in "qk"] for k in range(2)]
        v = [s.sb(f"v{k}", [P, 2, T, 2, HD + 1]) for k in range(2)]
        st = s.sb("st", [P, T, 6])
        tmp = s.sb("tmp", [P, 4, T])
        rstd, shift, minus_half = s.sb("rstd", [P, T]), s.sb("shift", [P, T]), s.sb("minus_half", [P, T])
        tp_ps = s.ps("tp_ps", [P, 2, BANK])
        qk_ps = s.ps("qk_ps", [P, 4, BANK])
        v_ps = s.ps("v_ps", [P, 2, BANK])
        weights_in, consts_ready, x_loaded = s.sem("weights_in"), s.sem("consts_ready"), [s.sem(f"x_loaded{k}") for k in range(2)]
        chain, rooted, normed, turned, hT_kept = s.sem("chain"), s.sem("rooted"), s.sem("normed"), s.sem("turned"), s.sem("hT_kept")
        qk_done, hi_done, lo_done, v_done, v_kept = (s.sem("qk_done"), s.sem("hi_done"), s.sem("lo_done"), s.sem("v_done"),
                                                     s.sem("v_kept"))
        stored = [s.sem(f"stored{k}") for k in range(2)]
        block = s.block()
        CHAIN = NORM_STEPS + 1
        QK = 2 * CH

        def turns(eng, first, turn, last):
            first()
            with eng.Fori(0, B // 2 - 1) as i:
                turn(2 * i, 0, i)
                turn(2 * i + 1, 1, i)
            turn(B - 2, 0, B // 2 - 1)
            last(B - 1, 1, B // 2 - 1)

        def last_two(i):
            return isinstance(i, int) and i == B // 2 - 1

        @block.sync
        def _(sp):
            def load(b, k):
                sp.dma_start(flat(x[k][:]), node_tiles(io["x1"], b)).then_inc(x_loaded[k], 16)

            def store(b, k, i):
                sp.wait_ge(hi_done, QK * (b + 1))
                sp.wait_ge(lo_done, QK * (b + 1))
                for part, names in ((hi[k], ("q_hi", "k_hi")), (lo[k], ("q_lo", "k_lo"))):
                    for buf, m in zip(part, names):
                        sp.dma_start(io[m][bass.ds(b, 1)].rearrange("one p n -> p (one n)"), buf[:]).then_inc(stored[k], 16)
                sp.wait_ge(v_kept, CH * (b + 1) + 2)
                sp.dma_start(io["v"][bass.ds(b, 1)].rearrange("one g p n -> p (one g) n"),
                             v[k][:].rearrange("p g t a d -> p g (t a d)")).then_inc(stored[k], 16)

            def first():
                load(0, 0)
                load(1, 1)
                for buf, m in ((wqk[0], "L1_gnn_W_q"), (wqk[1], "L1_gnn_W_k"), (wv, "L1_gnn_W_v")):
                    sp.dma_start(buf[:], io[m][:]).then_inc(weights_in, 16)

            def turn(b, k, i):
                if not last_two(i):
                    sp.wait_ge(normed, CH * (b + 1))
                    load(b + 2, k)
                store(b, k, i)

            turns(sp, first, turn, store)
            for k in range(2):
                sp.wait_ge(stored[k], 80 * B // 2)

        @block.gpsimd
        def _(pool):
            nc.gpsimd.memset(minus_half[:], -0.5).then_inc(consts_ready, 1)
            for k in range(2):
                nc.gpsimd.memset(v[k][:], 1.0).then_inc(consts_ready, 1)
            pool.wait_ge(consts_ready, 3)
            with pool.Fori(0, B) as b:
                norm_root(nc, pool, tmp, minus_half[:], rstd[:], chain, b * CHAIN + NORM_STEPS, rooted)

        @block.vector
        def _(dve):
            def stats(b, k, i):
                dve.wait_ge(x_loaded[k], 16 * (i + 1))
                for t in range(T):
                    last = nc.vector.bn_stats(st[:, t, :], x[k][:, t, :])
                last.then_inc(chain, 1)
                dve.wait_ge(chain, b * CHAIN + 1)
                dve.wait_ge(normed, CH * b)
                norm_stats(nc, dve, st, tmp, chain, b * CHAIN + 1)

            def shifts(b):
                norm_shift(nc, dve, tmp, rstd[:], shift[:], chain, rooted, b + 1)

            def split(b, k, i, q):
                for a in range(2):
                    c = 2 * q + a
                    dve.wait_ge(hi_done, QK * b + c + 1)
                    nc.vector.tensor_tensor(lo[k][a][:, q * BANK:(q + 1) * BANK], qk_ps[:, c % 4, :],
                                            hi[k][a][:, q * BANK:(q + 1) * BANK], ALU.subtract).then_inc(lo_done, 1)
                dve.wait_ge(v_done, CH * b + q + 1)
                for g in range(2):
                    ins = nc.vector.tensor_copy(v[k][:, g, 4 * q:4 * q + 4, :, 0:HD],
                                                v_ps[:, q % 2, :].rearrange("p (t g a d) -> p g t a d", g=2, a=2, d=HD)[:, g])
                ins.then_inc(v_kept, 1)

            def first():
                stats(0, 0, 0)
                shifts(0)

            def turn(b, k, i, more=True):
                if more:
                    stats(b + 1, 1 - k, i + k)
                dve.wait_ge(stored[k], 80 * i)
                split(b, k, i, 0)
                if more:
                    shifts(b + 1)
                for q in range(1, CH):
                    split(b, k, i, q)

            dve.sem_inc(v_kept, 2)
            dve.wait_ge(consts_ready, 3)
            turns(dve, first, turn, lambda b, k, i: turn(b, k, i, False))

        @block.scalar
        def _(act):
            def norm(b, k, q):
                if q == 0:
                    act.wait_ge(chain, (b + 1) * CHAIN)
                for t in range(4 * q, 4 * q + 4):
                    last = nc.scalar.activation(hn[:, t, :], x[k][:, t, :], ACT.Relu, bias=shift[:, t:t + 1], scale=rstd[:, t:t + 1])
                last.then_inc(normed, 1)

            def first():
                for q in range(CH):
                    norm(0, 0, q)

            def keep_hT(b, q):
                act.wait_ge(turned, CH * b + q + 1)
                nc.scalar.copy(hT[:, q * BANK:(q + 1) * BANK], tp_ps[:, q % 2, :]).then_inc(hT_kept, 1)

            def turn(b, k, i, more=True):
                act.wait_ge(stored[k], 80 * i)
                keep_hT(b, 0)
                for q in range(CH):
                    if q + 1 < CH:
                        keep_hT(b, q + 1)
                    if q >= 1 and more:
                        norm(b + 1, 1 - k, q - 1)
                    for a in range(2):
                        c = 2 * q + a
                        act.wait_ge(qk_done, QK * b + c + 1)
                        nc.scalar.copy(hi[k][a][:, q * BANK:(q + 1) * BANK], qk_ps[:, c % 4, :]).then_inc(hi_done, 1)
                if more:
                    norm(b + 1, 1 - k, CH - 1)

            act.sem_inc(hT_kept, 2)
            turns(act, first, turn, lambda b, k, i: turn(b, k, i, False))

        @block.tensor
        def _(pe):
            def turn_nodes(b, q):
                pe.wait_ge(normed, CH * b + q + 1)
                pe.wait_ge(hT_kept, CH * b + q + 1)
                for t in range(4 * q, 4 * q + 4):
                    mm = nc.tensor.transpose(tp_ps[:, q % 2, (t % 4) * P:(t % 4 + 1) * P], hn[:, t, :], keep["ident"][:])
                mm.then_inc(turned, 1)

            def batch(b):
                turn_nodes(b, 0)
                for q in range(CH):
                    if q + 1 < CH:
                        turn_nodes(b, q + 1)
                    pe.wait_ge(hT_kept, CH * b + q + 3)
                    for a in range(2):
                        c = 2 * q + a
                        pe.wait_ge(lo_done, QK * b + max(c - 3, 0))
                        nc.tensor.matmul(qk_ps[:, c % 4, :], wqk[a][:], hT[:, q * BANK:(q + 1) * BANK], start=True,
                                         stop=True).then_inc(qk_done, 1)
                    pe.wait_ge(v_kept, CH * b + q + 1)
                    for t in range(4 * q, 4 * q + 4):
                        mm = nc.tensor.matmul(v_ps[:, q % 2, (t % 4) * P:(t % 4 + 1) * P], hT[:, t * P:(t + 1) * P], wv[:],
                                              start=True, stop=True)
                    mm.then_inc(v_done, 1)

            pe.wait_ge(weights_in, 16 * 3)
            with pe.Fori(0, B) as b:
                batch(b)


def head_attention(nc, io, keep):
    SCALE = float(HD) ** -0.5
    K = 3 * HD
    STEPS = CH * T
    BODY = 2 * STEPS
    CHUNKS = 2 * CH
    RT = T // CH
    UNITS = 2 * RT * CH
    TURN = UNITS // 4
    SLOTS = UNITS + 1
    PB, LAG = 4, 3
    SB, MB = 3, 3
    mine = [g for g in range(BODY) if g % 4 == 1]
    with ExitStack() as stack:
        s = Scope(nc, stack, "a1")
        mbias = s.sb("mbias", [P, T, N], BF16)
        qs = [[s.sb(f"qs{u}{a}", [K + 1, N], F16) for a in range(2)] for u in range(2)]
        ks = [[s.sb(f"ks{u}{a}", [K + 1, N], F16) for a in range(2)] for u in range(2)]
        v = [s.sb(f"v{u}", [P, T, 2, HD + 1]) for u in range(2)]
        w = s.sb("w", [P, PB, 2, BANK])
        mx = s.sb("mx", [P, 2, 2 * RT, CH])
        mrow = s.sb("mrow", [P, 2 * RT])
        mshift = s.sb("mshift", [2 * RT, P], F16)
        oe = s.sb("oe", [2 * (HD * 2), 2, BANK])
        sc_ps = s.ps("sc_ps", [P, SB, BANK])
        mx_ps = s.ps("mx_ps", [P, MB, BANK])
        o_ps = s.ps("o_ps", [P, 2, BANK])
        mbias_early, mbias_loaded, units_ready = s.sem("mbias_early"), s.sem("mbias_loaded"), s.sem("units_ready")
        qk_loaded, v_loaded = [s.sem(f"qk_loaded{u}") for u in range(2)], [s.sem(f"v_loaded{u}") for u in range(2)]
        scored, exp_done, masked_pool, masked_dve, weighed = (s.sem("scored"), s.sem("exp_done"), s.sem("masked_pool"),
                                                              s.sem("masked_dve"), s.sem("weighed"))
        mx_scored, mx_taken, rows_done = s.sem("mx_scored"), s.sem("mx_taken"), s.sem("rows_done")
        shift_ready, shift_stored, shift_placed = s.sem("shift_ready"), s.sem("shift_stored"), s.sem("shift_placed")
        o_kept, o_stored = s.sem("o_kept"), [s.sem(f"o_stored{k}") for k in range(2)]
        block = s.block()

        def load(sp, b, u):
            for a in range(2):
                head = slice((2 * u + a) * HD, (2 * u + a + 1) * HD)
                for row, m in ((0, "k_hi"), (1, "k_lo"), (2, "k_hi")):
                    sp.dma_start(ks[u][a][row * HD:(row + 1) * HD, :],
                                 io[m][bass.ds(b, 1), head, :].rearrange("one p n -> p (one n)")).then_inc(qk_loaded[u], 16)
                for row, m in ((0, "q_hi"), (1, "q_hi"), (2, "q_lo")):
                    sp.dma_start(qs[u][a][row * HD:(row + 1) * HD, :],
                                 io[m][bass.ds(b, 1), head, :].rearrange("one p n -> p (one n)")).then_inc(qk_loaded[u], 16)

        def load_v(sp, b, u):
            sp.dma_start(v[u][:].rearrange("p t a d -> p (t a d)"),
                         io["v"][bass.ds(b, 1), u].rearrange("one p n -> p (one n)")).then_inc(v_loaded[u], 16)

        LOADS = 16 * 12

        def target(c):
            return (c + 2) // CHUNKS, (c + 2) % CHUNKS // CH, (c + 2) % CH

        def slots(first):
            return list(range(-1, UNITS)) if first else [*range(TURN), -1, *range(TURN, UNITS)]

        def of_step(jt):
            return [k for k, n in enumerate(slots(False)) if (TURN if n < 0 else n) // 2 == jt]

        def place_shift(sp, chunk, u, c):
            sp.wait_ge(shift_ready, chunk + 1)
            sp.dma_start(io["shifts"][:], mshift[:]).then_inc(shift_stored, 16)
            sp.wait_ge(shift_stored, 16 * (chunk + 1))
            for a in range(2):
                sp.dma_start(qs[u][a][K:K + 1, c * BANK:(c + 1) * BANK],
                             io["shifts"][a * RT:(a + 1) * RT, :].rearrange("(o t) p -> o (t p)", o=1)).then_inc(shift_placed, 16)

        @block.sync
        def _(sp):
            load(sp, 0, 0)
            for t in range(T):
                sp.dma_start(mbias[:, t, :], io["mask_bias"][t * P:(t + 1) * P, :]).then_inc(
                    mbias_early if t < 2 * RT else mbias_loaded, 16)
            load_v(sp, 0, 0)
            load(sp, 0, 1)
            load_v(sp, 0, 1)
            place_shift(sp, 0, 0, 0)

            def store(b, c):
                sp.wait_ge(o_kept, 2 * CH * b + c + 1 + 2)
                u, rows = c // CH, slice(c % CH * BANK, (c % CH + 1) * BANK)
                for a in range(2):
                    head = 2 * u + a
                    sp.dma_start(io["heads_t"][bass.ds(b, 1), head * HD:(head + 1) * HD, rows].rearrange("one p n -> p (one n)"),
                                 oe[2 * HD * a:2 * HD * a + HD, c % 2, :]).then_inc(o_stored[c % 2], 16)
                    sp.dma_start(io["sums"][bass.ds(b, 1), head:head + 1, rows].rearrange("one p n -> p (one n)"),
                                 oe[2 * HD * a + HD:2 * HD * a + HD + 1, c % 2, :]).then_inc(o_stored[c % 2], 16)

            with sp.Fori(0, B) as b:
                following = (b + 1) % B
                for c in range(CHUNKS):
                    if c == CH:
                        sp.wait_ge(scored, 2 * (BODY * b + STEPS))
                        load(sp, following, 0)
                    if c >= 1:
                        store(b, c - 1)
                    place_shift(sp, CHUNKS * b + c + 1, (c + 1) % CHUNKS // CH, (c + 1) % CH)
                    if c == CH:
                        sp.wait_ge(weighed, BODY * b + STEPS + PB)
                        load_v(sp, following, 0)
                sp.wait_ge(scored, 2 * BODY * (b + 1))
                load(sp, following, 1)
                store(b, CHUNKS - 1)
                sp.wait_ge(weighed, BODY * (b + 1) + PB)
                load_v(sp, following, 1)
            for u in range(2):
                sp.wait_ge(qk_loaded[u], LOADS * (B + 1))
                sp.wait_ge(v_loaded[u], 16 * (B + 1))
                sp.wait_ge(o_stored[u], 64 * CH * B)
            sp.wait_ge(shift_placed, 32 * (CHUNKS * B + 1))

        @block.tensor
        def _(pe):
            def slot(k, chunk, u, c, first=False):
                n = slots(first)[k]
                if n < 0 and first:
                    return
                if n < 0:
                    pe.wait_ge(rows_done, chunk)
                pe.wait_ge(mx_taken, SLOTS * chunk + k + 1)
                if n < 0:
                    mm = nc.tensor.transpose(mx_ps[0:2 * RT, k % MB, 0:P], mrow[:], keep["ident"][:])
                else:
                    a, t, kc = n // (RT * CH), RT * c + n // CH % RT, n % CH
                    mm = nc.tensor.matmul(mx_ps[:, k % MB, :], qs[u][a][0:K, t * P:(t + 1) * P], ks[u][a][0:K, kc * BANK:(kc + 1) * BANK],
                                          start=True, stop=True)
                mm.then_inc(mx_scored, 1)

            def weigh(g, i):
                u, c, jt = g // STEPS, g // T, g % T
                if jt == 0:
                    pe.wait_ge(o_kept, 2 * CH * i + c + 1)
                if g % STEPS == 0:
                    pe.wait_ge(v_loaded[u], 16 * (i + 1))
                if g in mine:
                    pe.wait_ge(masked_dve, len(mine) * i + mine.index(g) + 1)
                else:
                    pe.wait_ge(masked_pool, (BODY - len(mine)) * i + g - sum(m < g for m in mine) + 1)
                for a in range(2):
                    mm = nc.tensor.matmul(o_ps[2 * HD * a:2 * HD * a + HD + 1, c % 2, :], v[u][:, jt, a, :], w[:, g % PB, a, :],
                                          start=(jt == 0), stop=(jt == T - 1))
                mm.then_inc(weighed, 1)

            pe.sem_inc(weighed, PB)
            pe.sem_inc(mx_scored, 1)
            pe.wait_ge(qk_loaded[0], LOADS)
            for chunk in range(2):
                for k in range(SLOTS):
                    slot(k, chunk, 0, chunk, chunk == 0)
            pe.wait_ge(units_ready, 4)
            with pe.Fori(0, B) as i:
                for g in range(BODY):
                    u, r = g // STEPS, g % STEPS
                    c, jt = r // T, r % T
                    if jt == 0:
                        pe.wait_ge(shift_placed, 32 * (CHUNKS * i + g // T + 1))
                    for a in range(2):
                        n = 2 * g + a
                        pe.wait_ge(exp_done, 2 * BODY * i + (n + 1 if n else SB))
                        nc.tensor.matmul(sc_ps[:, n % SB, :], ks[u][a][:, jt * P:(jt + 1) * P],
                                         qs[u][a][:, c * BANK:(c + 1) * BANK], start=True, stop=True).then_inc(scored, 1)
                    on, tu, tc = target(g // T)
                    if jt == 0 and tc == 0:
                        pe.wait_ge(qk_loaded[tu], LOADS * (i + on + 1))
                    mine_now = of_step(jt)
                    slot(mine_now[0], CHUNKS * i + g // T + 2, tu, tc)
                    if g >= LAG:
                        weigh(g - LAG, i)
                    for k in mine_now[1:]:
                        slot(k, CHUNKS * i + g // T + 2, tu, tc)
                for g in range(BODY - LAG, BODY):
                    weigh(g, i)

        @block.vector
        def _(dve):
            def slot(k, chunk, c, parity, masks, first=False):
                n = slots(first)[k]
                if n < 0 and first:
                    return
                due = SLOTS * chunk + k + 1
                if n < 0:
                    dve.wait_ge(mx_scored, due)
                    dve.wait_ge(shift_stored, 16 * (chunk - 1))
                    nc.vector.tensor_scalar(mshift[:], mx_ps[0:2 * RT, k % MB, 0:P], -1.0 / SHIFT_UNIT, None,
                                            ALU.mult).then_inc(shift_ready, 1)
                    dve.wait_ge(shift_ready, chunk)
                    dve.sem_inc(mx_taken, 1)
                else:
                    if not isinstance(due, int):
                        dve.compute_val(due)
                    dve.wait_ge(*masks)
                    dve.wait_ge(mx_scored, due)
                    t, kc = RT * c + n // CH % RT, n % CH
                    nc.vector.tensor_tensor_reduce(out=mx_ps[:, k % MB, :], in0=mx_ps[:, k % MB, :],
                                                   in1=mbias[:, t, kc * BANK:(kc + 1) * BANK], scale=1.0, scalar=-3.0e38,
                                                   op0=ALU.add, op1=ALU.max,
                                                   accum_out=mx[:, parity, n // CH, kc:kc + 1]).then_inc(mx_taken, 1)
                if k == SLOTS - 1:
                    dve.wait_ge(mx_taken, SLOTS * (chunk + 1) + MB)
                    nc.vector.tensor_reduce(mrow[:], mx[:, parity], AX.X, ALU.max).then_inc(rows_done, 1)

            def mask(g, i):
                if g in mine:
                    c, jt = g // T % CH, g % T
                    dve.wait_ge(exp_done, 2 * (BODY * i + g + 1) + SB)
                    nc.vector.tensor_tensor(w[:, g % PB], w[:, g % PB],
                                            keep["mask_t"][:, jt, c * BANK:(c + 1) * BANK].unsqueeze(1).to_broadcast([P, 2, BANK]),
                                            ALU.mult).then_inc(masked_dve, 1)

            dve.sem_inc(mx_taken, MB + 1)
            for u in range(2):
                for a in range(2):
                    nc.vector.memset(ks[u][a][K:K + 1, :], SHIFT_UNIT).then_inc(units_ready, 1)
            for chunk in range(2):
                for k in range(SLOTS):
                    slot(k, chunk, chunk, chunk, (mbias_early, 16 * 2 * RT), chunk == 0)
            with dve.Fori(0, B) as i:
                for g in range(BODY):
                    if g >= 1:
                        mask(g - 1, i)
                    for k in of_step(g % T):
                        slot(k, CHUNKS * i + g // T + 2, target(g // T)[2], g // T % 2, (mbias_loaded, 16 * (T - 2 * RT)))
                mask(BODY - 1, i)

        @block.scalar
        def _(act):
            def keep_rows(c, i):
                act.wait_ge(weighed, BODY * i + (c + 1) * T + PB)
                act.wait_ge(o_stored[c % 2], 64 * (CH * i + c // 2))
                for a in range(2):
                    rows = slice(2 * HD * a, 2 * HD * a + HD + 1)
                    ins = nc.scalar.copy(oe[rows, c % 2, :], o_ps[rows, c % 2, :])
                ins.then_inc(o_kept, 1)

            act.sem_inc(exp_done, SB)
            act.sem_inc(o_kept, 2)
            with act.Fori(0, B) as i:
                for g in range(BODY):
                    act.wait_ge(weighed, BODY * i + g + 1)
                    for a in range(2):
                        n = 2 * g + a
                        act.wait_ge(scored, 2 * BODY * i + n + 1)
                        nc.scalar.activation(w[:, g % PB, a], sc_ps[:, n % SB], ACT.Exp, scale=SCALE).then_inc(exp_done, 1)
                    if g >= T + LAG and (g - LAG) % T == 0:
                        keep_rows((g - LAG) // T - 1, i)
                keep_rows(2 * CH - 1, i)

        @block.gpsimd
        def _(pool):
            with pool.Fori(0, B) as i:
                for g in range(BODY):
                    if g in mine:
                        continue
                    c, jt = g // T % CH, g % T
                    pool.wait_ge(exp_done, 2 * (BODY * i + g + 1) + SB)
                    nc.gpsimd.tensor_tensor(w[:, g % PB], w[:, g % PB],
                                            keep["mask_t"][:, jt, c * BANK:(c + 1) * BANK].unsqueeze(1).to_broadcast([P, 2, BANK]),
                                            ALU.mult).then_inc(masked_pool, 1)


def nodes2(nc, io, keep):
    GB = 4
    with ExitStack() as stack:
        s = Scope(nc, stack, "p2")
        ot = s.sb("ot", [P, N])
        all_sums = s.sb("all_sums", [P, BANK])
        rz = s.sb("rz", [HEADS, N])
        sel = s.sb("sel", [HEADS, HEADS, HD])
        x1 = s.sb("x1", [P, T, F])
        x1b = s.sb("x1b", [P, T, F])
        x2 = s.sb("x2", [P, T, F])
        hn = s.sb("hn", [P, T, F])
        hT = s.sb("hT", [P, N])
        g = s.sb("g", [P, T, 2, F], F16)
        own = s.sb("own", [P, T, F])
        wo = s.sb("wo", [P, F])
        wns = s.sb("wns", [P, 2 * F])
        bo, bs, bn = s.sb("bo", [P, F]), s.sb("bs", [P, F]), s.sb("bn", [P, F])
        bias = s.sb("bias", [P, T, F])
        st = s.sb("st", [P, T, 6])
        tmp = s.sb("tmp", [P, 4, T])
        rstd, shift, minus_half = s.sb("rstd", [P, T]), s.sb("shift", [P, T]), s.sb("minus_half", [P, T])
        ry_ps = s.ps("ry_ps", [P, 2, BANK])
        tp_ps = s.ps("tp_ps", [P, 2, BANK])
        g_ps = s.ps("g_ps", [P, GB, 2, 2 * F])
        weights_in, consts_ready, sel_ready, bias_ready = (s.sem("weights_in"), s.sem("consts_ready"), s.sem("sel_ready"),
                                                           s.sem("bias_ready"))
        heads_loaded, x1_loaded = s.sem("heads_loaded"), s.sem("x1_loaded")
        spread, divided, y_done, x1b_done, x2_done = (s.sem("spread"), s.sem("divided"), s.sem("y_done"),
                                                               s.sem("x1b_done"), s.sem("x2_done"))
        chain, rooted, normed, turned, hT_kept = s.sem("chain"), s.sem("rooted"), s.sem("normed"), s.sem("turned"), s.sem("hT_kept")
        g_done, hi_done, lo_done, own_done = s.sem("g_done"), s.sem("hi_done"), s.sem("lo_done"), s.sem("own_done")
        x2_stored, g_stored, own_stored = s.sem("x2_stored"), s.sem("g_stored"), s.sem("own_stored")
        sums_loaded, rz_done, rz_stored = s.sem("sums_loaded"), s.sem("rz_done"), s.sem("rz_stored")
        block = s.block()
        CHAIN = NORM_STEPS + 1
        PAIRS = T // 2

        @block.sync
        def _(sp):
            sp.dma_start(wo[:], io["L1_gnn_W_o"][:]).then_inc(weights_in, 16)
            sp.dma_start(wns[:, 0:F], io["L2_gnn_W_neigh"][:]).then_inc(weights_in, 16)
            sp.dma_start(wns[:, F:2 * F], io["L2_gnn_W_self"][:]).then_inc(weights_in, 16)
            for buf, m in ((bo, "L1_gnn_b_o"), (bs, "L2_gnn_b_self"), (bn, "L2_gnn_b_neigh")):
                sp.dma_start(buf[:], io[m][0:1, :].partition_broadcast(P)).then_inc(weights_in, 16)

            def load(b):
                sp.wait_ge(x1b_done, b)
                sp.dma_start(flat(x1[:]), node_tiles(io["x1"], b)).then_inc(x1_loaded, 16)
                sp.wait_ge(spread, CH * b)
                sp.dma_start(rz[:], io["sums"][bass.ds(b, 1)].rearrange("one p n -> p (one n)")).then_inc(heads_loaded, 16)
                sp.wait_ge(y_done, CH * b)
                sp.dma_start(ot[:], io["heads_t"][bass.ds(b, 1)].rearrange("one p n -> p (one n)")).then_inc(heads_loaded, 16)

            def store_x2(b):
                sp.wait_ge(x2_done, CH * (b + 1))
                sp.dma_start(node_tiles(io["x2"], b), flat(x2[:])).then_inc(x2_stored, 16)

            def store(b):
                sp.wait_ge(lo_done, PAIRS * (b + 1))
                sp.wait_ge(hi_done, PAIRS * (b + 1))
                sp.dma_start(io["g"][bass.ds(b, 1)].rearrange("one p n -> p (one n)"),
                             g[:].rearrange("p t k f -> p (t k f)")).then_inc(g_stored, 16)
                sp.wait_ge(own_done, PAIRS * (b + 1))
                sp.dma_start(io["own"][bass.ds(b, 1)].rearrange("one p n -> p (one n)"), flat(own[:])).then_inc(own_stored, 16)

            across = io["sums"].rearrange("b h (c n) -> (b h c) n", n=BANK)
            sp.dma_start(all_sums[:], across).then_inc(sums_loaded, 16)
            sp.wait_ge(rz_done, 1)
            sp.dma_start(across, all_sums[:]).then_inc(rz_stored, 16)
            sp.wait_ge(rz_stored, 16)
            load(0)
            load(1)
            store_x2(0)
            with sp.Fori(0, B - 2) as b:
                load(b + 2)
                store_x2(b + 1)
                store(b)
            store_x2(B - 1)
            store(B - 2)
            store(B - 1)
            sp.wait_ge(x2_stored, 16 * B)
            sp.wait_ge(g_stored, 16 * B)
            sp.wait_ge(own_stored, 16 * B)

        @block.gpsimd
        def _(pool):
            nc.gpsimd.memset(minus_half[:], -0.5).then_inc(consts_ready, 1)
            nc.gpsimd.memset(sel[:], 1.0).then_inc(sel_ready, 1)
            pool.wait_ge(sel_ready, 1)
            nc.gpsimd.affine_select(out=sel[:], in_=sel[:], compare_op=ALU.is_equal, fill=0.0, base=0,
                                    pattern=[[-1, HEADS], [0, HD]], channel_multiplier=1).then_inc(consts_ready, 1)
            pool.wait_ge(weights_in, 16 * 6)
            pool.wait_ge(consts_ready, 2)

            def first(b):
                pool.wait_ge(x1_loaded, 16 * (b + 1))
                pool.wait_ge(x2_done, CH * b)
                nc.gpsimd.tensor_tensor(x1b[:], x1[:], bo[:].unsqueeze(1).to_broadcast([P, T, F]), ALU.add).then_inc(x1b_done, 1)

            def root(b):
                norm_root(nc, pool, tmp, minus_half[:], rstd[:], chain, b * CHAIN + NORM_STEPS, rooted)

            first(0)
            root(0)
            with pool.Fori(0, B - 1) as b:
                first(b + 1)
                root(b + 1)

        @block.vector
        def _(dve):
            def divide(b):
                dve.wait_ge(heads_loaded, 32 * (b + 1))
                for q in range(CH):
                    dve.wait_ge(spread, CH * b + q + 1)
                    nc.vector.tensor_tensor(ot[:, q * BANK:(q + 1) * BANK], ot[:, q * BANK:(q + 1) * BANK], ry_ps[:, q % 2, :],
                                            ALU.mult).then_inc(divided, 1)

            def first(b):
                dve.wait_ge(x1b_done, b + 1)
                dve.wait_ge(x2_stored, 16 * b)
                dve.wait_ge(normed, b)
                for q in range(CH):
                    dve.wait_ge(y_done, CH * b + q + 1)
                    nc.vector.tensor_tensor(x2[:, 4 * q:4 * q + 4, :], ry_ps[:, q % 2, :].rearrange("p (t f) -> p t f", f=F),
                                            x1b[:, 4 * q:4 * q + 4, :], ALU.add).then_inc(x2_done, 1)
                    dve.wait_ge(x2_done, CH * b + q + 1)
                    for t in range(4 * q, 4 * q + 4):
                        last = nc.vector.bn_stats(st[:, t, :], x2[:, t, :])
                last.then_inc(chain, 1)
                dve.wait_ge(chain, b * CHAIN + 1)
                norm_stats(nc, dve, st, tmp, chain, b * CHAIN + 1)

            def shifts(b):
                norm_shift(nc, dve, tmp, rstd[:], shift[:], chain, rooted, b + 1)

            def second(b, part):
                if part == 0:
                    dve.wait_ge(g_stored, 16 * b)
                    dve.wait_ge(own_stored, 16 * b)
                for q in range(part * PAIRS // 2, (part + 1) * PAIRS // 2):
                    tiles = slice(2 * q, 2 * q + 2)
                    dve.wait_ge(hi_done, PAIRS * b + q + 1)
                    nc.vector.tensor_tensor(g[:, tiles, 1, :], g_ps[:, q % GB, :, 0:F], g[:, tiles, 0, :], ALU.subtract).then_inc(lo_done, 1)
                    nc.vector.tensor_tensor(own[:, tiles, :], g_ps[:, q % GB, :, F:2 * F], bias[:, tiles, :], ALU.add).then_inc(own_done, 1)

            dve.wait_ge(sums_loaded, 16)
            nc.vector.reciprocal(all_sums[:], all_sums[:]).then_inc(rz_done, 1)
            dve.wait_ge(weights_in, 16 * 6)
            for t in range(T):
                last = nc.vector.scalar_tensor_tensor(out=bias[:, t, :], in0=bn[:], scalar=keep["has_deg"][:, t:t + 1], in1=bs[:],
                                                      op0=ALU.mult, op1=ALU.add)
            last.then_inc(bias_ready, 1)
            dve.wait_ge(bias_ready, 1)
            divide(0)
            first(0)
            shifts(0)
            with dve.Fori(0, B - 1) as b:
                divide(b + 1)
                first(b + 1)
                second(b, 0)
                shifts(b + 1)
                second(b, 1)
            second(B - 1, 0)
            second(B - 1, 1)

        @block.scalar
        def _(act):
            def first(b):
                act.wait_ge(chain, (b + 1) * CHAIN)
                act.wait_ge(turned, CH * b)
                for t in range(T):
                    last = nc.scalar.activation(hn[:, t, :], x2[:, t, :], ACT.Relu, bias=shift[:, t:t + 1], scale=rstd[:, t:t + 1])
                last.then_inc(normed, 1)

            def keep_hT(b, q):
                act.wait_ge(turned, CH * b + q + 1)
                nc.scalar.copy(hT[:, q * BANK:(q + 1) * BANK], tp_ps[:, q % 2, :]).then_inc(hT_kept, 1)

            def second(b):
                act.wait_ge(g_stored, 16 * b)
                keep_hT(b, 0)
                for q in range(CH):
                    if q + 1 < CH:
                        keep_hT(b, q + 1)
                    for r in (2 * q, 2 * q + 1):
                        act.wait_ge(g_done, PAIRS * b + r + 1)
                        nc.scalar.copy(g[:, 2 * r:2 * r + 2, 0, :], g_ps[:, r % GB, :, 0:F]).then_inc(hi_done, 1)

            act.sem_inc(hT_kept, 2)
            first(0)
            with act.Fori(0, B - 1) as b:
                second(b)
                first(b + 1)
            second(B - 1)

        @block.tensor
        def _(pe):
            def divide(b):
                pe.wait_ge(heads_loaded, 32 * (b + 1))
                for q in range(CH):
                    if q < 2:
                        pe.wait_ge(x2_done, CH * b)
                    else:
                        pe.wait_ge(divided, CH * b + q - 1)
                    nc.tensor.matmul(ry_ps[:, q % 2, :], sel[:].rearrange("k h d -> k (h d)"), rz[:, q * BANK:(q + 1) * BANK],
                                     start=True, stop=True).then_inc(spread, 1)

            def first(b):
                for q in range(CH):
                    pe.wait_ge(divided, CH * b + min(q + 3, CH))
                    pe.wait_ge(x2_done, CH * b + max(q - 1, 0))
                    for t in range(4 * q, 4 * q + 4):
                        mm = nc.tensor.matmul(ry_ps[:, q % 2, (t % 4) * P:(t % 4 + 1) * P], ot[:, t * P:(t + 1) * P], wo[:],
                                              start=True, stop=True)
                    mm.then_inc(y_done, 1)

            def turn_nodes(b, q):
                pe.wait_ge(hT_kept, CH * b + q + 1)
                for t in range(4 * q, 4 * q + 4):
                    mm = nc.tensor.transpose(tp_ps[:, q % 2, (t % 4) * P:(t % 4 + 1) * P], hn[:, t, :], keep["ident"][:])
                mm.then_inc(turned, 1)

            def second(b):
                pe.wait_ge(normed, b + 1)
                turn_nodes(b, 0)
                for q in range(CH):
                    if q + 1 < CH:
                        turn_nodes(b, q + 1)
                    pe.wait_ge(hT_kept, CH * b + q + 3)
                    for r in (2 * q, 2 * q + 1):
                        pe.wait_ge(own_done, PAIRS * b + max(r - GB + 1, 0))
                        for t in (2 * r, 2 * r + 1):
                            mm = nc.tensor.matmul(g_ps[:, r % GB, t % 2, :], hT[:, t * P:(t + 1) * P], wns[:], start=True, stop=True)
                        mm.then_inc(g_done, 1)

            pe.wait_ge(weights_in, 16 * 6)
            pe.wait_ge(consts_ready, 2)
            divide(0)
            first(0)
            with pe.Fori(0, B - 1) as b:
                divide(b + 1)
                first(b + 1)
                second(b)
            second(B - 1)


def neighbours(nc, io, keep):
    SLOTS = 4
    with ExitStack() as stack:
        s = Scope(nc, stack, "p3")
        g = s.sb("g", [P, 2, T, 2 * F], F16)
        own = s.sb("own", [P, 2, T, F])
        x2 = s.sb("x2", [P, 2, T, F])
        part = s.sb("part", [P, T, F])
        x3 = s.sb("x3", [P, T, F])
        hn = s.sb("hn", [P, T, F])
        hT = s.sb("hT", [P, N])
        h = s.sb("h", [P, T, F + 1])
        w = s.sb("w", [P, F + 2])
        w_rows = s.sb("w_rows", [P, F])
        a_cols = s.sb("a_cols", [P, 2])
        st = s.sb("st", [P, T, 6])
        tmp = s.sb("tmp", [P, 4, T])
        rstd, shift, minus_half = s.sb("rstd", [P, T]), s.sb("shift", [P, T]), s.sb("minus_half", [P, T])
        dots = s.sb("dots", [P, T, 2])
        sum_ps = s.ps("sum_ps", [P, SLOTS, BANK])
        tp_ps = s.ps("tp_ps", [P, 2, BANK])
        h_ps = s.ps("h_ps", [P, 2, BANK])
        THREES = [range(t, min(t + 3, T)) for t in range(0, T, 3)]
        TH = len(THREES)
        weights_in, consts_ready, wa_done, w_ready = s.sem("weights_in"), s.sem("consts_ready"), s.sem("wa_done"), s.sem("w_ready")
        g_loaded, own_loaded, x2_loaded = s.sem("g_loaded"), s.sem("own_loaded"), s.sem("x2_loaded")
        summed, part_done, used, x3_done, x3_stored = (s.sem("summed"), s.sem("part_done"), s.sem("used"), s.sem("x3_done"),
                                                       s.sem("x3_stored"))
        chain, rooted, normed, turned, hT_kept = s.sem("chain"), s.sem("rooted"), s.sem("normed"), s.sem("turned"), s.sem("hT_kept")
        h_done, h_kept, scores_kept, h_stored = s.sem("h_done"), s.sem("h_kept"), s.sem("scores_kept"), s.sem("h_stored")
        block = s.block()
        CHAIN = NORM_STEPS + 1

        def of(buf, b):
            return buf[:, bass.ds(b % 2, 1)]

        @block.sync
        def _(sp):
            sp.dma_start(w[:, 0:F], io["L3_gnn_W_t"][:]).then_inc(weights_in, 16)
            sp.dma_start(w_rows[:], io["L3_gnn_W"][:]).then_inc(weights_in, 16)
            sp.dma_start(a_cols[:], io["L3_gnn_a"][:]).then_inc(weights_in, 16)

            def load(b):
                sp.dma_start(of(g, b).rearrange("p one t f -> p (one t f)"),
                             io["g"][bass.ds(b, 1)].rearrange("one p n -> p (one n)")).then_inc(g_loaded, 16)
                sp.dma_start(of(own, b).rearrange("p one t f -> p (one t f)"),
                             io["own"][bass.ds(b, 1)].rearrange("one p n -> p (one n)")).then_inc(own_loaded, 16)
                sp.dma_start(of(x2, b).rearrange("p one t f -> p (one t f)"), node_tiles(io["x2"], b)).then_inc(x2_loaded, 16)

            def loaded(b):
                for sem in (g_loaded, own_loaded, x2_loaded):
                    sp.wait_ge(sem, 16 * (b + 1))

            load(0)
            loaded(0)
            load(1)
            with sp.Fori(0, B - 2) as b:
                loaded(b + 1)
                sp.wait_ge(x3_done, CH * (b + 1))
                load(b + 2)

        @block.gpsimd
        def _(pool):
            nc.gpsimd.memset(minus_half[:], -0.5).then_inc(consts_ready, 1)
            nc.gpsimd.memset(h[:, :, F:F + 1], 1.0).then_inc(consts_ready, 1)
            pool.wait_ge(consts_ready, 2)
            with pool.Fori(0, B) as b:
                norm_root(nc, pool, tmp, minus_half[:], rstd[:], chain, b * CHAIN + NORM_STEPS, rooted)
                pool.dma_start(node_tiles(io["x3"], b), flat(x3[:])).then_inc(x3_stored, 16)
                pool.wait_ge(h_kept, TH * (b + 1))
                pool.dma_start(io["h_nodes"][bass.ds(b, 1)].rearrange("one p t f -> p (one t) f"), h[:]).then_inc(h_stored, 16)
            pool.wait_ge(x3_stored, 16 * B)
            pool.wait_ge(h_stored, 16 * B)

        @block.vector
        def _(dve):
            def first(b, tiles):
                dve.wait_ge(own_loaded, 16 * (b + 1))
                for t in tiles:
                    dve.wait_ge(summed, T * b + t + 1)
                    nc.vector.scalar_tensor_tensor(out=part[:, t, :], in0=sum_ps[:, t % SLOTS, 0:F], scalar=keep["rdeg"][:, t:t + 1],
                                                   in1=of(own, b)[:, 0, t, :], op0=ALU.mult, op1=ALU.add).then_inc(part_done, 1)
                    dve.wait_ge(part_done, T * b + t + 1)
                    nc.vector.scalar_tensor_tensor(out=part[:, t, :], in0=sum_ps[:, t % SLOTS, F:2 * F], scalar=keep["rdeg"][:, t:t + 1],
                                                   in1=part[:, t, :], op0=ALU.mult, op1=ALU.add).then_inc(used, 1)

            def residual(b, q):
                fourth = slice(4 * q, 4 * q + 4)
                dve.wait_ge(used, T * b + 4 * q + 4 + SLOTS)
                if q == 0:
                    dve.wait_ge(x2_loaded, 16 * (b + 1))
                    dve.wait_ge(x3_stored, 16 * b)
                    dve.wait_ge(normed, b)
                nc.vector.scalar_tensor_tensor(out=x3[:, fourth], in0=part[:, fourth], scalar=0.0, in1=of(x2, b)[:, 0, fourth],
                                               op0=ALU.max, op1=ALU.add).then_inc(x3_done, 1)
                dve.wait_ge(x3_done, CH * b + q + 1)
                for t in range(4 * q, 4 * q + 4):
                    last = nc.vector.bn_stats(st[:, t, :], x3[:, t, :])
                if q == CH - 1:
                    last.then_inc(chain, 1)

            def batch(b, behind):
                first(b, range(SLOTS))
                behind()
                first(b, range(SLOTS, T - 4))
                for q in range(CH - 1):
                    residual(b, q)
                first(b, range(T - 4, T))
                residual(b, CH - 1)

            def stats(b):
                dve.wait_ge(chain, b * CHAIN + 1)
                norm_stats(nc, dve, st, tmp, chain, b * CHAIN + 1)

            def shifts(b):
                norm_shift(nc, dve, tmp, rstd[:], shift[:], chain, rooted, b + 1)

            def scores(b):
                dve.wait_ge(h_kept, TH * (b + 1))
                for k, m in enumerate(("s1", "s2")):
                    nc.vector.tensor_copy(keep[m][:, bass.ds(b, 1), :], dots[:, :, k:k + 1].rearrange("p t one -> p one t")).then_inc(scores_kept, 1)

            dve.sem_inc(used, SLOTS)
            dve.wait_ge(wa_done, 1)
            nc.vector.tensor_copy(w[:, F:F + 2], h_ps[:, 0, 0:2]).then_inc(w_ready, 1)
            batch(0, lambda: None)
            with dve.Fori(0, B - 1) as b:
                stats(b)
                batch(b + 1, lambda: shifts(b))
                scores(b)
            stats(B - 1)
            shifts(B - 1)
            scores(B - 1)

        @block.scalar
        def _(act):
            act.sem_inc(hT_kept, 2)
            with act.Fori(0, B) as b:
                act.wait_ge(chain, (b + 1) * CHAIN)
                act.wait_ge(turned, CH * b)
                for t in range(T):
                    last = nc.scalar.activation(hn[:, t, :], x3[:, t, :], ACT.Relu, bias=shift[:, t:t + 1], scale=rstd[:, t:t + 1])
                last.then_inc(normed, 1)
                for q in range(CH):
                    act.wait_ge(turned, CH * b + q + 1)
                    nc.scalar.copy(hT[:, q * BANK:(q + 1) * BANK], tp_ps[:, q % 2, :]).then_inc(hT_kept, 1)
                act.wait_ge(h_stored, 16 * b)
                act.wait_ge(consts_ready, 2)
                act.wait_ge(scores_kept, 2 * b)
                for n, tiles in enumerate(THREES):
                    act.wait_ge(h_done, TH * b + n + 1)
                    m = len(tiles)
                    h3 = h_ps[:, n % 2, 0:m * (F + 2)].rearrange("p (t f) -> p t f", f=F + 2)
                    nc.scalar.copy(h[:, tiles[0]:tiles[0] + m, 0:F], h3[:, :, 0:F])
                    nc.scalar.copy(dots[:, tiles[0]:tiles[0] + m, :], h3[:, :, F:F + 2]).then_inc(h_kept, 1)

        @block.tensor
        def _(pe):
            def first(b, tiles):
                pe.wait_ge(g_loaded, 16 * (b + 1))
                for it in tiles:
                    pe.wait_ge(used, T * b + it + 1)
                    for jt in range(T):
                        mm = nc.tensor.matmul(sum_ps[:, it % SLOTS, 0:2 * F], keep["mask_t"][:, jt, it * P:(it + 1) * P],
                                              of(g, b)[:, 0, jt, :], start=(jt == 0), stop=(jt == T - 1))
                    mm.then_inc(summed, 1)

            def turn_nodes(b, qs):
                pe.wait_ge(normed, b + 1)
                for q in qs:
                    pe.wait_ge(hT_kept, CH * b + q + 1)
                    for t in range(4 * q, 4 * q + 4):
                        mm = nc.tensor.transpose(tp_ps[:, q % 2, (t % 4) * P:(t % 4 + 1) * P], hn[:, t, :], keep["ident"][:])
                    mm.then_inc(turned, 1)

            def features(b, ns):
                pe.wait_ge(hT_kept, CH * (b + 1) + 2)
                for n in ns:
                    pe.wait_ge(h_kept, TH * b + max(n - 1, 0))
                    for k, t in enumerate(THREES[n]):
                        mm = nc.tensor.matmul(h_ps[:, n % 2, k * (F + 2):(k + 1) * (F + 2)], hT[:, t * P:(t + 1) * P], w[:],
                                              start=True, stop=True)
                    mm.then_inc(h_done, 1)

            def step(b, it):
                if it in (9, 10):
                    turn_nodes(b, range(2 * (it - 9), 2 * (it - 9) + 2))
                if it in (12, 13, 14):
                    features(b, range(2 * (it - 12), 2 * (it - 12) + 2))

            pe.wait_ge(weights_in, 16 * 3)
            nc.tensor.matmul(h_ps[:, 0, 0:2], w_rows[:], a_cols[:], start=True, stop=True).then_inc(wa_done, 1)
            first(0, range(T))
            pe.wait_ge(w_ready, 1)
            with pe.Fori(0, B - 1) as b:
                for it in range(T):
                    first(b + 1, [it])
                    step(b, it)
            for it in range(T):
                step(B - 1, it)


_SHAPES = {"h_nodes": ((B, P, T, F + 1), F32), "mask_bias": ((N, N), BF16), "u_rows": ((B, N), F32), "v_rows": ((B, N), F32),
           "x1": ((B, N, F), F32),
           "q_hi": ((B, P, N), F16), "q_lo": ((B, P, N), F16), "k_hi": ((B, P, N), F16), "k_lo": ((B, P, N), F16),
           "v": ((B, 2, P, T * 2 * (HD + 1)), F32), "x2": ((B, N, F), F32), "x3": ((B, N, F), F32), "g": ((B, P, T * 2 * F), F16), "own": ((B, P, T * F), F32),
           "shifts": ((2 * T // CH, P), F16), "heads_t": ((B, P, N), F32), "sums": ((B, HEADS, N), F32)}


def build(nc, io):
    for name, (shape, dtype) in _SHAPES.items():
        io[name] = nc.dram_tensor(name, shape, dtype, kind="Internal").ap()
    with ExitStack() as stack:
        s = Scope(nc, stack, "keep")
        keep = {"mask_t": s.sb("mask_t", [P, T, N], BF16), "ident": s.sb("ident", [P, P]),
                "ident16": s.sb("ident16", [P, P], BF16)}
        for name in ("s1", "s2", "u", "v", "s2_08", "s2_02"):
            keep[name] = s.sb(name, [P, B, T])
        keep["rdeg"], keep["has_deg"] = s.sb("rdeg", [P, T]), s.sb("has_deg", [P, T])
        Scope.used_sems.clear()
        masks_and_nodes0(nc, io, keep)
        row_shifts(nc, io, keep, "l0", True)
        gat_attention(nc, io, keep, "g0", io["x"], io["x1"], True)
        nodes1(nc, io, keep)
        head_attention(nc, io, keep)
        clear_semaphores(nc)
        nodes2(nc, io, keep)
        neighbours(nc, io, keep)
        row_shifts(nc, io, keep, "l3", False)
        gat_attention(nc, io, keep, "g3", io["x3"], io["out"], False)


def kernel(**inputs):
    import numpy as _np
    import concourse.bacc as _bacc
    from concourse import mybir as _mybir
    from concourse.bass_utils import run_bass_kernel_spmd as _run

    laid = {name: _np.asarray(a) for name, a in inputs.items()}
    for name in ("L0_gnn_ln_gamma", "L0_gnn_ln_beta", "L1_gnn_b_o", "L2_gnn_b_self", "L2_gnn_b_neigh"):
        laid[name] = laid[name].reshape(1, F)
    for name in ("L0_gnn_node_weights", "L0_gnn_node_bias"):
        laid[name] = laid[name].reshape(P, T)
    laid["L0_gnn_a"] = laid["L0_gnn_a"].reshape(2, F)
    laid["L3_gnn_a"] = laid["L3_gnn_a"].reshape(2, F).T
    laid["L3_gnn_W_t"] = laid["L3_gnn_W"].T
    nc = _bacc.Bacc("TRN2", target_bir_lowering=False, num_devices=1)
    arrays, io = {}, {}
    for name, a in laid.items():
        arrays[f"in_{name}"] = a = _np.ascontiguousarray(a)
        io[name] = nc.dram_tensor(f"in_{name}", a.shape, _mybir.dt.from_np(a.dtype), kind="ExternalInput").ap()
    io["out"] = nc.dram_tensor("out_0", (B, N, F), F32, kind="ExternalOutput").ap()
    build(nc, io)
    r = _run(nc, [arrays], core_ids=[0])
    return r.results[0]["out_0"]
```
